# Optimizing a Trainium2 kernel written in Bass

```python
import numpy as np
import jax
import jax.numpy as jnp

def _softmax(x, axis=-1):
    return jax.nn.softmax(x, axis=axis)

def _gelu(x):
    return jax.nn.gelu(x, approximate=True)

def _silu(x):
    return jax.nn.silu(x)

def _sigmoid(x):
    return jax.nn.sigmoid(x)

def _layernorm(x, axis=-1, eps=1e-05):
    m = jnp.mean(x, axis=axis, keepdims=True)
    v = jnp.var(x, axis=axis, keepdims=True)
    return (x - m) / jnp.sqrt(v + eps)

def _scatter_add(tgt, idx, src, axis=0):
    return tgt.at[idx].add(src)

def _segment_sum(src, seg, n):
    return jax.ops.segment_sum(src, seg, n)
kernel_name = 'mk_pixart_seq_d4_seqx_r4_17e43a'

def setup_inputs(seed: int=0):
    np.random.seed(seed)
    _w = jnp.asarray

    def _rec_inputs():
        import jax
        import jax.numpy as jnp
        _rk = jax.random.key(seed)
        x = 7.22e-05 + 1 * jax.random.normal(jax.random.fold_in(_rk, 1), (4, 512, 256), jnp.float32)
        _lenS = 512 - jax.random.randint(jax.random.fold_in(_rk, 7), (4,), 0, max(1, 512 // 4) + 1, jnp.int32)
        _lenS2 = 64 - jax.random.randint(jax.random.fold_in(_rk, 8), (4,), 0, max(1, 64 // 4) + 1, jnp.int32)
        cond_1024 = 0.000887014 + 1.03683 * jax.random.normal(jax.random.fold_in(_rk, 11), (4, 256), jnp.float32)
        _ctx_1024P = jax.random.normal(jax.random.fold_in(_rk, 12), (4, 16, 256), jnp.float32)
        _ctx_1024c = jax.random.dirichlet(jax.random.fold_in(_rk, 512), 0.3 * jnp.ones((16,), jnp.float32), (4, 64))
        _ctx_1024t = jnp.einsum('bsk,bkd->bsd', _ctx_1024c, _ctx_1024P)
        _ctx_1024t = _ctx_1024t * jax.lax.rsqrt(jnp.mean(jnp.square(_ctx_1024t)) + 1e-12) * 0.953939
        ctx_1024 = 0.00086875 + 0.999764 * (_ctx_1024t + 0.3 * jax.random.normal(jax.random.fold_in(_rk, 612), (4, 64, 256), jnp.float32))
        return (x, cond_1024, ctx_1024)
    x, cond_1024, ctx_1024 = _rec_inputs()

    def _L0_xcond_setup():
        import jax, jax.numpy as jnp
        import numpy as np
        C = 256
        H = 16
        D = C // H
        WIN = 128
        SHIFT = 64
        TOPK = 16
        HID = 1024
        EPS = 1e-06

        def _ln(x):
            x32 = x.astype(jnp.float32)
            m = x32.mean(-1, keepdims=True)
            v = jnp.mean((x32 - m) ** 2, axis=-1, keepdims=True)
            return ((x32 - m) * jax.lax.rsqrt(v + EPS)).astype(x.dtype)

        def _self_attn(h, w_qkv, b_qkv, w_so, b_so):
            B, L, _ = h.shape
            qkv = h @ w_qkv + b_qkv
            qkv = jnp.roll(qkv, -SHIFT, axis=1)
            nw = L // WIN
            qkv = qkv.reshape(B, nw, WIN, 3, H, D)
            q, k, v = (qkv[:, :, :, 0], qkv[:, :, :, 1], qkv[:, :, :, 2])
            scores = jnp.einsum('bnqhd,bnkhd->bnhqk', q, k) / jnp.sqrt(jnp.float32(D)).astype(h.dtype)
            attn = jax.nn.softmax(scores, axis=-1)
            o = jnp.einsum('bnhqk,bnkhd->bnqhd', attn, v).reshape(B, L, C)
            o = jnp.roll(o, SHIFT, axis=1)
            return o @ w_so + b_so

        def _topk_cross_attn(h, ctx, w_q, b_q, w_kv, b_kv, w_co, b_co):
            B, L, _ = h.shape
            Lc = ctx.shape[1]
            q = (h @ w_q + b_q).reshape(B, L, H, D)
            kv = (ctx @ w_kv + b_kv).reshape(B, Lc, 2, H, D)
            k, v = (kv[:, :, 0], kv[:, :, 1])
            scores = jnp.einsum('bqhd,bkhd->bhqk', q, k) / jnp.sqrt(jnp.float32(D)).astype(h.dtype)
            top_s, top_i = jax.lax.top_k(scores, TOPK)
            attn = jax.nn.softmax(top_s, axis=-1)
            v_bh = jnp.transpose(v, (0, 2, 1, 3))
            vg = jnp.take_along_axis(v_bh[:, :, None, :, :], top_i[..., None], axis=3)
            o = jnp.einsum('bhqk,bhqkd->bqhd', attn, vg).reshape(B, L, C)
            return o @ w_co + b_co

        def _swiglu(h, w_m1, b_m1, w_m2, b_m2):
            u = h @ w_m1 + b_m1
            a, b = (u[..., :HID], u[..., HID:])
            return jax.nn.silu(a) * b @ w_m2 + b_m2
        key = jax.random.key(seed)
        ks = jax.random.split(key, 24)
        s = 0.02
        inp = {'x': jax.random.normal(ks[0], (2, 1024, C), jnp.float32), 'mod': jax.random.normal(ks[1], (2, C), jnp.float32), 'context': jax.random.normal(ks[2], (2, 256, C), jnp.float32), 'w_ada': jax.random.normal(ks[3], (C, 9 * C), jnp.float32) * s, 'b_ada': jnp.zeros((9 * C,), jnp.float32), 'w_qkv': jax.random.normal(ks[4], (C, 3 * C), jnp.float32) * s, 'b_qkv': jnp.zeros((3 * C,), jnp.float32), 'w_so': jax.random.normal(ks[5], (C, C), jnp.float32) * s, 'b_so': jnp.zeros((C,), jnp.float32), 'w_q': jax.random.normal(ks[6], (C, C), jnp.float32) * s, 'b_q': jnp.zeros((C,), jnp.float32), 'w_kv': jax.random.normal(ks[7], (C, 2 * C), jnp.float32) * s, 'b_kv': jnp.zeros((2 * C,), jnp.float32), 'w_co': jax.random.normal(ks[8], (C, C), jnp.float32) * s, 'b_co': jnp.zeros((C,), jnp.float32), 'w_m1': jax.random.normal(ks[9], (C, 2 * HID), jnp.float32) * s, 'b_m1': jnp.zeros((2 * HID,), jnp.float32), 'w_m2': jax.random.normal(ks[10], (HID, C), jnp.float32) * s, 'b_m2': jnp.zeros((C,), jnp.float32)}
        return inp
    _L0_xcond_all = _L0_xcond_setup()
    _L0_xcond_in = {k: v for k, v in _L0_xcond_all.items() if k in ('w_ada', 'b_ada', 'w_qkv', 'b_qkv', 'w_so', 'b_so', 'w_q', 'b_q', 'w_kv', 'b_kv', 'w_co', 'b_co', 'w_m1', 'b_m1', 'w_m2', 'b_m2')}
    del _L0_xcond_all

    def _L1_xcond_setup():
        import jax, jax.numpy as jnp
        import numpy as np
        EPS = 1e-05

        def _ada_ln(x, c, W_ss, b_ss):
            mu = jnp.mean(x, axis=-1, keepdims=True)
            var = jnp.mean((x - mu) ** 2, axis=-1, keepdims=True)
            h = (x - mu) / jnp.sqrt(var + EPS)
            ss = jax.nn.silu(c) @ W_ss + b_ss
            scale, bias = jnp.split(ss, 2, axis=-1)
            return (1.0 + scale)[:, None, :] * h + bias[:, None, :]
        key = jax.random.key(seed)
        ks = jax.random.split(key, 12)
        B, Lq, Lkv, H = (8, 512, 128, 256)
        s = 0.02
        return {'x_q': jax.random.normal(ks[0], (B, Lq, H), jnp.float32), 'x_kv': jax.random.normal(ks[1], (B, Lkv, H), jnp.float32), 't_vec': jax.random.normal(ks[2], (B, H), jnp.float32), 'Wq': jax.random.normal(ks[3], (H, H), jnp.float32) * s, 'bq': jnp.zeros((H,), jnp.float32), 'Wkv': jax.random.normal(ks[4], (H, 2 * H), jnp.float32) * s, 'bkv': jnp.zeros((2 * H,), jnp.float32), 'Wp': jax.random.normal(ks[5], (H, H), jnp.float32) * s, 'bp': jnp.zeros((H,), jnp.float32), 'Wss_q': jax.random.normal(ks[6], (H, 2 * H), jnp.float32) * s, 'bss_q': jnp.zeros((2 * H,), jnp.float32), 'Wss_kv': jax.random.normal(ks[7], (H, 2 * H), jnp.float32) * s, 'bss_kv': jnp.zeros((2 * H,), jnp.float32)}
    _L1_xcond_all = _L1_xcond_setup()
    _L1_xcond_in = {k: v for k, v in _L1_xcond_all.items() if k in ('Wq', 'bq', 'Wkv', 'bkv', 'Wp', 'bp', 'Wss_q', 'bss_q', 'Wss_kv', 'bss_kv')}
    del _L1_xcond_all

    def _L2_xcond_setup():
        import jax, jax.numpy as jnp
        import numpy as np
        LN_EPS = 1e-06

        def _ln(x):
            mu = jnp.mean(x, axis=-1, keepdims=True)
            var = jnp.var(x, axis=-1, keepdims=True)
            return (x - mu) * jax.lax.rsqrt(var + LN_EPS)
        key = jax.random.key(seed)
        H, NH = (256, 16)
        B, N, S = (4, 256, 77)
        MLP = int(H * 4.0)
        ks = jax.random.split(key, 20)
        s = 1.0 / np.sqrt(H)
        return {'x': jax.random.normal(ks[0], (B, N, H), jnp.float32), 'c': jax.random.normal(ks[1], (B, H), jnp.float32), 'context': jax.random.normal(ks[2], (B, S, H), jnp.float32), 'W_mod': jax.random.normal(ks[3], (H, 6 * H), jnp.float32) * s, 'b_mod': jnp.zeros((6 * H,), jnp.float32), 'W_qkv': jax.random.normal(ks[4], (H, 3 * H), jnp.float32) * s, 'b_qkv': jnp.zeros((3 * H,), jnp.float32), 'W_proj': jax.random.normal(ks[5], (H, H), jnp.float32) * s, 'b_proj': jnp.zeros((H,), jnp.float32), 'W_qc': jax.random.normal(ks[6], (H, H), jnp.float32) * s, 'b_qc': jnp.zeros((H,), jnp.float32), 'W_kvc': jax.random.normal(ks[7], (H, 2 * H), jnp.float32) * s, 'b_kvc': jnp.zeros((2 * H,), jnp.float32), 'W_cproj': jax.random.normal(ks[8], (H, H), jnp.float32) * s, 'b_cproj': jnp.zeros((H,), jnp.float32), 'W_mlp1': jax.random.normal(ks[9], (H, MLP), jnp.float32) * s, 'b_mlp1': jnp.zeros((MLP,), jnp.float32), 'W_mlp2': jax.random.normal(ks[10], (MLP, H), jnp.float32) * (1.0 / np.sqrt(MLP)), 'b_mlp2': jnp.zeros((H,), jnp.float32)}
    _L2_xcond_all = _L2_xcond_setup()
    _L2_xcond_in = {k: v for k, v in _L2_xcond_all.items() if k in ('W_mod', 'b_mod', 'W_qkv', 'b_qkv', 'W_proj', 'b_proj', 'W_qc', 'b_qc', 'W_kvc', 'b_kvc', 'W_cproj', 'b_cproj', 'W_mlp1', 'b_mlp1', 'W_mlp2', 'b_mlp2')}
    del _L2_xcond_all

    def _L3_xcond_setup():
        import jax, jax.numpy as jnp
        import numpy as np
        D = 256
        H = 16
        HD = D // H
        MLP = 4 * D
        EPS = 1e-06
        SCALE = HD ** (-0.5)

        def _p(key, shape, s=0.02):
            return jax.random.normal(key, shape, dtype=jnp.float32) * s

        def _ln(x):
            mu = jnp.mean(x, axis=-1, keepdims=True)
            var = jnp.var(x, axis=-1, keepdims=True)
            return (x - mu) * jax.lax.rsqrt(var + EPS)

        def _heads(t):
            B, L, _ = t.shape
            return t.reshape(B, L, H, HD).transpose(0, 2, 1, 3)

        def _attend(q, k, v):
            attn = jnp.einsum('bhnd,bhsd->bhns', q, k) * SCALE
            attn = jax.nn.softmax(attn, axis=-1)
            o = jnp.einsum('bhns,bhsd->bhnd', attn, v)
            B, _, N, _ = q.shape
            return o.transpose(0, 2, 1, 3).reshape(B, N, D)
        key = jax.random.key(seed)
        ks = jax.random.split(key, 24)
        B, N, S = (4, 256, 77)
        return {'x': jax.random.normal(ks[0], (B, N, D), dtype=jnp.float32), 't_emb': jax.random.normal(ks[1], (B, D), dtype=jnp.float32), 'context': jax.random.normal(ks[2], (B, S, D), dtype=jnp.float32), 'adaln_w': _p(ks[3], (D, 6 * D)), 'adaln_b': _p(ks[4], (6 * D,)), 'qkv_w': _p(ks[5], (D, 3 * D)), 'qkv_b': _p(ks[6], (3 * D,)), 'sa_proj_w': _p(ks[7], (D, D)), 'sa_proj_b': _p(ks[8], (D,)), 'q_w': _p(ks[9], (D, D)), 'q_b': _p(ks[10], (D,)), 'kv_w': _p(ks[11], (D, 2 * D)), 'kv_b': _p(ks[12], (2 * D,)), 'ca_proj_w': _p(ks[13], (D, D)), 'ca_proj_b': _p(ks[14], (D,)), 'fc1_w': _p(ks[15], (D, MLP)), 'fc1_b': _p(ks[16], (MLP,)), 'fc2_w': _p(ks[17], (MLP, D)), 'fc2_b': _p(ks[18], (D,))}
    _L3_xcond_all = _L3_xcond_setup()
    _L3_xcond_in = {k: v for k, v in _L3_xcond_all.items() if k in ('adaln_w', 'adaln_b', 'qkv_w', 'qkv_b', 'sa_proj_w', 'sa_proj_b', 'q_w', 'q_b', 'kv_w', 'kv_b', 'ca_proj_w', 'ca_proj_b', 'fc1_w', 'fc1_b', 'fc2_w', 'fc2_b')}
    del _L3_xcond_all
    return {'x': x, 'cond_1024': cond_1024, 'ctx_1024': ctx_1024, 'L0_xcond_w_ada': _L0_xcond_in['w_ada'], 'L0_xcond_b_ada': _L0_xcond_in['b_ada'], 'L0_xcond_w_qkv': _L0_xcond_in['w_qkv'], 'L0_xcond_b_qkv': _L0_xcond_in['b_qkv'], 'L0_xcond_w_so': _L0_xcond_in['w_so'], 'L0_xcond_b_so': _L0_xcond_in['b_so'], 'L0_xcond_w_q': _L0_xcond_in['w_q'], 'L0_xcond_b_q': _L0_xcond_in['b_q'], 'L0_xcond_w_kv': _L0_xcond_in['w_kv'], 'L0_xcond_b_kv': _L0_xcond_in['b_kv'], 'L0_xcond_w_co': _L0_xcond_in['w_co'], 'L0_xcond_b_co': _L0_xcond_in['b_co'], 'L0_xcond_w_m1': _L0_xcond_in['w_m1'], 'L0_xcond_b_m1': _L0_xcond_in['b_m1'], 'L0_xcond_w_m2': _L0_xcond_in['w_m2'], 'L0_xcond_b_m2': _L0_xcond_in['b_m2'], 'L1_xcond_Wq': _L1_xcond_in['Wq'], 'L1_xcond_bq': _L1_xcond_in['bq'], 'L1_xcond_Wkv': _L1_xcond_in['Wkv'], 'L1_xcond_bkv': _L1_xcond_in['bkv'], 'L1_xcond_Wp': _L1_xcond_in['Wp'], 'L1_xcond_bp': _L1_xcond_in['bp'], 'L1_xcond_Wss_q': _L1_xcond_in['Wss_q'], 'L1_xcond_bss_q': _L1_xcond_in['bss_q'], 'L1_xcond_Wss_kv': _L1_xcond_in['Wss_kv'], 'L1_xcond_bss_kv': _L1_xcond_in['bss_kv'], 'L2_xcond_W_mod': _L2_xcond_in['W_mod'], 'L2_xcond_b_mod': _L2_xcond_in['b_mod'], 'L2_xcond_W_qkv': _L2_xcond_in['W_qkv'], 'L2_xcond_b_qkv': _L2_xcond_in['b_qkv'], 'L2_xcond_W_proj': _L2_xcond_in['W_proj'], 'L2_xcond_b_proj': _L2_xcond_in['b_proj'], 'L2_xcond_W_qc': _L2_xcond_in['W_qc'], 'L2_xcond_b_qc': _L2_xcond_in['b_qc'], 'L2_xcond_W_kvc': _L2_xcond_in['W_kvc'], 'L2_xcond_b_kvc': _L2_xcond_in['b_kvc'], 'L2_xcond_W_cproj': _L2_xcond_in['W_cproj'], 'L2_xcond_b_cproj': _L2_xcond_in['b_cproj'], 'L2_xcond_W_mlp1': _L2_xcond_in['W_mlp1'], 'L2_xcond_b_mlp1': _L2_xcond_in['b_mlp1'], 'L2_xcond_W_mlp2': _L2_xcond_in['W_mlp2'], 'L2_xcond_b_mlp2': _L2_xcond_in['b_mlp2'], 'L3_xcond_adaln_w': _L3_xcond_in['adaln_w'], 'L3_xcond_adaln_b': _L3_xcond_in['adaln_b'], 'L3_xcond_qkv_w': _L3_xcond_in['qkv_w'], 'L3_xcond_qkv_b': _L3_xcond_in['qkv_b'], 'L3_xcond_sa_proj_w': _L3_xcond_in['sa_proj_w'], 'L3_xcond_sa_proj_b': _L3_xcond_in['sa_proj_b'], 'L3_xcond_q_w': _L3_xcond_in['q_w'], 'L3_xcond_q_b': _L3_xcond_in['q_b'], 'L3_xcond_kv_w': _L3_xcond_in['kv_w'], 'L3_xcond_kv_b': _L3_xcond_in['kv_b'], 'L3_xcond_ca_proj_w': _L3_xcond_in['ca_proj_w'], 'L3_xcond_ca_proj_b': _L3_xcond_in['ca_proj_b'], 'L3_xcond_fc1_w': _L3_xcond_in['fc1_w'], 'L3_xcond_fc1_b': _L3_xcond_in['fc1_b'], 'L3_xcond_fc2_w': _L3_xcond_in['fc2_w'], 'L3_xcond_fc2_b': _L3_xcond_in['fc2_b']}

def reference(x, cond_1024, ctx_1024, L0_xcond_w_ada, L0_xcond_b_ada, L0_xcond_w_qkv, L0_xcond_b_qkv, L0_xcond_w_so, L0_xcond_b_so, L0_xcond_w_q, L0_xcond_b_q, L0_xcond_w_kv, L0_xcond_b_kv, L0_xcond_w_co, L0_xcond_b_co, L0_xcond_w_m1, L0_xcond_b_m1, L0_xcond_w_m2, L0_xcond_b_m2, L1_xcond_Wq, L1_xcond_bq, L1_xcond_Wkv, L1_xcond_bkv, L1_xcond_Wp, L1_xcond_bp, L1_xcond_Wss_q, L1_xcond_bss_q, L1_xcond_Wss_kv, L1_xcond_bss_kv, L2_xcond_W_mod, L2_xcond_b_mod, L2_xcond_W_qkv, L2_xcond_b_qkv, L2_xcond_W_proj, L2_xcond_b_proj, L2_xcond_W_qc, L2_xcond_b_qc, L2_xcond_W_kvc, L2_xcond_b_kvc, L2_xcond_W_cproj, L2_xcond_b_cproj, L2_xcond_W_mlp1, L2_xcond_b_mlp1, L2_xcond_W_mlp2, L2_xcond_b_mlp2, L3_xcond_adaln_w, L3_xcond_adaln_b, L3_xcond_qkv_w, L3_xcond_qkv_b, L3_xcond_sa_proj_w, L3_xcond_sa_proj_b, L3_xcond_q_w, L3_xcond_q_b, L3_xcond_kv_w, L3_xcond_kv_b, L3_xcond_ca_proj_w, L3_xcond_ca_proj_b, L3_xcond_fc1_w, L3_xcond_fc1_b, L3_xcond_fc2_w, L3_xcond_fc2_b):
    import jax
    import jax.numpy as jnp

    def _L0_xcond_ref(x, mod, context, w_ada, b_ada, w_qkv, b_qkv, w_so, b_so, w_q, b_q, w_kv, b_kv, w_co, b_co, w_m1, b_m1, w_m2, b_m2):
        import jax, jax.numpy as jnp
        import numpy as np
        C = 256
        H = 16
        D = C // H
        WIN = 128
        SHIFT = 64
        TOPK = 16
        HID = 1024
        EPS = 1e-06

        def _ln(x):
            x32 = x.astype(jnp.float32)
            m = x32.mean(-1, keepdims=True)
            v = jnp.mean((x32 - m) ** 2, axis=-1, keepdims=True)
            return ((x32 - m) * jax.lax.rsqrt(v + EPS)).astype(x.dtype)

        def _self_attn(h, w_qkv, b_qkv, w_so, b_so):
            B, L, _ = h.shape
            qkv = h @ w_qkv + b_qkv
            qkv = jnp.roll(qkv, -SHIFT, axis=1)
            nw = L // WIN
            qkv = qkv.reshape(B, nw, WIN, 3, H, D)
            q, k, v = (qkv[:, :, :, 0], qkv[:, :, :, 1], qkv[:, :, :, 2])
            scores = jnp.einsum('bnqhd,bnkhd->bnhqk', q, k) / jnp.sqrt(jnp.float32(D)).astype(h.dtype)
            attn = jax.nn.softmax(scores, axis=-1)
            o = jnp.einsum('bnhqk,bnkhd->bnqhd', attn, v).reshape(B, L, C)
            o = jnp.roll(o, SHIFT, axis=1)
            return o @ w_so + b_so

        def _topk_cross_attn(h, ctx, w_q, b_q, w_kv, b_kv, w_co, b_co):
            B, L, _ = h.shape
            Lc = ctx.shape[1]
            q = (h @ w_q + b_q).reshape(B, L, H, D)
            kv = (ctx @ w_kv + b_kv).reshape(B, Lc, 2, H, D)
            k, v = (kv[:, :, 0], kv[:, :, 1])
            scores = jnp.einsum('bqhd,bkhd->bhqk', q, k) / jnp.sqrt(jnp.float32(D)).astype(h.dtype)
            top_s, top_i = jax.lax.top_k(scores, TOPK)
            attn = jax.nn.softmax(top_s, axis=-1)
            v_bh = jnp.transpose(v, (0, 2, 1, 3))
            vg = jnp.take_along_axis(v_bh[:, :, None, :, :], top_i[..., None], axis=3)
            o = jnp.einsum('bhqk,bhqkd->bqhd', attn, vg).reshape(B, L, C)
            return o @ w_co + b_co

        def _swiglu(h, w_m1, b_m1, w_m2, b_m2):
            u = h @ w_m1 + b_m1
            a, b = (u[..., :HID], u[..., HID:])
            return jax.nn.silu(a) * b @ w_m2 + b_m2
        m = jax.nn.silu(mod) @ w_ada + b_ada
        sh_msa, sc_msa, g_msa, sh_mca, sc_mca, g_mca, sh_mlp, sc_mlp, g_mlp = [m[:, i * C:(i + 1) * C][:, None, :] for i in range(9)]
        h = _ln(x) * (1 + sc_msa) + sh_msa
        h = _self_attn(h, w_qkv, b_qkv, w_so, b_so)
        x = x + h * g_msa
        h = _ln(x) * (1 + sc_mca) + sh_mca
        h = _topk_cross_attn(h, context, w_q, b_q, w_kv, b_kv, w_co, b_co)
        x = x + h * g_mca
        h = _ln(x) * (1 + sc_mlp) + sh_mlp
        h = _swiglu(h, w_m1, b_m1, w_m2, b_m2)
        x = x + h * g_mlp
        return x

    def _L1_xcond_ref(x_q, x_kv, t_vec, Wq, bq, Wkv, bkv, Wp, bp, Wss_q, bss_q, Wss_kv, bss_kv):
        import jax, jax.numpy as jnp
        import numpy as np
        EPS = 1e-05

        def _ada_ln(x, c, W_ss, b_ss):
            mu = jnp.mean(x, axis=-1, keepdims=True)
            var = jnp.mean((x - mu) ** 2, axis=-1, keepdims=True)
            h = (x - mu) / jnp.sqrt(var + EPS)
            ss = jax.nn.silu(c) @ W_ss + b_ss
            scale, bias = jnp.split(ss, 2, axis=-1)
            return (1.0 + scale)[:, None, :] * h + bias[:, None, :]
        B, Lq, H = x_q.shape
        Lkv = x_kv.shape[1]
        nh = 16
        dh = H // nh
        xq = _ada_ln(x_q, t_vec, Wss_q, bss_q)
        xkv = _ada_ln(x_kv, t_vec, Wss_kv, bss_kv)
        q = (xq @ Wq + bq).reshape(B, Lq, nh, dh)
        kv = (xkv @ Wkv + bkv).reshape(B, Lkv, 2, nh, dh)
        k = kv[:, :, 0]
        v = kv[:, :, 1]
        scores = jnp.einsum('bqhd,bkhd->bhqk', q, k) / jnp.sqrt(jnp.float32(dh))
        attn = jax.nn.softmax(scores, axis=-1)
        out = jnp.einsum('bhqk,bkhd->bqhd', attn, v).reshape(B, Lq, H)
        return x_q + (out @ Wp + bp)

    def _L2_xcond_ref(x, c, context, W_mod, b_mod, W_qkv, b_qkv, W_proj, b_proj, W_qc, b_qc, W_kvc, b_kvc, W_cproj, b_cproj, W_mlp1, b_mlp1, W_mlp2, b_mlp2):
        import jax, jax.numpy as jnp
        import numpy as np
        LN_EPS = 1e-06

        def _ln(x):
            mu = jnp.mean(x, axis=-1, keepdims=True)
            var = jnp.var(x, axis=-1, keepdims=True)
            return (x - mu) * jax.lax.rsqrt(var + LN_EPS)
        B, N, H = x.shape
        NH = 16
        hd = H // NH
        scale = hd ** (-0.5)
        c_proj = jax.nn.silu(c) @ W_mod + b_mod
        shift_a, scale_a, gate_a, shift_m, scale_m, gate_m = jnp.split(c_proj, 6, axis=-1)

        def modulate(t, shift, sc):
            return t * (1 + sc[:, None]) + shift[:, None]
        x_norm = modulate(_ln(x), shift_a, scale_a)
        qkv = x_norm @ W_qkv + b_qkv
        q, k, v = jnp.split(qkv, 3, axis=-1)
        q = q.reshape(B, N, NH, hd).transpose(0, 2, 1, 3)
        k = k.reshape(B, N, NH, hd).transpose(0, 2, 1, 3)
        v = v.reshape(B, N, NH, hd).transpose(0, 2, 1, 3)
        attn_w = jax.nn.softmax(jnp.einsum('bhqd,bhkd->bhqk', q, k) * scale, axis=-1)
        attn_out = jnp.einsum('bhqk,bhkd->bhqd', attn_w, v)
        attn_out = attn_out.transpose(0, 2, 1, 3).reshape(B, N, H)
        attn_out = attn_out @ W_proj + b_proj
        x = x + gate_a[:, None] * attn_out
        S = context.shape[1]
        q_c = _ln(x) @ W_qc + b_qc
        kv_c = _ln(context) @ W_kvc + b_kvc
        k_c, v_c = jnp.split(kv_c, 2, axis=-1)
        q_c = q_c.reshape(B, N, NH, hd).transpose(0, 2, 1, 3)
        k_c = k_c.reshape(B, S, NH, hd).transpose(0, 2, 1, 3)
        v_c = v_c.reshape(B, S, NH, hd).transpose(0, 2, 1, 3)
        c_attn_w = jax.nn.softmax(jnp.einsum('bhqd,bhsd->bhqs', q_c, k_c) * scale, axis=-1)
        c_attn_out = jnp.einsum('bhqs,bhsd->bhqd', c_attn_w, v_c)
        c_attn_out = c_attn_out.transpose(0, 2, 1, 3).reshape(B, N, H)
        c_attn_out = c_attn_out @ W_cproj + b_cproj
        x = x + c_attn_out
        x_norm2 = modulate(_ln(x), shift_m, scale_m)
        h = jax.nn.gelu(x_norm2 @ W_mlp1 + b_mlp1)
        h = h @ W_mlp2 + b_mlp2
        x = x + gate_m[:, None] * h
        return x

    def _L3_xcond_ref(x, t_emb, context, adaln_w, adaln_b, qkv_w, qkv_b, sa_proj_w, sa_proj_b, q_w, q_b, kv_w, kv_b, ca_proj_w, ca_proj_b, fc1_w, fc1_b, fc2_w, fc2_b):
        import jax, jax.numpy as jnp
        import numpy as np
        D = 256
        H = 16
        HD = D // H
        MLP = 4 * D
        EPS = 1e-06
        SCALE = HD ** (-0.5)

        def _p(key, shape, s=0.02):
            return jax.random.normal(key, shape, dtype=jnp.float32) * s

        def _ln(x):
            mu = jnp.mean(x, axis=-1, keepdims=True)
            var = jnp.var(x, axis=-1, keepdims=True)
            return (x - mu) * jax.lax.rsqrt(var + EPS)

        def _heads(t):
            B, L, _ = t.shape
            return t.reshape(B, L, H, HD).transpose(0, 2, 1, 3)

        def _attend(q, k, v):
            attn = jnp.einsum('bhnd,bhsd->bhns', q, k) * SCALE
            attn = jax.nn.softmax(attn, axis=-1)
            o = jnp.einsum('bhns,bhsd->bhnd', attn, v)
            B, _, N, _ = q.shape
            return o.transpose(0, 2, 1, 3).reshape(B, N, D)
        B, N, _ = x.shape
        S = context.shape[1]
        mod = jax.nn.silu(t_emb) @ adaln_w + adaln_b
        sh_sa, sc_sa, g_sa, sh_ff, sc_ff, g_ff = jnp.split(mod[:, None, :], 6, axis=-1)
        xm = _ln(x) * (1.0 + sc_sa) + sh_sa
        qkv = (xm @ qkv_w + qkv_b).reshape(B, N, 3, H, HD)
        q = qkv[:, :, 0].transpose(0, 2, 1, 3)
        k = qkv[:, :, 1].transpose(0, 2, 1, 3)
        v = qkv[:, :, 2].transpose(0, 2, 1, 3)
        x_sa = _attend(q, k, v) @ sa_proj_w + sa_proj_b
        x = x + g_sa * x_sa
        xn = _ln(x)
        q = _heads(xn @ q_w + q_b)
        kv = (context @ kv_w + kv_b).reshape(B, S, 2, H, HD)
        k = kv[:, :, 0].transpose(0, 2, 1, 3)
        v = kv[:, :, 1].transpose(0, 2, 1, 3)
        x_ca = _attend(q, k, v) @ ca_proj_w + ca_proj_b
        x = x + x_ca
        xm = _ln(x) * (1.0 + sc_ff) + sh_ff
        h = jax.nn.gelu(xm @ fc1_w + fc1_b, approximate=True)
        x_ff = h @ fc2_w + fc2_b
        x = x + g_ff * x_ff
        return x
    x = _L0_xcond_ref(x, cond_1024, ctx_1024, L0_xcond_w_ada, L0_xcond_b_ada, L0_xcond_w_qkv, L0_xcond_b_qkv, L0_xcond_w_so, L0_xcond_b_so, L0_xcond_w_q, L0_xcond_b_q, L0_xcond_w_kv, L0_xcond_b_kv, L0_xcond_w_co, L0_xcond_b_co, L0_xcond_w_m1, L0_xcond_b_m1, L0_xcond_w_m2, L0_xcond_b_m2)
    x = _L1_xcond_ref(x, ctx_1024, cond_1024, L1_xcond_Wq, L1_xcond_bq, L1_xcond_Wkv, L1_xcond_bkv, L1_xcond_Wp, L1_xcond_bp, L1_xcond_Wss_q, L1_xcond_bss_q, L1_xcond_Wss_kv, L1_xcond_bss_kv)
    x = _L2_xcond_ref(x, cond_1024, ctx_1024, L2_xcond_W_mod, L2_xcond_b_mod, L2_xcond_W_qkv, L2_xcond_b_qkv, L2_xcond_W_proj, L2_xcond_b_proj, L2_xcond_W_qc, L2_xcond_b_qc, L2_xcond_W_kvc, L2_xcond_b_kvc, L2_xcond_W_cproj, L2_xcond_b_cproj, L2_xcond_W_mlp1, L2_xcond_b_mlp1, L2_xcond_W_mlp2, L2_xcond_b_mlp2)
    x = _L3_xcond_ref(x, cond_1024, ctx_1024, L3_xcond_adaln_w, L3_xcond_adaln_b, L3_xcond_qkv_w, L3_xcond_qkv_b, L3_xcond_sa_proj_w, L3_xcond_sa_proj_b, L3_xcond_q_w, L3_xcond_q_b, L3_xcond_kv_w, L3_xcond_kv_b, L3_xcond_ca_proj_w, L3_xcond_ca_proj_b, L3_xcond_fc1_w, L3_xcond_fc1_b, L3_xcond_fc2_w, L3_xcond_fc2_b)
    return x

_drawn_inputs = setup_inputs


def setup_inputs(seed=0):
    import zlib

    import numpy as np

    out = dict(_drawn_inputs(seed))
    spreads = {'L0_xcond_b_ada': (0.0, 0.387),
     'L0_xcond_b_qkv': (0.0, 0.8),
     'L0_xcond_b_so': (0.0, 0.376),
     'L0_xcond_b_q': (0.0, 0.8),
     'L0_xcond_b_kv': (0.0, 0.8),
     'L0_xcond_b_co': (0.0, 0.399),
     'L0_xcond_b_m1': (0.0, 0.8),
     'L0_xcond_b_m2': (0.0, 2.0),
     'L1_xcond_bq': (0.0, 2.0),
     'L1_xcond_bkv': (0.0, 0.8),
     'L1_xcond_bp': (0.0, 0.8),
     'L1_xcond_bss_q': (0.0, 2.0),
     'L1_xcond_bss_kv': (0.0, 2.0),
     'L2_xcond_b_mod': (0.0, 0.617),
     'L2_xcond_b_qkv': (0.0, 0.8),
     'L2_xcond_b_proj': (0.0, 0.8),
     'L2_xcond_b_qc': (0.0, 2.0),
     'L2_xcond_b_kvc': (0.0, 0.8),
     'L2_xcond_b_cproj': (0.0, 0.8),
     'L2_xcond_b_mlp1': (0.0, 0.8),
     'L2_xcond_b_mlp2': (0.0, 0.8)}
    factors = {'L0_xcond_w_qkv': 8.0,
     'L0_xcond_w_so': 5.709,
     'L0_xcond_w_q': 8.0,
     'L0_xcond_w_kv': 4.142,
     'L0_xcond_w_co': 3.629,
     'L0_xcond_w_m1': 7.295,
     'L0_xcond_w_m2': 7.28,
     'L1_xcond_Wq': 64.0,
     'L1_xcond_Wss_q': 64.0,
     'L3_xcond_adaln_w': 2.86,
     'L3_xcond_adaln_b': 8.0,
     'L3_xcond_qkv_w': 5.441,
     'L3_xcond_qkv_b': 21.977,
     'L3_xcond_sa_proj_w': 6.037,
     'L3_xcond_sa_proj_b': 62.053,
     'L3_xcond_q_w': 64.0,
     'L3_xcond_q_b': 64.0,
     'L3_xcond_kv_b': 64.0,
     'L3_xcond_ca_proj_b': 31.944,
     'L3_xcond_fc1_w': 3.578,
     'L3_xcond_fc1_b': 40.247,
     'L3_xcond_fc2_w': 3.464,
     'L3_xcond_fc2_b': 61.805,
     'L1_xcond_Wkv': 5.866,
     'L1_xcond_Wp': 5.748,
     'L1_xcond_Wss_kv': 8.0,
     'L2_xcond_W_qc': 3.645,
     'L3_xcond_kv_w': 8.0,
     'L3_xcond_ca_proj_w': 8.0}
    for name, (base, spread) in spreads.items():
        noise = np.random.default_rng([zlib.crc32(name.encode()), seed]).standard_normal(out[name].shape)
        drawn = base * np.exp(spread * noise) if base else spread * noise
        out[name] = jnp.asarray(drawn.astype(out[name].dtype))
    for name, factor in factors.items():
        out[name] = (out[name] * factor).astype(out[name].dtype)
    return out
```

```python
from contextlib import ExitStack

import concourse.bass as bass
import concourse.mybir as mybir

F32 = mybir.dt.float32
ALU = mybir.AluOpType
ACT = mybir.ActivationFunctionType
AX = mybir.AxisListType

P = 128
B, L, C = 4, 512, 256
LC = 64
H, D = 16, 16
CH = C // P
TT = L // P
HC = H // CH
HID = 1024
MC = HID // P
LANES = 2
PASSES = B // LANES
SHIFT = 64
TOPK = 16
SCALE = D ** -0.5
PAD = 1024
RP = 3
RT = 2
LOWEST = -3.4028234e38

MODS = [("L0_xcond_w_ada", "L0_xcond_b_ada", 9), ("L1_xcond_Wss_q", "L1_xcond_bss_q", 2),
        ("L1_xcond_Wss_kv", "L1_xcond_bss_kv", 2), ("L2_xcond_W_mod", "L2_xcond_b_mod", 6),
        ("L3_xcond_adaln_w", "L3_xcond_adaln_b", 6)]
NMOD = sum(n for _, _, n in MODS)
SCALES = [1, 4, 7, 9, 11, 14, 17, 20, 23]
GATES = [2, 5, 8, 15, 18, 21, 24]

COLS = [("L0_xcond_b_qkv", 4), ("L0_xcond_b_q", 2), ("L0_xcond_b_kv", 2), ("L0_xcond_b_m1", 16),
        ("L1_xcond_bq", 2), ("L1_xcond_bkv", 2), ("L2_xcond_b_qkv", 4), ("L2_xcond_b_qc", 2),
        ("L2_xcond_b_kvc", 2), ("L2_xcond_b_mlp1", 8), ("L3_xcond_qkv_b", 4), ("L3_xcond_q_b", 2),
        ("L3_xcond_kv_b", 2), ("L3_xcond_fc1_b", 8)]

SITES = [
    dict(name="self0", kind="win", layer=0, ln=(1e-6, 1, 0), wqkv="L0_xcond_w_qkv", bqkv="L0_xcond_b_qkv",
         wo="L0_xcond_w_so", bo="L0_xcond_b_so", gate=2),
    dict(name="cross0", kind="topk", layer=0, ln=(1e-6, 4, 3), ctx_ln=None, wq="L0_xcond_w_q", bq="L0_xcond_b_q",
         wkv="L0_xcond_w_kv", bkv="L0_xcond_b_kv", wo="L0_xcond_w_co", bo="L0_xcond_b_co", gate=5),
    dict(name="mlp0", kind="swiglu", layer=0, ln=(1e-6, 7, 6), w1="L0_xcond_w_m1", b1="L0_xcond_b_m1",
         w2="L0_xcond_w_m2", bo="L0_xcond_b_m2", gate=8),
    dict(name="cross1", kind="cross", layer=1, ln=(1e-5, 9, 10), ctx_ln=(1e-5, 11, 12), wq="L1_xcond_Wq",
         bq="L1_xcond_bq", wkv="L1_xcond_Wkv", bkv="L1_xcond_bkv", wo="L1_xcond_Wp", bo="L1_xcond_bp", gate=None),
    dict(name="self2", kind="full", layer=2, ln=(1e-6, 14, 13), wqkv="L2_xcond_W_qkv", bqkv="L2_xcond_b_qkv",
         wo="L2_xcond_W_proj", bo="L2_xcond_b_proj", gate=15),
    dict(name="cross2", kind="cross", layer=2, ln=(1e-6, None, None), ctx_ln=(1e-6, None, None),
         wq="L2_xcond_W_qc", bq="L2_xcond_b_qc", wkv="L2_xcond_W_kvc", bkv="L2_xcond_b_kvc",
         wo="L2_xcond_W_cproj", bo="L2_xcond_b_cproj", gate=None),
    dict(name="mlp2", kind="gelu", layer=2, ln=(1e-6, 17, 16), w1="L2_xcond_W_mlp1", b1="L2_xcond_b_mlp1",
         w2="L2_xcond_W_mlp2", bo="L2_xcond_b_mlp2", gate=18),
    dict(name="self3", kind="full", layer=3, ln=(1e-6, 20, 19), wqkv="L3_xcond_qkv_w", bqkv="L3_xcond_qkv_b",
         wo="L3_xcond_sa_proj_w", bo="L3_xcond_sa_proj_b", gate=21),
    dict(name="cross3", kind="cross", layer=3, ln=(1e-6, None, None), ctx_ln=None, wq="L3_xcond_q_w",
         bq="L3_xcond_q_b", wkv="L3_xcond_kv_w", bkv="L3_xcond_kv_b", wo="L3_xcond_ca_proj_w",
         bo="L3_xcond_ca_proj_b", gate=None),
    dict(name="mlp3", kind="gelu", layer=3, ln=(1e-6, 23, 22), w1="L3_xcond_fc1_w", b1="L3_xcond_fc1_b",
         w2="L3_xcond_fc2_w", bo="L3_xcond_fc2_b", gate=24),
]
SELF, CROSS, MLP = ("win", "full"), ("topk", "cross"), ("swiglu", "gelu")
KEYS = {"win": P, "full": L, "topk": LC, "cross": LC}


class Signal:

    def __init__(self, sem, known, step=1):
        self.sem, self.known, self.step = sem, known or {}, step
        self.order = {}

    def mark(self, event):
        assert event not in self.order, event
        self.order[event] = len(self.order) + 1
        return self.step

    def at(self, event):
        return self.step * self.known.get(event, 1)


def units_of(site):
    nh = PAD // KEYS[site["kind"]]
    return [(t, h0, nh) for t in range(TT) for h0 in range(0, H, nh)]


def build(nc, a, out, known):
    ctx = ExitStack()
    with ctx:
        def sb(name, shape):
            return ctx.enter_context(nc.sbuf_tensor(name, shape, F32))

        x = sb("x", [P, LANES, TT, C])
        hn = sb("hn", [P, TT, C])
        hT = sb("hT", [P, LANES, CH, L])
        qT = sb("qT", [P, LANES, CH, L])
        kT = sb("kT", [P, LANES, CH, L])
        kd = sb("kd", [P, CH, HC, L])
        vp = sb("vp", [P, LANES, TT, H // 2, 2, 2 * D])
        pr = sb("pr", [P, RP, PAD])
        pT = sb("pT", [P, RT, PAD // P, P])
        oT = sb("oT", [P, LANES, CH, L])
        tmp = sb("tmp", [P, TT, C])
        rk = sb("rk", [P, PAD])
        wA = sb("wA", [P, 16 * C])
        wB = sb("wB", [P, 16 * C])
        wM = sb("wM", [P, 24 * C])
        rows = sb("rows", [P, 2, 5, C])
        gate = sb("gate", [P, LANES, C])
        ctok = sb("ctok", [P, C])
        cn = sb("cn", [P, C])
        cT = sb("cT", [P, CH, LANES, 2, LC])
        kTc = sb("kTc", [P, CH, LANES, LC])
        kc = sb("kc", [P, LANES, CH, HC, LC])
        vc = sb("vc", [P, LANES, H // 2, 2 * D])
        ident = sb("ident", [P, P])
        mask = sb("mask", [P, HC])
        bcol = sb("bcol", [P, P])
        modT = sb("modT", [P, NMOD * CH, B])
        cur = sb("cur", [P, NMOD * CH, LANES])
        stats = sb("stats", [P, 2, TT, 6])
        mv = sb("mv", [P, 2, TT, 2])
        rstd = sb("rstd", [P, 2, TT])
        cstats = sb("cstats", [P, 10])
        half = sb("half", [P, TT])
        mx = sb("mx", [P, RP, H])
        sm = sb("sm", [P, RP, H])
        top = sb("top", [P, 2, H, 8])
        condT = sb("condT", [P, CH, B])
        crow = tmp[0:B, 0, :]
        grow = pT[0:B].rearrange("p r a b -> p (r a b)")[:, 0:len(GATES) * C]
        pads = [ctx.enter_context(nc.psum_tensor(f"pad{i}", [P, PAD], F32)) for i in range(4)]
        brow = rk[:, 0:P]
        gates_dram = nc.dram_tensor("gate_rows", (B, len(GATES), C), F32, kind="Internal").ap()

        signals = {}

        def signal(name, step=1):
            sem = ctx.enter_context(nc.semaphore(name))
            signals[name] = Signal(sem, known.get(name), step)
            return signals[name]

        tensor = signal("tensor_filled")
        scalar = signal("scalar_wrote")
        vector = signal("vector_wrote")
        pool = signal("pool_wrote")
        set_tensor = signal("setup_tensor")
        set_scalar = signal("setup_scalar")
        set_vector = signal("setup_vector")
        set_pool = signal("setup_pool")
        load_cond = signal("cond_loaded", 16)
        load_rows = signal("bias_rows_loaded", 16)
        load_mod = [signal(f"mod_weights_loaded{i}", 16) for i in range(16)]
        gates_out = signal("gates_stored", 16)
        load_x = [signal(f"x_loaded{u}", 16) for u in range(LANES)]
        load_ctx = signal("context_loaded", 16)
        load_w = [signal(f"weights_loaded{i}", 16) for i in range(len(SITES))]
        load_gate = signal("gate_loaded", 16)
        stored = signal("stored", 16)
        in_pass = [tensor, scalar, vector, pool, *load_x, load_ctx, *load_w, load_gate, stored]
        arrived = ctx.enter_context(nc.semaphore("arrived"))
        resume = {e: ctx.enter_context(nc.semaphore(f"resume_{e}")) for e in ("tensor", "scalar", "vector", "pool")}

        def end_pass(eng, name):
            eng.wait_ge(stored.sem, stored.at(("start", LANES - 1)))
            eng.sem_inc(arrived, 1)
            eng.wait_ge(resume[name], 1)
            eng.sem_clear(resume[name])

        place = {}
        for s in SITES:
            region, par = (wA, 0) if s["layer"] % 2 == 0 else (wB, 1)
            first = 0 if s["kind"] in SELF or s["layer"] == 1 else 8 * C
            n = s["name"]
            if s["kind"] in SELF:
                place[n] = dict(qkv=region[:, 0:6 * C].rearrange("p (c n) -> p c n", c=CH),
                                o=region[:, 6 * C:8 * C].rearrange("p (c n) -> p c n", c=CH),
                                vrow=rows[:, par, 0, :], orow=rows[:, par, 1, :])
            elif s["kind"] in CROSS:
                place[n] = dict(q=region[:, first:first + 2 * C].rearrange("p (c n) -> p c n", c=CH),
                                kv=region[:, first + 2 * C:first + 6 * C].rearrange("p (c n) -> p c n", c=CH),
                                o=region[:, first + 6 * C:first + 8 * C].rearrange("p (c n) -> p c n", c=CH),
                                vrow=rows[:, par, 2, :], orow=rows[:, par, 3, :])
            else:
                up = 2 * HID if s["kind"] == "swiglu" else HID
                place[n] = dict(w1=wM[:, 0:CH * up].rearrange("p (c n) -> p c n", c=CH),
                                w2=wM[:, 16 * C:24 * C].rearrange("p (m n) -> p m n", m=MC),
                                orow=rows[:, par, 4, :])
        hid = kd[:, :, :, :].rearrange("p c h l -> p (c h) l").rearrange("p (u m) l -> p u m l", u=LANES)

        col_of, n = {}, 0
        for name, k in COLS:
            col_of[name] = n
            n += k
        mod_col = n
        nrows = mod_col + NMOD * CH
        assert nrows <= P

        def column(name, i):
            return bcol[:, col_of[name] + i:col_of[name] + i + 1]

        def modulation(vec, c, u):
            return cur[:, vec * CH + c, u:u + 1]

        def cols(pad, shape):
            return pads[pad][:, :].rearrange("p (a b) -> p a b", a=shape)

        attn_units = []
        first_unit = {}
        for s in SITES:
            if s["kind"] in KEYS:
                for u in range(LANES):
                    first_unit[s["name"], u] = len(attn_units)
                    attn_units += [(s, u, *x_) for x_ in units_of(s)]

        def last_user_of_weights(site):
            names = [s["name"] for s in SITES]
            i = names.index(site["name"])
            mine = (site["kind"] in MLP, site["layer"] % 2)
            if site["kind"] in MLP:
                prev = [s for s in SITES[:i] if s["kind"] in MLP]
            else:
                prev = [s for s in SITES[:i] if s["kind"] not in MLP and s["layer"] == site["layer"] - 2]
            return ("out", prev[-1]["name"], LANES - 1) if prev else None

        block = ctx.enter_context(nc.Block())

        @block.sync
        def _(sp):
            sp.dma_start(crow, a["cond_1024"]).then_inc(load_cond.sem, load_cond.mark("cond"))
            for name, k in COLS:
                r = col_of[name]
                sp.dma_start(brow[r:r + k, :], a[name][0:k * P].rearrange("(k p) -> k p", p=P)) \
                    .then_inc(load_rows.sem, load_rows.mark(name))
            r = mod_col
            for _, name, k in MODS:
                sp.dma_start(brow[r:r + CH * k, :], a[name].rearrange("(k p) -> k p", p=P)) \
                    .then_inc(load_rows.sem, load_rows.mark(name))
                r += CH * k
            ring = kd[:, :, :, :].rearrange("p c h l -> p (c h l)").rearrange("p (s c n) -> p s c n", s=16, c=CH)
            vec = 0
            for w, _, k in MODS:
                for i in range(k):
                    if vec >= 16:
                        sp.wait_ge(set_tensor.sem, set_tensor.at(("mod", vec - 16)))
                    ld = load_mod[vec % 16]
                    sp.dma_start(ring[:, vec % 16], a[w][:, i * C:(i + 1) * C].rearrange("(c p) n -> p c n", p=P)) \
                        .then_inc(ld.sem, ld.mark(vec))
                    vec += 1
            sp.wait_ge(set_vector.sem, set_vector.at("gate rows"))
            sp.dma_start(gates_dram.rearrange("b g n -> b (g n)"), grow) \
                .then_inc(gates_out.sem, gates_out.mark("gates"))
            sp.wait_ge(gates_out.sem, gates_out.at("gates"))

            with sp.Fori(0, PASSES) as it:
                def load_weights(i):
                    s, pl, ld = SITES[i], place[SITES[i]["name"]], load_w[i]
                    before = last_user_of_weights(s)
                    if before:
                        sp.wait_ge(tensor.sem, tensor.at(before))
                        sp.wait_ge(vector.sem, vector.at(("branch",) + before[1:]))

                    def w(dst, src):
                        sp.dma_start(dst, src).then_inc(ld.sem, ld.mark((s["name"], len(ld.order))))

                    def row(dst, src):
                        w(dst, src.unsqueeze(0).broadcast_to([P, C]))

                    if s["kind"] in SELF:
                        w(pl["qkv"], a[s["wqkv"]].rearrange("(c p) n -> p c n", p=P))
                        row(pl["vrow"], a[s["bqkv"]][2 * C:3 * C])
                    elif s["kind"] in CROSS:
                        w(pl["q"], a[s["wq"]].rearrange("(c p) n -> p c n", p=P))
                        w(pl["kv"], a[s["wkv"]].rearrange("(c p) n -> p c n", p=P))
                        row(pl["vrow"], a[s["bkv"]][C:2 * C])
                    else:
                        w(pl["w1"], a[s["w1"]].rearrange("(c p) n -> p c n", p=P))
                        w(pl["w2"], a[s["w2"]].rearrange("(m p) n -> p m n", p=P))
                    if s["kind"] not in MLP:
                        w(pl["o"], a[s["wo"]].rearrange("(c p) n -> p c n", p=P))
                    row(pl["orow"], a[s["bo"]])

                for u in range(LANES):
                    b = it * LANES + u
                    xb = a["x"][bass.ds(b, 1), :, :].rearrange("o t c -> (o t) c")
                    ld = load_x[u]
                    sp.dma_start(x[:, u, 0:TT - 1, :],
                                 xb[SHIFT:SHIFT + (TT - 1) * P, :].rearrange("(t p) c -> p t c", p=P)) \
                        .then_inc(ld.sem, ld.mark("tiles"))
                    sp.dma_start(x[0:P - SHIFT, u, TT - 1, :], xb[L - SHIFT:L, :]).then_inc(ld.sem, ld.mark("end"))
                    sp.dma_start(x[P - SHIFT:P, u, TT - 1, :], xb[0:SHIFT, :]).then_inc(ld.sem, ld.mark("start"))
                sp.dma_start(ctok[:, :], a["ctx_1024"][bass.ds(it * LANES, LANES), :, :].rearrange("u t c -> (u t) c")) \
                    .then_inc(load_ctx.sem, load_ctx.mark("context"))
                loaded = set()
                for i, s in enumerate(SITES):
                    if last_user_of_weights(s) is None:
                        load_weights(i)
                        loaded.add(i)
                gated = [s for s in SITES if s["gate"] is not None]
                for i, s in enumerate(SITES):
                    if s["gate"] is not None:
                        g = gated.index(s)
                        if g >= 1:
                            sp.wait_ge(pool.sem, pool.at(("gated", gated[g - 1]["name"], LANES - 1)))
                        gi = GATES.index(s["gate"])
                        sp.dma_start(gate[:, :, :],
                                     gates_dram[bass.ds(it * LANES, LANES), gi, :].unsqueeze(0)
                                     .broadcast_to([P, LANES, C])) \
                            .then_inc(load_gate.sem, load_gate.mark(s["name"]))
                    for j in range(i + 1, len(SITES)):
                        before = last_user_of_weights(SITES[j])
                        if j not in loaded and before and before[1] == s["name"]:
                            load_weights(j)
                            loaded.add(j)
                assert len(loaded) == len(SITES)
                for u in range(LANES):
                    last = SITES[-1]["name"]
                    sp.wait_ge(pool.sem, pool.at(("x", last, u)))
                    ob = out[bass.ds(it * LANES + u, 1), :, :].rearrange("o t c -> (o t) c")
                    sp.dma_start(ob[SHIFT:SHIFT + (TT - 1) * P, :].rearrange("(t p) c -> p t c", p=P),
                                 x[:, u, 0:TT - 1, :]).then_inc(stored.sem, stored.mark(("tiles", u)))
                    sp.dma_start(ob[L - SHIFT:L, :], x[0:P - SHIFT, u, TT - 1, :]) \
                        .then_inc(stored.sem, stored.mark(("end", u)))
                    sp.dma_start(ob[0:SHIFT, :], x[P - SHIFT:P, u, TT - 1, :]) \
                        .then_inc(stored.sem, stored.mark(("start", u)))
                sp.wait_ge(stored.sem, stored.at(("start", LANES - 1)))
                sp.wait_ge(arrived, len(resume))
                for sig in in_pass:
                    sp.sem_clear(sig.sem)
                sp.sem_clear(arrived)
                for sem in resume.values():
                    sp.sem_inc(sem, 1)

        @block.gpsimd
        def _(gp):
            gp.memset(ident[:, :], 0.0).then_inc(set_pool.sem, set_pool.mark("ident 0"))
            gp.memset(mask[:, :], 1.0).then_inc(set_pool.sem, set_pool.mark("mask 1"))
            gp.memset(vp[:, :, :, :, :, :], 0.0).then_inc(set_pool.sem, set_pool.mark("vp"))
            gp.memset(vc[:, :, :, :], 0.0).then_inc(set_pool.sem, set_pool.mark("vc"))
            gp.memset(half[:, :], -0.5).then_inc(set_pool.sem, set_pool.mark("half"))
            gp.wait_ge(set_pool.sem, set_pool.at("half"))
            gp.affine_select(out=ident[:, :], in_=ident[:, :], compare_op=ALU.not_equal, fill=1.0, base=0,
                             pattern=[[-1, P]], channel_multiplier=1) \
                .then_inc(set_pool.sem, set_pool.mark("ident"))
            gp.affine_select(out=mask[:, :], in_=mask[:, :], compare_op=ALU.is_ge, fill=0.0, base=0,
                             pattern=[[-D, HC]], channel_multiplier=1) \
                .then_inc(set_pool.sem, set_pool.mark("mask low"))
            gp.wait_ge(set_pool.sem, set_pool.at("mask low"))
            gp.affine_select(out=mask[:, :], in_=mask[:, :], compare_op=ALU.is_ge, fill=0.0, base=D - 1,
                             pattern=[[D, HC]], channel_multiplier=-1) \
                .then_inc(set_pool.sem, set_pool.mark("mask"))
            gp.wait_ge(set_pool.sem, set_pool.at("mask"))
            gp.wait_ge(set_tensor.sem, set_tensor.at("gates"))

            with gp.Fori(0, PASSES) as it:
                for s in SITES:
                    name, kind = s["name"], s["kind"]
                    if kind in CROSS:
                        if s["ctx_ln"]:
                            gp.wait_ge(vector.sem, vector.at(("ctx stats", name)))
                            gp.tensor_scalar(cstats[:, 8:9], cstats[:, 7:8], s["ctx_ln"][0], None, ALU.add) \
                                .then_inc(pool.sem, pool.mark(("ctx var", name)))
                            gp.wait_ge(pool.sem, pool.at(("ctx var", name)))
                            gp.tensor_tensor(cstats[:, 9:10], cstats[:, 8:9], half[:, 0:1], ALU.pow) \
                                .then_inc(pool.sem, pool.mark(("ctx rstd", name)))
                        gp.wait_ge(scalar.sem, scalar.at(("ctx keys", name, CH - 1)))
                        for u in range(LANES):
                            for c in range(CH):
                                gp.tensor_tensor(kc[:, u, c], kTc[:, c, u, :].unsqueeze(1).broadcast_to([P, HC, LC]),
                                                 mask[:, :].unsqueeze(2).broadcast_to([P, HC, LC]), ALU.mult) \
                                    .then_inc(pool.sem, pool.mark(("ctx blocks", name, u, c)))
                    for u in range(LANES):
                        gp.wait_ge(vector.sem, vector.at(("stats", name, u)))
                        gp.tensor_scalar(rstd[:, u, :], mv[:, u, :, 1], s["ln"][0], None, ALU.add) \
                            .then_inc(pool.sem, pool.mark(("var", name, u)))
                        gp.wait_ge(pool.sem, pool.at(("var", name, u)))
                        gp.tensor_tensor(rstd[:, u, :], rstd[:, u, :], half[:, :], ALU.pow) \
                            .then_inc(pool.sem, pool.mark(("rstd", name, u)))
                    if kind in KEYS:
                        for u in range(LANES):
                            if kind in SELF:
                                gp.wait_ge(scalar.sem, scalar.at(("keys", name, u)))
                                if u:
                                    gp.wait_ge(tensor.sem, tensor.at(("scores", first_unit[name, u] - 1)))
                                for c in range(CH):
                                    for h in range(HC):
                                        gp.tensor_scalar(kd[:, c, h, :], kT[:, u, c, :], mask[:, h:h + 1], None,
                                                         ALU.mult) \
                                            .then_inc(pool.sem, pool.mark(("blocks", name, u, c, h)))
                            for j, (t, h0, nh) in enumerate(units_of(s)):
                                n = first_unit[name, u] + j
                                nk = KEYS[kind]
                                p3 = pr[:, n % RP, :].rearrange("p (h k) -> p h k", k=nk)
                                if kind == "topk":
                                    gp.wait_ge(scalar.sem, scalar.at(("exp", n)))
                                    gp.wait_ge(vector.sem, vector.at(("selected", n)))
                                    gp.tensor_tensor(pr[:, n % RP, :], pr[:, n % RP, :], rk[:, :], ALU.mult) \
                                        .then_inc(pool.sem, pool.mark(("kept", n)))
                                gp.wait_ge(vector.sem, vector.at(("1/sum", n)))
                                gp.tensor_tensor(p3, p3, sm[:, n % RP, 0:nh].unsqueeze(2).broadcast_to([P, nh, nk]),
                                                 ALU.mult).then_inc(pool.sem, pool.mark(("probs", n)))
                    for u in range(LANES):
                        gp.wait_ge(vector.sem, vector.at(("branch", name, u)))
                        if s["gate"] is not None:
                            gp.wait_ge(load_gate.sem, load_gate.at(name))
                            gp.tensor_tensor(tmp[:, :, :], tmp[:, :, :],
                                             gate[:, u, :].unsqueeze(1).broadcast_to([P, TT, C]), ALU.mult) \
                                .then_inc(pool.sem, pool.mark(("gated", name, u)))
                            gp.wait_ge(pool.sem, pool.at(("gated", name, u)))
                        gp.tensor_tensor(x[:, u], x[:, u], tmp[:, :, :], ALU.add) \
                            .then_inc(pool.sem, pool.mark(("x", name, u)))
                end_pass(gp, "pool")

        @block.scalar
        def _(act):
            act.wait_ge(set_tensor.sem, set_tensor.at("cond"))
            act.activation(condT[:, :, :].rearrange("p c b -> p (c b)"), pads[0][:, 0:CH * B], ACT.Silu) \
                .then_inc(set_scalar.sem, set_scalar.mark("silu"))

            with act.Fori(0, PASSES) as it:
                def modulate(dst, src, vecs, c, u, event):
                    if vecs[1] is None:
                        i = act.activation(dst, src, ACT.Copy)
                    else:
                        i = act.activation(dst, src, ACT.Identity, bias=modulation(vecs[2], c, u),
                                           scale=modulation(vecs[1], c, u))
                    i.then_inc(scalar.sem, scalar.mark(event))

                act.wait_ge(vector.sem, vector.at("modulation"))
                for s in SITES:
                    name, kind = s["name"], s["kind"]
                    if kind in CROSS:
                        act.wait_ge(tensor.sem, tensor.at(("ctx turned", name)))
                        lnv = s["ctx_ln"] or (0, None, None)
                        for c in range(CH):
                            for u in range(LANES):
                                src = pads[1][:, c * P + u * LC:c * P + (u + 1) * LC]
                                modulate(cT[:, c, u], src.unsqueeze(1).broadcast_to([P, 2, LC]), lnv, c, u,
                                         ("ctx", name, c, u))
                        act.wait_ge(tensor.sem, tensor.at(("ctx keys", name)))
                        for c in range(CH):
                            act.activation(kTc[:, c].rearrange("p u k -> p (u k)"), pads[2][:, c * P:(c + 1) * P],
                                           ACT.Identity, bias=column(s["bkv"], c)) \
                                .then_inc(scalar.sem, scalar.mark(("ctx keys", name, c)))
                    for u in range(LANES):
                        act.wait_ge(tensor.sem, tensor.at(("turned", name, u)))
                        for c in range(CH):
                            modulate(hT[:, u, c, :], cols(u, CH)[:, c, :], s["ln"], c, u, ("h", name, u, c))
                    if kind in KEYS:
                        for u in range(LANES):
                            act.wait_ge(tensor.sem, tensor.at(("queries", name, u)))
                            for c in range(CH):
                                act.activation(qT[:, u, c, :], cols(2, CH)[:, c, :], ACT.Identity,
                                               bias=column(s.get("bq") or s["bqkv"], c)) \
                                    .then_inc(scalar.sem, scalar.mark(("q", name, u, c)))
                            if kind in SELF:
                                act.wait_ge(tensor.sem, tensor.at(("keys", name, u)))
                                for c in range(CH):
                                    i = act.activation(kT[:, u, c, :], cols(3, CH)[:, c, :], ACT.Identity,
                                                       bias=column(s["bqkv"], CH + c))
                                    i.then_inc(scalar.sem, scalar.mark(("keys", name, u) if c else ("k0", name, u)))
                        N = len(units_of(s))
                        for u in range(LANES):
                            f = first_unit[name, u]

                            def probs_turned(n):
                                act.wait_ge(tensor.sem, tensor.at(("turned probs", n)))
                                if n >= RT:
                                    act.wait_ge(tensor.sem, tensor.at(("values", n - RT)))
                                act.activation(pT[:, n % RT].rearrange("p a b -> p (a b)"), pads[2][:, :], ACT.Copy) \
                                    .then_inc(scalar.sem, scalar.mark(("pT", n)))

                            for j, (t, h0, nh) in enumerate(units_of(s)):
                                n = f + j
                                if kind == "topk":
                                    act.wait_ge(tensor.sem, tensor.at(("scores", n)))
                                    if n >= RP:
                                        act.wait_ge(tensor.sem, tensor.at(("turned probs", n - RP)))
                                    act.activation(pr[:, n % RP, :], pads[n % 2][:, :], ACT.Copy) \
                                        .then_inc(scalar.sem, scalar.mark(("copied", n)))
                                if kind == "full":
                                    act.wait_ge(vector.sem, vector.at(("max", n)))
                                    if n >= RP:
                                        act.wait_ge(tensor.sem, tensor.at(("turned probs", n - RP)))
                                    for e in range(nh):
                                        act.activation(pr[:, n % RP, e * L:(e + 1) * L],
                                                       pads[n % 2][:, e * L:(e + 1) * L], ACT.Exp,
                                                       bias=mx[:, n % RP, e:e + 1], scale=SCALE,
                                                       accum_out=sm[:, n % RP, e:e + 1]) \
                                            .then_inc(scalar.sem, scalar.mark(("exp", n) if e else ("exp0", n)))
                                else:
                                    act.wait_ge(vector.sem, vector.at(("shifted", n)))
                                    act.activation(pr[:, n % RP, :], pr[:, n % RP, :], ACT.Exp, scale=SCALE) \
                                        .then_inc(scalar.sem, scalar.mark(("exp", n)))
                                if j >= 2:
                                    probs_turned(n - 2)
                            probs_turned(f + N - 2)
                            probs_turned(f + N - 1)
                            act.wait_ge(tensor.sem, tensor.at(("values", f + N - 1)))
                            act.activation(oT[:, u].rearrange("p c l -> p (c l)"), pads[3][:, :], ACT.Copy) \
                                .then_inc(scalar.sem, scalar.mark(("o", name, u)))
                    elif kind == "swiglu":
                        for u in range(LANES):
                            for m in range(MC):
                                act.wait_ge(tensor.sem, tensor.at(("up", name, u, m)))
                                k = u * MC + m
                                if k >= 2:
                                    act.wait_ge(vector.sem, vector.at(("hidden", name, (k - 2) // MC, (k - 2) % MC)))
                                act.activation(rk[:, (k % 2) * L:(k % 2 + 1) * L], pads[k % 3][:, 0:L], ACT.Silu,
                                               bias=column(s["b1"], m)) \
                                    .then_inc(scalar.sem, scalar.mark(("silu", name, u, m)))
                    else:
                        for u in range(LANES):
                            for m in range(MC):
                                act.wait_ge(tensor.sem, tensor.at(("up", name, u, m - m % 2)))
                                k = (u * MC + m) // 2
                                act.activation(hid[:, u, m, :], pads[k % 3][:, (m % 2) * L:(m % 2 + 1) * L],
                                               ACT.Gelu_apprx_tanh, bias=column(s["b1"], m)) \
                                    .then_inc(scalar.sem, scalar.mark(("hidden", name, u, m)))
                end_pass(act, "scalar")

        @block.vector
        def _(dve):
            dve.wait_ge(set_tensor.sem, set_tensor.at("bias columns"))
            dve.tensor_copy(bcol[:, 0:nrows], pads[1][:, 0:nrows]).then_inc(set_vector.sem, set_vector.mark("bias columns"))
            dve.wait_ge(set_vector.sem, set_vector.at("bias columns"))
            dve.wait_ge(set_tensor.sem, set_tensor.at(("mod", NMOD - 1)))
            dve.tensor_tensor(modT[:, :, :], pads[2][:, 0:NMOD * CH * B].rearrange("p (m b) -> p m b", b=B),
                              bcol[:, mod_col:mod_col + NMOD * CH].unsqueeze(2).broadcast_to([P, NMOD * CH, B]),
                              ALU.add).then_inc(set_vector.sem, set_vector.mark("modulation"))
            dve.wait_ge(set_vector.sem, set_vector.at("modulation"))
            for v in SCALES:
                i = dve.tensor_scalar(modT[:, v * CH:(v + 1) * CH, :], modT[:, v * CH:(v + 1) * CH, :], 1.0, None,
                                      ALU.add)
            i.then_inc(set_vector.sem, set_vector.mark("1 + scale"))
            dve.wait_ge(set_vector.sem, set_vector.at("1 + scale"))
            dve.wait_ge(set_tensor.sem, set_tensor.at("gates"))
            dve.tensor_copy(grow[:, 0:PAD], pads[0][0:B, :]).then_inc(set_vector.sem, set_vector.mark("gate rows 0"))
            dve.tensor_copy(grow[:, PAD:], pads[1][0:B, 0:len(GATES) * C - PAD]) \
                .then_inc(set_vector.sem, set_vector.mark("gate rows"))

            with dve.Fori(0, PASSES) as it:
                dve.tensor_copy(cur[:, :, :], modT[:, :, bass.ds(it * LANES, LANES)]) \
                    .then_inc(vector.sem, vector.mark("modulation"))
                for si, s in enumerate(SITES):
                    name, kind = s["name"], s["kind"]
                    pl = place[name]

                    def mine(event):
                        dve.wait_ge(vector.sem, vector.at(event))

                    if kind in CROSS:
                        if s["ctx_ln"]:
                            dve.wait_ge(load_ctx.sem, load_ctx.at("context"))
                            dve.bn_stats(cstats[:, 0:6], ctok[:, :]).then_inc(vector.sem, vector.mark(("ctx bn", name)))
                            mine(("ctx bn", name))
                            dve.bn_aggr(cstats[:, 6:8], cstats[:, 0:6]) \
                                .then_inc(vector.sem, vector.mark(("ctx stats", name)))
                            dve.wait_ge(pool.sem, pool.at(("ctx rstd", name)))
                            dve.tensor_scalar(cn[:, :], ctok[:, :], cstats[:, 6:7], cstats[:, 9:10], ALU.subtract,
                                              ALU.mult).then_inc(vector.sem, vector.mark(("ctx normed", name)))
                        dve.wait_ge(load_w[si].sem, load_w[si].at((name, 4)))
                        dve.wait_ge(tensor.sem, tensor.at(("ctx values", name)))
                        for u in range(LANES):
                            for e in range(2):
                                r = slice(e * LC, (e + 1) * LC)
                                src = pads[3][r, u * C:(u + 1) * C].rearrange("p (a e d) -> p a e d", e=2, d=D)
                                bias = pl["vrow"][r, :].rearrange("p (a e d) -> p a e d", e=2, d=D)
                                dve.tensor_tensor(vc[r, u, :, e * D:(e + 1) * D], src[:, :, e, :], bias[:, :, e, :],
                                                  ALU.add) \
                                    .then_inc(vector.sem, vector.mark(("ctx values", name, u, e)))
                    for u in range(LANES):
                        if si == 0:
                            dve.wait_ge(load_x[u].sem, load_x[u].at("start"))
                        else:
                            dve.wait_ge(pool.sem, pool.at(("x", SITES[si - 1]["name"], u)))
                        for t in range(TT):
                            dve.bn_stats(stats[:, u, t, :], x[:, u, t, :]) \
                                .then_inc(vector.sem, vector.mark(("bn", name, u, t)))
                        for t in range(TT):
                            mine(("bn", name, u, t))
                            dve.bn_aggr(mv[:, u, t, :], stats[:, u, t, :]).then_inc(
                                vector.sem, vector.mark(("stats", name, u) if t == TT - 1 else ("aggr", name, u, t)))
                    for u in range(LANES):
                        dve.wait_ge(pool.sem, pool.at(("rstd", name, u)))
                        if u:
                            dve.wait_ge(tensor.sem, tensor.at(("turned", name, u - 1)))
                        for t in range(TT):
                            dve.tensor_scalar(hn[:, t, :], x[:, u, t, :], mv[:, u, t, 0:1], rstd[:, u, t:t + 1],
                                              ALU.subtract, ALU.mult) \
                                .then_inc(vector.sem, vector.mark(("normed", name, u, t)))
                    if kind in SELF:
                        for u in range(LANES):
                            dve.wait_ge(load_w[si].sem, load_w[si].at((name, 3)))
                            dve.wait_ge(tensor.sem, tensor.at(("v", name, u)))
                            for e in range(2):
                                src = pads[u][:, :].rearrange("p (t a e d) -> p t a e d", t=TT, e=2, d=D)
                                bias = pl["vrow"].rearrange("p (a e d) -> p a e d", e=2, d=D)
                                dve.tensor_tensor(vp[:, u, :, :, e, e * D:(e + 1) * D], src[:, :, :, e, :],
                                                  bias[:, :, e, :].unsqueeze(1).broadcast_to([P, TT, H // 2, D]),
                                                  ALU.add) \
                                    .then_inc(vector.sem, vector.mark(("v", name, u, e)))
                    if kind in KEYS:
                        nk = KEYS[kind]
                        nh = PAD // nk
                        for u in range(LANES):
                            f = first_unit[name, u]

                            def row_sums(n):
                                p3 = pr[:, n % RP, :].rearrange("p (h k) -> p h k", k=nk)
                                if kind == "topk":
                                    dve.wait_ge(pool.sem, pool.at(("kept", n)))
                                else:
                                    dve.wait_ge(scalar.sem, scalar.at(("exp", n)))
                                if kind != "full":
                                    dve.tensor_reduce(sm[:, n % RP, 0:nh], p3, AX.X, ALU.add) \
                                        .then_inc(vector.sem, vector.mark(("row sums", n)))
                                    mine(("row sums", n))
                                dve.reciprocal(sm[:, n % RP, 0:nh], sm[:, n % RP, 0:nh]) \
                                    .then_inc(vector.sem, vector.mark(("1/sum", n)))

                            N = len(units_of(s))
                            for j in range(N):
                                n = f + j
                                scores = cols(n % 2, nh)
                                maxima = mx[:, n % RP, 0:nh]
                                p3 = pr[:, n % RP, :].rearrange("p (h k) -> p h k", k=nk)
                                if kind == "topk":
                                    dve.wait_ge(scalar.sem, scalar.at(("copied", n)))
                                    if n > f:
                                        dve.wait_ge(pool.sem, pool.at(("kept", n - 1)))
                                    r3 = rk[:, :].rearrange("p (h k) -> p h k", k=nk)
                                    for step in range(TOPK // 8):
                                        src = r3 if step else p3
                                        for h in range(nh):
                                            i = dve.max(top[:, step, h, :], src[:, h, :])
                                        i.then_inc(vector.sem, vector.mark(("top", n, step)))
                                        mine(("top", n, step))
                                        for h in range(nh):
                                            i = dve.match_replace(out=r3[:, h, :], in_to_replace=top[:, step, h, :],
                                                                  in_values=src[:, h, :], imm_value=LOWEST)
                                        i.then_inc(vector.sem, vector.mark(("replaced", n, step)))
                                        mine(("replaced", n, step))
                                    dve.tensor_tensor(r3, p3, r3, ALU.is_gt) \
                                        .then_inc(vector.sem, vector.mark(("selected", n)))
                                    mine(("selected", n))
                                    dve.tensor_tensor(p3, p3, top[:, 0, :, 0:1].broadcast_to([P, nh, nk]),
                                                      ALU.subtract).then_inc(vector.sem, vector.mark(("shifted", n)))
                                    row_sums(n)
                                    continue
                                dve.wait_ge(tensor.sem, tensor.at(("scores", n)))
                                if n >= RP:
                                    dve.wait_ge(tensor.sem, tensor.at(("turned probs", n - RP)))
                                if kind == "full":
                                    dve.tensor_reduce(maxima, scores, AX.X, ALU.max, negate=True) \
                                        .then_inc(vector.sem, vector.mark(("raw max", n)))
                                    mine(("raw max", n))
                                    dve.tensor_scalar(maxima, maxima, SCALE, None, ALU.mult) \
                                        .then_inc(vector.sem, vector.mark(("max", n)))
                                else:
                                    dve.tensor_reduce(maxima, scores, AX.X, ALU.max) \
                                        .then_inc(vector.sem, vector.mark(("max", n)))
                                    mine(("max", n))
                                    dve.tensor_tensor(p3, scores, maxima.unsqueeze(2).broadcast_to([P, nh, nk]),
                                                      ALU.subtract).then_inc(vector.sem, vector.mark(("shifted", n)))
                                if j >= 1:
                                    row_sums(n - 1)
                            if kind != "topk":
                                row_sums(f + N - 1)
                    if kind == "swiglu":
                        for u in range(LANES):
                            for m in range(MC):
                                k = u * MC + m
                                dve.wait_ge(scalar.sem, scalar.at(("silu", name, u, m)))
                                dve.scalar_tensor_tensor(out=hid[:, u, m, :], in0=pads[k % 3][:, L:2 * L],
                                                         scalar=column(s["b1"], MC + m),
                                                         in1=rk[:, (k % 2) * L:(k % 2 + 1) * L],
                                                         op0=ALU.add, op1=ALU.mult) \
                                    .then_inc(vector.sem, vector.mark(("hidden", name, u, m)))
                    for u in range(LANES):
                        nl = {"win": 4, "full": 4, "topk": 5, "cross": 5, "swiglu": 3, "gelu": 3}[kind]
                        dve.wait_ge(load_w[si].sem, load_w[si].at((name, nl - 1)))
                        dve.wait_ge(tensor.sem, tensor.at(("out", name, u)))
                        if u:
                            dve.wait_ge(pool.sem, pool.at(("x", name, u - 1)))
                        dve.tensor_tensor(tmp[:, :, :], cols(u, TT), pl["orow"].unsqueeze(1).broadcast_to([P, TT, C]),
                                          ALU.add).then_inc(vector.sem, vector.mark(("branch", name, u)))
                end_pass(dve, "vector")

        @block.tensor
        def _(pe):
            mm = pe.matmul
            pe.wait_ge(set_pool.sem, set_pool.at("ident"))
            pe.wait_ge(load_cond.sem, load_cond.at("cond"))
            for c in range(CH):
                i = pe.transpose(pads[0][:, c * B:(c + 1) * B], crow[:, c * P:(c + 1) * P], ident[0:B, 0:B])
            i.then_inc(set_tensor.sem, set_tensor.mark("cond"))
            pe.wait_ge(load_rows.sem, load_rows.at(MODS[-1][1]))
            pe.wait_ge(set_pool.sem, set_pool.at("mask"))
            pe.transpose(pads[1][:, 0:nrows], brow[0:nrows, :], ident[0:nrows, 0:nrows]) \
                .then_inc(set_tensor.sem, set_tensor.mark("bias columns"))
            pe.wait_ge(set_scalar.sem, set_scalar.at("silu"))
            ring = kd[:, :, :, :].rearrange("p c h l -> p (c h l)").rearrange("p (s c n) -> p s c n", s=16, c=CH)
            for vec in range(NMOD):
                ld = load_mod[vec % 16]
                pe.wait_ge(ld.sem, ld.at(vec))
                for m in range(CH):
                    k = vec * CH + m
                    for c in range(CH):
                        i = mm(pads[2][:, k * B:(k + 1) * B], ring[:, vec % 16, c, m * P:(m + 1) * P], condT[:, c, :],
                               start=(c == 0), stop=(c == CH - 1))
                i.then_inc(set_tensor.sem, set_tensor.mark(("mod", vec)))
            pe.wait_ge(set_vector.sem, set_vector.at("1 + scale"))
            for g, vec in enumerate(GATES):
                for c in range(CH):
                    k = g * CH + c
                    pad, o = pads[k // 8], (k % 8) * P
                    i = pe.transpose(pad[0:B, o:o + P], modT[:, vec * CH + c, :], ident[:, :])
            i.then_inc(set_tensor.sem, set_tensor.mark("gates"))
            pe.wait_ge(set_vector.sem, set_vector.at("gate rows"))

            with pe.Fori(0, PASSES) as it:
                holder = [[], [], [], []]

                def claim(pad, *drained_by):
                    for sig, event in holder[pad]:
                        pe.wait_ge(sig.sem, sig.at(event))
                    holder[pad] = list(drained_by)

                for si, s in enumerate(SITES):
                    name, kind = s["name"], s["kind"]
                    pl, lw = place[name], load_w[si]
                    if kind in CROSS:
                        claim(1, (scalar, ("ctx", name, CH - 1, LANES - 1)))
                        if s["ctx_ln"]:
                            pe.wait_ge(vector.sem, vector.at(("ctx normed", name)))
                            src = cn
                        else:
                            pe.wait_ge(load_ctx.sem, load_ctx.at("context"))
                            src = ctok
                        for c in range(CH):
                            i = pe.transpose(pads[1][:, c * P:(c + 1) * P], src[:, c * P:(c + 1) * P], ident[:, :])
                        i.then_inc(tensor.sem, tensor.mark(("ctx turned", name)))
                        claim(2, (scalar, ("ctx keys", name, CH - 1)))
                        claim(3, (vector, ("ctx values", name, LANES - 1, 1)))
                        pe.wait_ge(lw.sem, lw.at((name, 4)))
                        pe.wait_ge(scalar.sem, scalar.at(("ctx", name, CH - 1, LANES - 1)))
                        for m in range(CH):
                            for c in range(CH):
                                i = mm(pads[2][:, m * P:(m + 1) * P].rearrange("p (u k) -> p u k", u=LANES),
                                       pl["kv"][:, c, m * P:(m + 1) * P], cT[:, c, :, 0, :],
                                       start=(c == 0), stop=(c == CH - 1))
                        i.then_inc(tensor.sem, tensor.mark(("ctx keys", name)))
                        for u in range(LANES):
                            for c in range(CH):
                                i = mm(pads[3][:, u * C:(u + 1) * C], cT[:, c, u].rearrange("p e k -> p (e k)"),
                                       pl["kv"][:, c, C:2 * C], start=(c == 0), stop=(c == CH - 1))
                        i.then_inc(tensor.sem, tensor.mark(("ctx values", name)))
                    for u in range(LANES):
                        claim(u, (scalar, ("h", name, u, CH - 1)))
                        for t in range(TT):
                            pe.wait_ge(vector.sem, vector.at(("normed", name, u, t)))
                            for c in range(CH):
                                i = pe.transpose(cols(u, CH)[:, c, t * P:(t + 1) * P], hn[:, t, c * P:(c + 1) * P],
                                                 ident[:, :])
                        i.then_inc(tensor.sem, tensor.mark(("turned", name, u)))
                    if kind in KEYS:
                        nk = KEYS[kind]
                        pe.wait_ge(lw.sem, lw.at((name, 3 if kind in SELF else 4)))
                        for u in range(LANES):
                            pe.wait_ge(scalar.sem, scalar.at(("h", name, u, CH - 1)))
                            wq = pl["qkv"] if kind in SELF else pl["q"]
                            claim(2, (scalar, ("q", name, u, CH - 1)))
                            for m in range(CH):
                                for c in range(CH):
                                    i = mm(cols(2, CH)[:, m, :], wq[:, c, m * P:(m + 1) * P], hT[:, u, c, :],
                                           start=(c == 0), stop=(c == CH - 1))
                            i.then_inc(tensor.sem, tensor.mark(("queries", name, u)))
                            if kind in SELF:
                                claim(3, (scalar, ("keys", name, u)))
                                for m in range(CH):
                                    for c in range(CH):
                                        i = mm(cols(3, CH)[:, m, :], wq[:, c, C + m * P:C + (m + 1) * P],
                                               hT[:, u, c, :], start=(c == 0), stop=(c == CH - 1))
                                i.then_inc(tensor.sem, tensor.mark(("keys", name, u)))
                                claim(u, (vector, ("v", name, u, 1)))
                                for t in range(TT):
                                    for c in range(CH):
                                        i = mm(cols(u, TT)[:, t, :], hT[:, u, c, t * P:(t + 1) * P],
                                               wq[:, c, 2 * C:3 * C], start=(c == 0), stop=(c == CH - 1))
                                i.then_inc(tensor.sem, tensor.mark(("v", name, u)))
                        for u in range(LANES):
                            f, units = first_unit[name, u], units_of(s)
                            N = len(units)

                            def scores(j):
                                n = f + j
                                t, h0, nh = units[j]
                                if kind == "topk":
                                    claim(n % 2, (scalar, ("copied", n)))
                                elif kind == "full":
                                    claim(n % 2, (scalar, ("exp", n)))
                                else:
                                    claim(n % 2, (vector, ("shifted", n)))
                                if j == 0:
                                    pe.wait_ge(scalar.sem, scalar.at(("q", name, u, CH - 1)))
                                    if kind in CROSS:
                                        pe.wait_ge(pool.sem, pool.at(("ctx blocks", name, u, CH - 1)))
                                if kind in SELF and j < H // nh:
                                    hl = h0 + nh - 1
                                    pe.wait_ge(pool.sem, pool.at(("blocks", name, u, hl // HC, hl % HC)))
                                for g in range(2):
                                    o = pads[n % 2][:, g * L:(g + 1) * L]
                                    if kind == "win":
                                        c, h = h0 // HC, h0 % HC + g * (L // nk)
                                        rhs = kd[:, c, h:h + L // nk, t * P:(t + 1) * P]
                                        o = o.rearrange("p (h k) -> p h k", k=nk)
                                    elif kind == "full":
                                        c, h = (h0 + g) // HC, (h0 + g) % HC
                                        rhs = kd[:, c, h, :]
                                    else:
                                        c, rhs = g, kc[:, u, g].rearrange("p h k -> p (h k)")
                                    i = mm(o, qT[:, u, c, t * P:(t + 1) * P], rhs, start=True, stop=True)
                                i.then_inc(tensor.sem, tensor.mark(("scores", n)))

                            def turn(j):
                                n = f + j
                                claim(2, (scalar, ("pT", n)))
                                pe.wait_ge(pool.sem, pool.at(("probs", n)))
                                for k in range(PAD // P):
                                    i = pe.transpose(pads[2][:, k * P:(k + 1) * P],
                                                     pr[:, n % RP, k * P:(k + 1) * P], ident[:, :])
                                i.then_inc(tensor.sem, tensor.mark(("turned probs", n)))

                            def values(j):
                                n = f + j
                                t, h0, nh = units[j]
                                if j == 0:
                                    claim(3, (scalar, ("o", name, u)))
                                    if kind in SELF:
                                        pe.wait_ge(vector.sem, vector.at(("v", name, u, 1)))
                                    else:
                                        pe.wait_ge(vector.sem, vector.at(("ctx values", name, u, 1)))
                                pe.wait_ge(scalar.sem, scalar.at(("pT", n)))
                                for k in range(nh // 2):
                                    a_ = h0 // 2 + k
                                    q = 2 * D * (a_ % (HC // 2))
                                    o = cols(3, CH)[q:q + 2 * D, a_ // (HC // 2), t * P:(t + 1) * P]
                                    if kind in CROSS:
                                        i = mm(o, vc[:, u, a_, :], pT[:, n % RT, k, :], start=True, stop=True)
                                        continue
                                    parts = [(e, kt) for e in range(2) for kt in (range(TT) if kind == "full" else [t])]
                                    for x_, (e, kt) in enumerate(parts):
                                        blk = e * TT + kt if kind == "full" else 2 * k + e
                                        i = mm(o, vp[:, u, kt, a_, e, :], pT[:, n % RT, blk, :],
                                               start=(x_ == 0), stop=(x_ == len(parts) - 1))
                                i.then_inc(tensor.sem, tensor.mark(("values", n)))

                            for j in range(N + 3):
                                if j < N:
                                    scores(j)
                                if 0 <= j - 2 < N:
                                    turn(j - 2)
                                if 0 <= j - 3 < N:
                                    values(j - 3)
                        for u in range(LANES):
                            claim(u, (vector, ("branch", name, u)))
                            pe.wait_ge(scalar.sem, scalar.at(("o", name, u)))
                            for t in range(TT):
                                for c in range(CH):
                                    i = mm(cols(u, TT)[:, t, :], oT[:, u, c, t * P:(t + 1) * P], pl["o"][:, c, :],
                                           start=(c == 0), stop=(c == CH - 1))
                            i.then_inc(tensor.sem, tensor.mark(("out", name, u)))
                    else:
                        pe.wait_ge(lw.sem, lw.at((name, 2)))
                        for u in range(LANES):
                            pe.wait_ge(scalar.sem, scalar.at(("h", name, u, CH - 1)))
                            for m in range(MC):
                                if kind == "swiglu":
                                    k = u * MC + m
                                    claim(k % 3, (vector, ("hidden", name, u, m)))
                                    halves = [(0, m * P), (1, HID + m * P)]
                                else:
                                    if m % 2:
                                        continue
                                    k = (u * MC + m) // 2
                                    claim(k % 3, (scalar, ("hidden", name, u, m + 1)))
                                    halves = [(0, m * P), (1, (m + 1) * P)]
                                for g, col in halves:
                                    for c in range(CH):
                                        i = mm(cols(k % 3, 2)[:, g, :], pl["w1"][:, c, col:col + P], hT[:, u, c, :],
                                               start=(c == 0), stop=(c == CH - 1))
                                i.then_inc(tensor.sem, tensor.mark(("up", name, u, m)))
                        for u in range(LANES):
                            claim(u, (vector, ("branch", name, u)))
                            sig = vector if kind == "swiglu" else scalar
                            pe.wait_ge(sig.sem, sig.at(("hidden", name, u, MC - 1)))
                            for t in range(TT):
                                for m in range(MC):
                                    i = mm(cols(u, TT)[:, t, :], hid[:, u, m, t * P:(t + 1) * P], pl["w2"][:, m, :],
                                           start=(m == 0), stop=(m == MC - 1))
                            i.then_inc(tensor.sem, tensor.mark(("out", name, u)))
                end_pass(pe, "tensor")
    return {name: s.order for name, s in signals.items()}


def kernel(**inputs):
    import numpy as np
    from concourse import bacc
    from concourse.bass_utils import run_bass_kernel_spmd

    arrays = {f"in_{k}": np.ascontiguousarray(v) for k, v in inputs.items()}

    def program(known):
        nc = bacc.Bacc("TRN2", target_bir_lowering=False, num_devices=1)
        a = {k: nc.dram_tensor(f"in_{k}", v.shape, F32, kind="ExternalInput").ap() for k, v in inputs.items()}
        out = nc.dram_tensor("out", (B, L, C), F32, kind="ExternalOutput").ap()
        return nc, build(nc, a, out, known)

    _, events = program({})
    nc, _ = program(events)
    r = run_bass_kernel_spmd(nc, [arrays], core_ids=[0])
    return r.results[0]["out"]
```

```python
from contextlib import ExitStack

import concourse.bass as bass
import concourse.mybir as mybir

F32 = mybir.dt.float32
F32R = mybir.dt.float32r
ALU = mybir.AluOpType
ACT = mybir.ActivationFunctionType
AX = mybir.AxisListType

P = 128
B, L, C = 4, 512, 256
LC = 64
H, D = 16, 16
CH = C // P
TT = L // P
HC = H // CH
HID = 1024
MC = HID // P
LANES = 2
PASSES = B // LANES
SHIFT = 64
TOPK = 16
SCALE = D ** -0.5
PAD = 1024
RP = 4
GROUPS, GH = 4, 4
LEAD = 20
RT = 2
LOWEST = -3.4028234e38

MODS = [("L0_xcond_w_ada", "L0_xcond_b_ada", 9), ("L1_xcond_Wss_q", "L1_xcond_bss_q", 2),
        ("L1_xcond_Wss_kv", "L1_xcond_bss_kv", 2), ("L2_xcond_W_mod", "L2_xcond_b_mod", 6),
        ("L3_xcond_adaln_w", "L3_xcond_adaln_b", 6)]
NMOD = sum(n for _, _, n in MODS)
SCALES = [1, 4, 7, 9, 11, 14, 17, 20, 23]
GATES = [2, 5, 8, 15, 18, 21, 24]

COLS = [("L0_xcond_b_qkv", 4), ("L0_xcond_b_q", 2), ("L0_xcond_b_kv", 2), ("L0_xcond_b_m1", 16),
        ("L1_xcond_bq", 2), ("L1_xcond_bkv", 2), ("L2_xcond_b_qkv", 4), ("L2_xcond_b_qc", 2),
        ("L2_xcond_b_kvc", 2), ("L2_xcond_b_mlp1", 8), ("L3_xcond_qkv_b", 4), ("L3_xcond_q_b", 2),
        ("L3_xcond_kv_b", 2), ("L3_xcond_fc1_b", 8)]

SITES = [
    dict(name="self0", kind="win", layer=0, ln=(1e-6, 1, 0), wqkv="L0_xcond_w_qkv", bqkv="L0_xcond_b_qkv",
         wo="L0_xcond_w_so", bo="L0_xcond_b_so", gate=2),
    dict(name="cross0", kind="topk", layer=0, ln=(1e-6, 4, 3), ctx_ln=None, wq="L0_xcond_w_q", bq="L0_xcond_b_q",
         wkv="L0_xcond_w_kv", bkv="L0_xcond_b_kv", wo="L0_xcond_w_co", bo="L0_xcond_b_co", gate=5),
    dict(name="mlp0", kind="swiglu", layer=0, ln=(1e-6, 7, 6), w1="L0_xcond_w_m1", b1="L0_xcond_b_m1",
         w2="L0_xcond_w_m2", bo="L0_xcond_b_m2", gate=8),
    dict(name="cross1", kind="cross", layer=1, ln=(1e-5, 9, 10), ctx_ln=(1e-5, 11, 12), wq="L1_xcond_Wq",
         bq="L1_xcond_bq", wkv="L1_xcond_Wkv", bkv="L1_xcond_bkv", wo="L1_xcond_Wp", bo="L1_xcond_bp", gate=None),
    dict(name="self2", kind="full", layer=2, ln=(1e-6, 14, 13), wqkv="L2_xcond_W_qkv", bqkv="L2_xcond_b_qkv",
         wo="L2_xcond_W_proj", bo="L2_xcond_b_proj", gate=15),
    dict(name="cross2", kind="cross", layer=2, ln=(1e-6, None, None), ctx_ln=(1e-6, None, None),
         wq="L2_xcond_W_qc", bq="L2_xcond_b_qc", wkv="L2_xcond_W_kvc", bkv="L2_xcond_b_kvc",
         wo="L2_xcond_W_cproj", bo="L2_xcond_b_cproj", gate=None),
    dict(name="mlp2", kind="gelu", layer=2, ln=(1e-6, 17, 16), w1="L2_xcond_W_mlp1", b1="L2_xcond_b_mlp1",
         w2="L2_xcond_W_mlp2", bo="L2_xcond_b_mlp2", gate=18),
    dict(name="self3", kind="full", layer=3, ln=(1e-6, 20, 19), wqkv="L3_xcond_qkv_w", bqkv="L3_xcond_qkv_b",
         wo="L3_xcond_sa_proj_w", bo="L3_xcond_sa_proj_b", gate=21),
    dict(name="cross3", kind="cross", layer=3, ln=(1e-6, None, None), ctx_ln=None, wq="L3_xcond_q_w",
         bq="L3_xcond_q_b", wkv="L3_xcond_kv_w", bkv="L3_xcond_kv_b", wo="L3_xcond_ca_proj_w",
         bo="L3_xcond_ca_proj_b", gate=None),
    dict(name="mlp3", kind="gelu", layer=3, ln=(1e-6, 23, 22), w1="L3_xcond_fc1_w", b1="L3_xcond_fc1_b",
         w2="L3_xcond_fc2_w", bo="L3_xcond_fc2_b", gate=24),
]
SELF, CROSS, MLP = ("win", "full"), ("topk", "cross"), ("swiglu", "gelu")
LOADS = {"win": 4, "full": 4, "topk": 5, "cross": 5, "swiglu": 3, "gelu": 3}
KEYS = {"win": P, "full": L, "topk": LC, "cross": LC}


class Signal:

    def __init__(self, sem, known, step=1):
        self.sem, self.known, self.step = sem, known or {}, step
        self.order = {}

    def mark(self, event):
        assert event not in self.order, event
        self.order[event] = len(self.order) + 1
        return self.step

    def at(self, event):
        return self.step * self.known.get(event, 1)


def full_order():
    order, ahead = [("project", 0, 0)], []
    for x in range(LANES * GROUPS):
        ahead += [("maxima", x, k) for k in range(GH * TT)] + [("turn", x, 0)]

    def more(n):
        while n and ahead:
            n -= ahead[0][0] == "maxima"
            order.append(ahead.pop(0))
        if ahead and ahead[0][0] == "turn":
            order.append(ahead.pop(0))

    more(LEAD)
    steps = [(x, k) for x in range(LANES * GROUPS) for k in range(2 * TT)]
    for i, (x, k) in enumerate(steps):
        order.append(("scores", x, k))
        more(1)
        if i >= 2:
            order.append(("values", *steps[i - 2]))
        more(1)
        if (x, k) == (0, 2 * TT - 1):
            order.append(("project", 1, 0))
        for at, what in (3, "split"), (5, "turn back"), (7, "out"):
            if (x, k) == (GROUPS, at):
                order.append((what, 0, 0))
    return order + [("values", *steps[-2]), ("values", *steps[-1]), ("split", 1, 0), ("turn back", 1, 0), ("out", 1, 0)]


def units_of(site):
    if site["kind"] == "full":
        return []
    nh = PAD // KEYS[site["kind"]]
    return [(t, h0, nh) for t in range(TT) for h0 in range(0, H, nh)]


def build(nc, a, out, known):
    ctx = ExitStack()
    with ctx:
        def sb(name, shape):
            return ctx.enter_context(nc.sbuf_tensor(name, shape, F32))

        x = sb("x", [P, LANES, TT, C])
        ht = sb("ht", [P, 2, TT, C])
        hn = ht
        on = ht
        tmp = ht[:, 1]
        O4 = ht[:, :, :, :].rearrange("p a t c -> p (a t c)").rearrange("p (g l) -> p g l", g=GROUPS)
        hT = sb("hT", [P, LANES, CH, L])
        qT = sb("qT", [P, LANES, CH, L])
        kT = sb("kT", [P, LANES, CH, L])
        start, half_bytes = nc.sbuf_base, GROUPS * GH * L * 4
        arena = sb("arena", [P, 2 * GROUPS * GH * L])

        def in_arena(name, shape, dt, part, skip=0):
            return nc.alloc_sbuf_tensor_at(name, shape, dt, offset=start + part * half_bytes + skip)

        kd = in_arena("kd", [P, LANES, CH, HC, L], F32, 0)
        kc = in_arena("kc", [P, LANES, CH, HC, LC], F32, 0)
        hid = in_arena("hid", [P, LANES, MC, L], F32, 1)
        Qs = in_arena("Qs", [P, GROUPS, CH, 2, L], F32R, 0)
        Ks = in_arena("Ks", [P, GROUPS, CH, 2, L], F32R, 1)
        vp = sb("vp", [P, LANES, TT, H, 2 * D])
        pr = sb("pr", [P, RP, PAD])
        pT = sb("pT", [P, RT, PAD // P, P])
        oT = hT
        rk = in_arena("rk", [P, 2, PAD], F32, 0, half_bytes // 2)
        wA = sb("wA", [P, 2, 8 * C])
        nm = sb("nm", [P, 2, GH * TT])
        nmT = sb("nmT", [GH * TT, 2, 2, P])
        wM = sb("wM", [P, 24 * C])
        rows = sb("rows", [P, 5, C])
        gate = sb("gate", [P, LANES, C])
        ctok = sb("ctok", [P, C])
        cn = in_arena("cn", [P, C], F32, 1)
        cT = in_arena("cT", [P, CH, LANES, 2, LC], F32, 1, C * 4)
        kTc = in_arena("kTc", [P, CH, LANES, LC], F32, 1, 3 * C * 4)
        vc = sb("vc", [P, LANES, H // 2, 2, D + 1])
        ident = sb("ident", [P, P])
        mask = sb("mask", [P, HC])
        bcol = sb("bcol", [P, P])
        modT = sb("modT", [P, NMOD * CH, B])
        cur = sb("cur", [P, NMOD * CH, LANES])
        stats = sb("stats", [P, 2, TT, 6])
        mv = sb("mv", [P, 2, TT, 2])
        rstd = sb("rstd", [P, 2, TT])
        cstats = sb("cstats", [P, 10])
        half = sb("half", [P, TT])
        mx = sb("mx", [P, RP, H])
        rs = sb("rs", [P, 2, H])
        gb = sb("gb", [P, C])
        top = sb("top", [P, 2, 2, H, 8])
        condT = sb("condT", [P, CH, B])
        crow = tmp[0:B, 0, :]
        grow = pT[0:B].rearrange("p r a b -> p (r a b)")[:, 0:len(GATES) * C]
        pads = [ctx.enter_context(nc.psum_tensor(f"pad{i}", [P, PAD], F32)) for i in range(4)]
        brow = hid[:, 0, 0, 0:P]
        nm_dram = nc.dram_tensor("maxima_rows", (2, 2, GH * TT * P), F32, kind="Internal").ap()
        q_dram = nc.dram_tensor("stack_queries", (LANES, H, D, 2, L), F32, kind="Internal").ap()
        k_dram = nc.dram_tensor("stack_keys", (LANES, 2, H, D, 2, L), F32, kind="Internal").ap()
        gates_dram = nc.dram_tensor("gate_rows", (B, len(GATES), C), F32, kind="Internal").ap()

        on4 = pT[:, 0].rearrange("p a b -> p (a b)").rearrange("p (t c) -> p t c", t=TT)
        MR = 96
        signals = {}

        def signal(name, step=1):
            sem = ctx.enter_context(nc.semaphore(name))
            signals[name] = Signal(sem, known.get(name), step)
            return signals[name]

        tensor = signal("tensor_filled")
        scalar = signal("scalar_wrote")
        vector = signal("vector_wrote")
        pool = signal("pool_wrote")
        set_tensor = signal("setup_tensor")
        set_scalar = signal("setup_scalar")
        set_vector = signal("setup_vector")
        set_pool = signal("setup_pool")
        load_cond = signal("cond_loaded", 16)
        load_rows = signal("bias_rows_loaded", 16)
        load_mod = [signal(f"mod_weights_loaded{i}", 16) for i in range(16)]
        gates_out = signal("gates_stored", 16)
        load_x = [signal(f"x_loaded{u}", 16) for u in range(LANES)]
        load_ctx = signal("context_loaded", 16)
        load_w = [signal(f"weights_loaded{i}", 16) for i in range(len(SITES))]
        load_gate = signal("gate_loaded", 16)
        load_stack = [signal(f"stack_loaded{i}", 16) for i in range(GROUPS)]
        load_max = [signal(f"maxima_loaded{i}", 16) for i in range(GROUPS)]
        max_out = signal("maxima_stored", 16)
        stack_out = [signal(f"stack_stored{c}", 16) for c in range(CH)]
        stored = signal("stored", 16)
        in_pass = [tensor, scalar, vector, pool, *load_x, load_ctx, *load_w, load_gate, *load_stack, *load_max,
                   max_out, *stack_out, stored]
        arrived = ctx.enter_context(nc.semaphore("arrived"))
        resume = {e: ctx.enter_context(nc.semaphore(f"resume_{e}")) for e in ("tensor", "scalar", "vector", "pool")}

        def end_pass(eng, name):
            eng.wait_ge(stored.sem, stored.at(("start", LANES - 1)))
            eng.sem_inc(arrived, 1)
            eng.wait_ge(resume[name], 1)
            eng.sem_clear(resume[name])

        place = {}
        attention_sites = [s["name"] for s in SITES if s["kind"] in KEYS]
        for s in SITES:
            n = s["name"]
            par = attention_sites.index(n) % 2 if n in attention_sites else 0
            region, first = wA[:, par], 0
            if s["kind"] in SELF:
                place[n] = dict(qkv=region[:, 0:6 * C].rearrange("p (c n) -> p c n", c=CH),
                                o=region[:, 6 * C:8 * C].rearrange("p (c n) -> p c n", c=CH),
                                vrow=rows[:, 2 * par], orow=rows[:, 2 * par + 1])
            elif s["kind"] in CROSS:
                place[n] = dict(q=region[:, first:first + 2 * C].rearrange("p (c n) -> p c n", c=CH),
                                kv=region[:, first + 2 * C:first + 6 * C].rearrange("p (c n) -> p c n", c=CH),
                                o=region[:, first + 6 * C:first + 8 * C].rearrange("p (c n) -> p c n", c=CH),
                                vrow=rows[:, 2 * par], orow=rows[:, 2 * par + 1])
            else:
                up = 2 * HID if s["kind"] == "swiglu" else HID
                place[n] = dict(w1=wM[:, 0:CH * up].rearrange("p (c n) -> p c n", c=CH),
                                w2=wM[:, 16 * C:24 * C].rearrange("p (m n) -> p m n", m=MC),
                                orow=rows[:, 4])

        col_of, n = {}, 0
        for name, k in COLS:
            col_of[name] = n
            n += k
        mod_col = n
        nrows = mod_col + NMOD * CH
        assert nrows <= P

        def column(name, i):
            return bcol[:, col_of[name] + i:col_of[name] + i + 1]

        def modulation(vec, c, u):
            return cur[:, vec * CH + c, u:u + 1]

        def cols(pad, shape):
            return pads[pad][:, :].rearrange("p (a b) -> p a b", a=shape)

        attn_units = []
        first_unit = {}
        for s in SITES:
            if s["kind"] in KEYS:
                for u in range(LANES):
                    first_unit[s["name"], u] = len(attn_units)
                    attn_units += [(s, u, *x_) for x_ in units_of(s)]

        def last_user_of_weights(site):
            names = [s["name"] for s in SITES]
            same = [s for s in SITES[:names.index(site["name"])] if (s["kind"] in MLP) == (site["kind"] in MLP)]
            back = 1 if site["kind"] in MLP else 2
            return ("out", same[-back]["name"], LANES - 1) if len(same) >= back else None

        def tile_done(site, j):
            units = units_of(site)
            return 0 <= j < len(units) and units[j][1] + units[j][2] == H

        block = ctx.enter_context(nc.Block())

        @block.sync
        def _(sp):
            sp.dma_start(crow, a["cond_1024"]).then_inc(load_cond.sem, load_cond.mark("cond"))
            for name, k in COLS:
                r = col_of[name]
                sp.dma_start(brow[r:r + k, :], a[name][0:k * P].rearrange("(k p) -> k p", p=P)) \
                    .then_inc(load_rows.sem, load_rows.mark(name))
            r = mod_col
            for _, name, k in MODS:
                sp.dma_start(brow[r:r + CH * k, :], a[name].rearrange("(k p) -> k p", p=P)) \
                    .then_inc(load_rows.sem, load_rows.mark(name))
                r += CH * k
            ring = arena[:, 0:16 * CH * C].rearrange("p (s c n) -> p s c n", s=16, c=CH)
            vec = 0
            for w, _, k in MODS:
                for i in range(k):
                    if vec >= 16:
                        sp.wait_ge(set_tensor.sem, set_tensor.at(("mod", vec - 16)))
                    ld = load_mod[vec % 16]
                    sp.dma_start(ring[:, vec % 16], a[w][:, i * C:(i + 1) * C].rearrange("(c p) n -> p c n", p=P)) \
                        .then_inc(ld.sem, ld.mark(vec))
                    vec += 1
            sp.wait_ge(set_vector.sem, set_vector.at("gate rows"))
            sp.dma_start(gates_dram.rearrange("b g n -> b (g n)"), grow) \
                .then_inc(gates_out.sem, gates_out.mark("gates"))
            sp.wait_ge(gates_out.sem, gates_out.at("gates"))

            with sp.Fori(0, PASSES) as it:
                def load_weights(i):
                    s, pl, ld = SITES[i], place[SITES[i]["name"]], load_w[i]
                    before = last_user_of_weights(s)
                    if before:
                        sp.wait_ge(tensor.sem, tensor.at(before))
                        sp.wait_ge(vector.sem, vector.at(("x",) + before[1:]))
                        sp.wait_ge(pool.sem, pool.at(("biased",) + before[1:]))

                    def w(dst, src):
                        sp.dma_start(dst, src).then_inc(ld.sem, ld.mark((s["name"], len(ld.order))))

                    def row(dst, src):
                        w(dst, src.unsqueeze(0).broadcast_to([P, C]))

                    if s["kind"] in SELF:
                        w(pl["qkv"], a[s["wqkv"]].rearrange("(c p) n -> p c n", p=P))
                        row(pl["vrow"], a[s["bqkv"]][2 * C:3 * C])
                    elif s["kind"] in CROSS:
                        w(pl["q"], a[s["wq"]].rearrange("(c p) n -> p c n", p=P))
                        w(pl["kv"], a[s["wkv"]].rearrange("(c p) n -> p c n", p=P))
                        row(pl["vrow"], a[s["bkv"]][C:2 * C])
                    else:
                        w(pl["w1"], a[s["w1"]].rearrange("(c p) n -> p c n", p=P))
                        w(pl["w2"], a[s["w2"]].rearrange("(m p) n -> p m n", p=P))
                    if s["kind"] not in MLP:
                        w(pl["o"], a[s["wo"]].rearrange("(c p) n -> p c n", p=P))
                    row(pl["orow"], a[s["bo"]])

                for u in range(LANES):
                    b = it * LANES + u
                    xb = a["x"][bass.ds(b, 1), :, :].rearrange("o t c -> (o t) c")
                    ld = load_x[u]
                    sp.dma_start(x[:, u, 0:TT - 1, :],
                                 xb[SHIFT:SHIFT + (TT - 1) * P, :].rearrange("(t p) c -> p t c", p=P)) \
                        .then_inc(ld.sem, ld.mark("tiles"))
                    sp.dma_start(x[0:P - SHIFT, u, TT - 1, :], xb[L - SHIFT:L, :]).then_inc(ld.sem, ld.mark("end"))
                    sp.dma_start(x[P - SHIFT:P, u, TT - 1, :], xb[0:SHIFT, :]).then_inc(ld.sem, ld.mark("start"))
                sp.dma_start(ctok[:, :], a["ctx_1024"][bass.ds(it * LANES, LANES), :, :].rearrange("u t c -> (u t) c")) \
                    .then_inc(load_ctx.sem, load_ctx.mark("context"))
                loaded = set()
                for i, s in enumerate(SITES):
                    if last_user_of_weights(s) is None:
                        load_weights(i)
                        loaded.add(i)
                gated = [s for s in SITES if s["gate"] is not None]
                for i, s in enumerate(SITES):
                    if s["gate"] is not None:
                        g = gated.index(s)
                        if g >= 1:
                            sp.wait_ge(pool.sem, pool.at(("biased", gated[g - 1]["name"], LANES - 1)))
                            sp.wait_ge(vector.sem, vector.at(("x", gated[g - 1]["name"], LANES - 1)))
                        gi = GATES.index(s["gate"])
                        sp.dma_start(gate[:, :, :],
                                     gates_dram[bass.ds(it * LANES, LANES), gi, :].unsqueeze(0)
                                     .broadcast_to([P, LANES, C])) \
                            .then_inc(load_gate.sem, load_gate.mark(s["name"]))
                    if s["kind"] == "full":
                        name = s["name"]

                        def store_heads(u, c):
                            for w, src in (("q", qT), ("k", kT)):
                                sp.wait_ge(scalar.sem, scalar.at(("high", name, u, w, c)))
                                sp.wait_ge(vector.sem, vector.at(("low", name, u, w, c)))
                                for low in range(2):
                                    for part in range(2 if w == "k" else 1):
                                        hs = slice(c * HC, (c + 1) * HC)
                                        dst = k_dram[u, part, hs, :, low ^ part, :] if w == "k" else \
                                            q_dram[u, hs, :, low, :]
                                        sp.dma_start(dst.rearrange("h d l -> (h d) l"), src[:, low, c, :]) \
                                            .then_inc(stack_out[c].sem, stack_out[c].mark((name, u, w, low, part)))

                        def load_stacks(x_):
                            u, g = x_ // GROUPS, x_ % GROUPS
                            if x_ >= GROUPS:
                                sp.wait_ge(tensor.sem, tensor.at(("scores", name, x_ - GROUPS, 2 * TT - 1)))
                            so = stack_out[g // (GROUPS // CH)]
                            sp.wait_ge(so.sem, so.at((name, u, "k", 1, 1)))
                            ld, hs = load_stack[g], slice(GH * g, GH * (g + 1))
                            for part in range(2):
                                rows_ = slice(2 * D * part, 2 * D * (part + 1))
                                sp.dma_start(Qs[rows_, g].rearrange("p c e l -> p (c e) l").bitcast(F32),
                                             q_dram[u, hs].rearrange("h d s l -> (d s) h l")) \
                                    .then_inc(ld.sem, ld.mark((name, x_, "q", part)))
                                sp.dma_start(Ks[rows_, g].rearrange("p c e l -> p (c e) l").bitcast(F32),
                                             k_dram[u, part, hs].rearrange("h d s l -> (d s) h l")) \
                                    .then_inc(ld.sem, ld.mark((name, x_, "k", part)))

                        for what, x_, k in full_order():
                            g = x_ % GROUPS
                            if what == "project":
                                for c in range(CH):
                                    store_heads(x_, c)
                                    if x_ == 0 and c == 0:
                                        load_stacks(0)
                                        load_stacks(1)
                                if x_ == 1:
                                    load_stacks(GROUPS)
                            if what == "turn":
                                sp.wait_ge(vector.sem, vector.at(("max low", name, x_)))
                                if x_ >= 2:
                                    sp.wait_ge(load_max[(x_ - 2) % GROUPS].sem,
                                               load_max[(x_ - 2) % GROUPS].at((name, x_ - 2)))
                                sp.dma_start(nm_dram[x_ % 2].rearrange("s (r q) -> r s q", q=P), nmT[:, x_ % 2]) \
                                    .then_inc(max_out.sem, max_out.mark((name, x_)))
                                sp.wait_ge(max_out.sem, max_out.at((name, x_)))
                                if x_ >= GROUPS:
                                    sp.wait_ge(tensor.sem, tensor.at(("scores", name, x_ - GROUPS, 2 * TT - 1)))
                                if x_ == 0:
                                    sp.wait_ge(pool.sem, pool.at(("cleared", name)))
                                sp.dma_start(Qs[MR:MR + 2, g].rearrange("p c e l -> p (c e l)").bitcast(F32),
                                             nm_dram[x_ % 2]) \
                                    .then_inc(load_max[g].sem, load_max[g].mark((name, x_)))
                                if x_ + 2 < GROUPS:
                                    load_stacks(x_ + 2)
                            if what == "scores" and k == 2 * TT - 1 and 1 <= x_ < GROUPS:
                                load_stacks(x_ + GROUPS)
                    for j in range(i + 1, len(SITES)):
                        before = last_user_of_weights(SITES[j])
                        if j not in loaded and before and before[1] == s["name"]:
                            load_weights(j)
                            loaded.add(j)
                assert len(loaded) == len(SITES)
                for u in range(LANES):
                    last = SITES[-1]["name"]
                    sp.wait_ge(vector.sem, vector.at(("x", last, u)))
                    ob = out[bass.ds(it * LANES + u, 1), :, :].rearrange("o t c -> (o t) c")
                    sp.dma_start(ob[SHIFT:SHIFT + (TT - 1) * P, :].rearrange("(t p) c -> p t c", p=P),
                                 x[:, u, 0:TT - 1, :]).then_inc(stored.sem, stored.mark(("tiles", u)))
                    sp.dma_start(ob[L - SHIFT:L, :], x[0:P - SHIFT, u, TT - 1, :]) \
                        .then_inc(stored.sem, stored.mark(("end", u)))
                    sp.dma_start(ob[0:SHIFT, :], x[P - SHIFT:P, u, TT - 1, :]) \
                        .then_inc(stored.sem, stored.mark(("start", u)))
                sp.wait_ge(stored.sem, stored.at(("start", LANES - 1)))
                sp.wait_ge(arrived, len(resume))
                for sig in in_pass:
                    sp.sem_clear(sig.sem)
                sp.sem_clear(arrived)
                for sem in resume.values():
                    sp.sem_inc(sem, 1)

        @block.gpsimd
        def _(gp):
            gp.memset(ident[:, :], 0.0).then_inc(set_pool.sem, set_pool.mark("ident 0"))
            gp.memset(mask[:, :], 1.0).then_inc(set_pool.sem, set_pool.mark("mask 1"))
            gp.memset(vc[:, :, :, :], 0.0).then_inc(set_pool.sem, set_pool.mark("vc"))
            gp.memset(vp[:, :, :, :, D:2 * D], 1.0).then_inc(set_pool.sem, set_pool.mark("ones"))
            gp.memset(half[:, :], -0.5).then_inc(set_pool.sem, set_pool.mark("half"))
            gp.wait_ge(set_pool.sem, set_pool.at("half"))
            for e in range(2):
                gp.memset(vc[e * LC:(e + 1) * LC, :, :, e, D:D + 1], 1.0) \
                    .then_inc(set_pool.sem, set_pool.mark(("context ones", e)))
                gp.wait_ge(set_pool.sem, set_pool.at(("context ones", e)))
            gp.affine_select(out=ident[:, :], in_=ident[:, :], compare_op=ALU.not_equal, fill=1.0, base=0,
                             pattern=[[-1, P]], channel_multiplier=1) \
                .then_inc(set_pool.sem, set_pool.mark("ident"))
            gp.affine_select(out=mask[:, :], in_=mask[:, :], compare_op=ALU.is_ge, fill=0.0, base=0,
                             pattern=[[-D, HC]], channel_multiplier=1) \
                .then_inc(set_pool.sem, set_pool.mark("mask low"))
            gp.wait_ge(set_pool.sem, set_pool.at("mask low"))
            gp.affine_select(out=mask[:, :], in_=mask[:, :], compare_op=ALU.is_ge, fill=0.0, base=D - 1,
                             pattern=[[D, HC]], channel_multiplier=-1) \
                .then_inc(set_pool.sem, set_pool.mark("mask"))
            gp.wait_ge(set_pool.sem, set_pool.at("mask"))
            gp.wait_ge(set_tensor.sem, set_tensor.at("gates"))

            def bias(s, u):
                name = s["name"]
                row = place[name]["orow"]
                gp.wait_ge(load_w[SITES.index(s)].sem, load_w[SITES.index(s)].at((name, LOADS[s["kind"]] - 1)))
                gp.wait_ge(vector.sem, vector.at(("normed", name, u, TT - 1)))
                if s["gate"] is not None:
                    gp.wait_ge(load_gate.sem, load_gate.at(name))
                    gp.tensor_tensor(gb[:, :], row, gate[:, u, :], ALU.mult) \
                        .then_inc(pool.sem, pool.mark(("gated bias", name, u)))
                    gp.wait_ge(pool.sem, pool.at(("gated bias", name, u)))
                    row = gb[:, :]
                gp.tensor_tensor(x[:, u], x[:, u], row.unsqueeze(1).broadcast_to([P, TT, C]), ALU.add) \
                    .then_inc(pool.sem, pool.mark(("biased", name, u)))
                gp.wait_ge(pool.sem, pool.at(("biased", name, u)))

            with gp.Fori(0, PASSES) as it:
                for s in SITES:
                    name, kind = s["name"], s["kind"]
                    for u in range(LANES):
                        gp.wait_ge(vector.sem, vector.at(("stats", name, u)))
                        gp.tensor_scalar(rstd[:, u, :], mv[:, u, :, 1], s["ln"][0], None, ALU.add) \
                            .then_inc(pool.sem, pool.mark(("var", name, u)))
                        gp.wait_ge(pool.sem, pool.at(("var", name, u)))
                        gp.tensor_tensor(rstd[:, u, :], rstd[:, u, :], half[:, :], ALU.pow) \
                            .then_inc(pool.sem, pool.mark(("rstd", name, u)))
                    if kind in CROSS:
                        if s["ctx_ln"]:
                            gp.wait_ge(vector.sem, vector.at(("ctx stats", name)))
                            gp.tensor_scalar(cstats[:, 8:9], cstats[:, 7:8], s["ctx_ln"][0], None, ALU.add) \
                                .then_inc(pool.sem, pool.mark(("ctx var", name)))
                            gp.wait_ge(pool.sem, pool.at(("ctx var", name)))
                            gp.tensor_tensor(cstats[:, 9:10], cstats[:, 8:9], half[:, 0:1], ALU.pow) \
                                .then_inc(pool.sem, pool.mark(("ctx rstd", name)))
                        gp.wait_ge(scalar.sem, scalar.at(("ctx keys", name, CH - 1)))
                        for c in range(CH):
                            gp.tensor_tensor(kc[:, 1, c], kTc[:, c, 1, :].unsqueeze(1).broadcast_to([P, HC, LC]),
                                             mask[:, :].unsqueeze(2).broadcast_to([P, HC, LC]), ALU.mult) \
                                .then_inc(pool.sem, pool.mark(("ctx blocks", name, 1, c)))
                    if kind == "full":
                        gp.wait_ge(pool.sem, pool.at(("rstd", name, LANES - 1)))
                        for i, (t_, lo, hi, v) in enumerate([(Ks, MR, P, 0.0), (Ks, 4 * D, MR, 0.0), (Qs, 4 * D, P, 0.0),
                                                             (Ks, MR, MR + 2, 1.0)]):
                            event = ("cleared", name) if v else ("cleared", name, i)
                            gp.memset(t_[lo:hi].rearrange("p g c e l -> p (g c e l)").bitcast(F32), v) \
                                .then_inc(pool.sem, pool.mark(event))
                            gp.wait_ge(pool.sem, pool.at(event))
                        for u in range(LANES):
                            bias(s, u)
                        continue
                    if kind == "win":
                        gp.wait_ge(scalar.sem, scalar.at(("keys", name, 1)))
                        for c in range(CH):
                            for h in range(HC):
                                gp.tensor_scalar(kd[:, 1, c, h, :], kT[:, 1, c, :], mask[:, h:h + 1], None,
                                                 ALU.mult).then_inc(pool.sem, pool.mark(("blocks", name, 1, c, h)))
                    for u in range(LANES):
                        bias(s, u)
                    if kind == "topk":
                        for n in range(first_unit[name, 0], first_unit[name, 0] + LANES * len(units_of(s))):
                            p3 = pr[:, n % RP, :].rearrange("p (h k) -> p h k", k=LC)
                            gp.wait_ge(vector.sem, vector.at(("selected", n)))
                            gp.tensor_tensor(p3, p3, top[:, n % 2, 0, :, 0:1].broadcast_to([P, H, LC]), ALU.subtract) \
                                .then_inc(pool.sem, pool.mark(("shifted", n)))
                            gp.wait_ge(scalar.sem, scalar.at(("exp", n)))
                            gp.tensor_tensor(pr[:, n % RP, :], pr[:, n % RP, :], rk[:, n % 2, :], ALU.mult) \
                                .then_inc(pool.sem, pool.mark(("kept", n)))
                end_pass(gp, "pool")

        @block.scalar
        def _(act):
            act.wait_ge(set_tensor.sem, set_tensor.at("cond"))
            act.activation(condT[:, :, :].rearrange("p c b -> p (c b)"), pads[0][:, 0:CH * B], ACT.Silu) \
                .then_inc(set_scalar.sem, set_scalar.mark("silu"))

            with act.Fori(0, PASSES) as it:
                def modulate(dst, src, vecs, c, u, event):
                    if vecs[1] is None:
                        i = act.activation(dst, src, ACT.Copy)
                    else:
                        i = act.activation(dst, src, ACT.Identity, bias=modulation(vecs[2], c, u),
                                           scale=modulation(vecs[1], c, u))
                    i.then_inc(scalar.sem, scalar.mark(event))

                act.wait_ge(vector.sem, vector.at("modulation"))
                for s in SITES:
                    name, kind = s["name"], s["kind"]
                    for u in range(LANES):
                        act.wait_ge(tensor.sem, tensor.at(("turned", name, u)))
                        for c in range(CH):
                            modulate(hT[:, u, c, :], cols(u, CH)[:, c, :], s["ln"], c, u, ("h", name, u, c))
                    if kind in CROSS:
                        act.wait_ge(tensor.sem, tensor.at(("ctx turned", name)))
                        lnv = s["ctx_ln"] or (0, None, None)
                        for c in range(CH):
                            for u in range(LANES):
                                src = pads[3][:, c * P + u * LC:c * P + (u + 1) * LC]
                                modulate(cT[:, c, u], src.unsqueeze(1).broadcast_to([P, 2, LC]), lnv, c, u,
                                         ("ctx", name, c, u))
                    if kind == "full":
                        for what, x_, k in full_order():
                            if what == "project":
                                for w, dst, pad in (("q", qT, 1), ("k", kT, 2)):
                                    act.wait_ge(tensor.sem, tensor.at((w, name, x_)))
                                    if x_ and w == "q":
                                        for so in stack_out:
                                            act.wait_ge(so.sem, so.at((name, x_ - 1, "k", 1, 1)))
                                    for c in range(CH):
                                        act.activation(dst[:, 0, c, :].bitcast(F32R), cols(pad, CH)[:, c, :],
                                                       ACT.Identity,
                                                       bias=column(s["bqkv"], c + (CH if w == "k" else 0))) \
                                            .then_inc(scalar.sem, scalar.mark(("high", name, x_, w, c)))
                            if what == "scores":
                                n = x_ * 2 * TT + k
                                act.wait_ge(tensor.sem, tensor.at(("scores", name, x_, k)))
                                if n >= RP:
                                    m = n - RP
                                    act.wait_ge(tensor.sem, tensor.at(("values", name, m // (2 * TT), m % (2 * TT))))
                                act.activation(pr[:, n % RP, :], pads[1 + k % 2][:, :], ACT.Exp, scale=SCALE) \
                                    .then_inc(scalar.sem, scalar.mark(("probs", name, x_, k)))
                            if what == "values" and k == 2 * TT - 1:
                                act.wait_ge(tensor.sem, tensor.at(("values", name, x_, k)))
                                if x_ == GROUPS:
                                    act.wait_ge(tensor.sem, tensor.at(("split", name, 0)))
                                if x_ == GROUPS + 2:
                                    act.wait_ge(vector.sem, vector.at(("x", name, 0)))
                                act.activation(O4[:, x_ % GROUPS, :], pads[3][:, (x_ % 2) * L:(x_ % 2 + 1) * L],
                                               ACT.Copy).then_inc(scalar.sem, scalar.mark(("o", name, x_)))
                            if what == "turn back":
                                act.wait_ge(tensor.sem, tensor.at(("turned back", name, x_)))
                                act.activation(oT[:, x_].rearrange("p c l -> p (c l)"), pads[1][:, :], ACT.Copy) \
                                    .then_inc(scalar.sem, scalar.mark(("oT", name, x_)))
                        continue
                    if kind in KEYS:
                        for u in range(LANES):
                            act.wait_ge(tensor.sem, tensor.at(("queries", name, u)))
                            for c in range(CH):
                                act.activation(qT[:, u, c, :], cols(2 - u, CH)[:, c, :], ACT.Identity,
                                               bias=column(s.get("bq") or s["bqkv"], c)) \
                                    .then_inc(scalar.sem, scalar.mark(("q", name, u, c)))
                            if kind in SELF:
                                act.wait_ge(tensor.sem, tensor.at(("keys", name, u)))
                                for c in range(CH):
                                    i = act.activation(kT[:, u, c, :], cols(3, CH)[:, c, :], ACT.Identity,
                                                       bias=column(s["bqkv"], CH + c))
                                    i.then_inc(scalar.sem, scalar.mark(("keys", name, u) if c else ("k0", name, u)))
                        if kind in CROSS:
                            act.wait_ge(tensor.sem, tensor.at(("ctx keys", name)))
                            for c in range(CH):
                                act.activation(kTc[:, c].rearrange("p u k -> p (u k)"), pads[0][:, c * P:(c + 1) * P],
                                               ACT.Identity, bias=column(s["bkv"], c)) \
                                    .then_inc(scalar.sem, scalar.mark(("ctx keys", name, c)))
                        N = len(units_of(s))
                        for u in range(LANES):
                            f = first_unit[name, u]

                            def copied(n):
                                act.wait_ge(tensor.sem, tensor.at(("scores", n)))
                                if n >= RP:
                                    act.wait_ge(tensor.sem, tensor.at(("turned probs", n - RP)))
                                act.activation(pr[:, n % RP, :], pads[n % 2][:, :], ACT.Copy) \
                                    .then_inc(scalar.sem, scalar.mark(("copied", n)))

                            for j in range(N + 4):
                                n = f + j
                                if j < N and kind == "topk":
                                    if j == 0:
                                        copied(n)
                                    if j + 1 < N:
                                        copied(n + 1)
                                if j < N:
                                    sig = pool if kind == "topk" else vector
                                    act.wait_ge(sig.sem, sig.at(("shifted", n)))
                                    act.activation(pr[:, n % RP, :], pr[:, n % RP, :], ACT.Exp, scale=SCALE) \
                                        .then_inc(scalar.sem, scalar.mark(("exp", n)))
                                if 0 <= j - 2 < N:
                                    n = f + j - 2
                                    act.wait_ge(tensor.sem, tensor.at(("turned probs", n)))
                                    if n >= RT:
                                        act.wait_ge(tensor.sem, tensor.at(("values", n - RT)))
                                    act.activation(pT[:, n % RT].rearrange("p a b -> p (a b)"), pads[2][:, :],
                                                   ACT.Copy).then_inc(scalar.sem, scalar.mark(("pT", n)))
                                if tile_done(s, j - 4):
                                    t = units_of(s)[j - 4][0]
                                    act.wait_ge(tensor.sem, tensor.at(("o turned", name, u, t)))
                                    src = pads[3][:, (t % 2) * L:(t % 2) * L + C].rearrange("p (c q) -> p c q", c=CH)
                                    act.activation(oT[:, u, :, t * P:(t + 1) * P], src, ACT.Copy) \
                                        .then_inc(scalar.sem, scalar.mark(("o", name, u, t)))
                    elif kind == "swiglu":
                        for u in range(LANES):
                            for m in range(MC):
                                act.wait_ge(tensor.sem, tensor.at(("up", name, u, m)))
                                k = u * MC + m
                                if k >= 2:
                                    act.wait_ge(vector.sem, vector.at(("hidden", name, (k - 2) // MC, (k - 2) % MC)))
                                act.activation(rk[:, 0, (k % 2) * L:(k % 2 + 1) * L], pads[k % 3][:, 0:L], ACT.Silu,
                                               bias=column(s["b1"], m)) \
                                    .then_inc(scalar.sem, scalar.mark(("silu", name, u, m)))
                    else:
                        for u in range(LANES):
                            for m in range(MC):
                                act.wait_ge(tensor.sem, tensor.at(("up", name, u, m - m % 2)))
                                k = (u * MC + m) // 2
                                act.activation(hid[:, u, m, :], pads[k % 3][:, (m % 2) * L:(m % 2 + 1) * L],
                                               ACT.Gelu_apprx_tanh, bias=column(s["b1"], m)) \
                                    .then_inc(scalar.sem, scalar.mark(("hidden", name, u, m)))
                end_pass(act, "scalar")

        @block.vector
        def _(dve):
            dve.wait_ge(set_tensor.sem, set_tensor.at("bias columns"))
            dve.tensor_copy(bcol[:, 0:nrows], pads[1][:, 0:nrows]).then_inc(set_vector.sem, set_vector.mark("bias columns"))
            dve.wait_ge(set_vector.sem, set_vector.at("bias columns"))
            dve.wait_ge(set_tensor.sem, set_tensor.at(("mod", NMOD - 1)))
            dve.tensor_tensor(modT[:, :, :], pads[2][:, 0:NMOD * CH * B].rearrange("p (m b) -> p m b", b=B),
                              bcol[:, mod_col:mod_col + NMOD * CH].unsqueeze(2).broadcast_to([P, NMOD * CH, B]),
                              ALU.add).then_inc(set_vector.sem, set_vector.mark("modulation"))
            dve.wait_ge(set_vector.sem, set_vector.at("modulation"))
            for v in SCALES:
                i = dve.tensor_scalar(modT[:, v * CH:(v + 1) * CH, :], modT[:, v * CH:(v + 1) * CH, :], 1.0, None,
                                      ALU.add)
            i.then_inc(set_vector.sem, set_vector.mark("1 + scale"))
            dve.wait_ge(set_vector.sem, set_vector.at("1 + scale"))
            dve.wait_ge(set_tensor.sem, set_tensor.at("gates"))
            dve.tensor_copy(grow[:, 0:PAD], pads[0][0:B, :]).then_inc(set_vector.sem, set_vector.mark("gate rows 0"))
            dve.tensor_copy(grow[:, PAD:], pads[1][0:B, 0:len(GATES) * C - PAD]) \
                .then_inc(set_vector.sem, set_vector.mark("gate rows"))

            with dve.Fori(0, PASSES) as it:
                dve.tensor_copy(cur[:, :, :], modT[:, :, bass.ds(it * LANES, LANES)]) \
                    .then_inc(vector.sem, vector.mark("modulation"))
                for si, s in enumerate(SITES):
                    name, kind = s["name"], s["kind"]
                    pl = place[name]

                    def mine(event):
                        dve.wait_ge(vector.sem, vector.at(event))

                    def branch(u, pad):
                        dve.wait_ge(pool.sem, pool.at(("biased", name, u)))
                        dve.wait_ge(tensor.sem, tensor.at(("out", name, u)))
                        out_ = cols(pad, TT)
                        if s["gate"] is not None:
                            dve.wait_ge(load_gate.sem, load_gate.at(name))
                            if u:
                                mine(("x", name, u - 1))
                            dve.tensor_tensor(tmp, out_, gate[:, u, :].unsqueeze(1).broadcast_to([P, TT, C]),
                                              ALU.mult).then_inc(vector.sem, vector.mark(("branch", name, u)))
                            mine(("branch", name, u))
                            out_ = tmp
                        dve.tensor_tensor(x[:, u], x[:, u], out_, ALU.add) \
                            .then_inc(vector.sem, vector.mark(("x", name, u)))

                    for u in range(LANES):
                        if si == 0:
                            dve.wait_ge(load_x[u].sem, load_x[u].at("start"))
                        else:
                            mine(("x", SITES[si - 1]["name"], u))
                        for t in range(TT):
                            dve.bn_stats(stats[:, u, t, :], x[:, u, t, :]) \
                                .then_inc(vector.sem, vector.mark(("bn", name, u, t)))
                        for t in range(TT):
                            mine(("bn", name, u, t))
                            dve.bn_aggr(mv[:, u, t, :], stats[:, u, t, :]).then_inc(
                                vector.sem, vector.mark(("stats", name, u) if t == TT - 1 else ("aggr", name, u, t)))
                    if kind in CROSS and s["ctx_ln"]:
                        dve.wait_ge(load_ctx.sem, load_ctx.at("context"))
                        dve.bn_stats(cstats[:, 0:6], ctok[:, :]).then_inc(vector.sem, vector.mark(("ctx bn", name)))
                        mine(("ctx bn", name))
                        dve.bn_aggr(cstats[:, 6:8], cstats[:, 0:6]) \
                            .then_inc(vector.sem, vector.mark(("ctx stats", name)))
                    for u in range(LANES):
                        dve.wait_ge(pool.sem, pool.at(("rstd", name, u)))
                        for t in range(TT):
                            dve.tensor_scalar(hn[:, u, t, :], x[:, u, t, :], mv[:, u, t, 0:1], rstd[:, u, t:t + 1],
                                              ALU.subtract, ALU.mult) \
                                .then_inc(vector.sem, vector.mark(("normed", name, u, t)))
                    if kind in CROSS:
                        if s["ctx_ln"]:
                            dve.wait_ge(pool.sem, pool.at(("ctx rstd", name)))
                            dve.tensor_scalar(cn[:, :], ctok[:, :], cstats[:, 6:7], cstats[:, 9:10], ALU.subtract,
                                              ALU.mult).then_inc(vector.sem, vector.mark(("ctx normed", name)))
                        dve.wait_ge(set_pool.sem, set_pool.at("mask"))
                        dve.wait_ge(scalar.sem, scalar.at(("ctx keys", name, CH - 1)))
                        for c in range(CH):
                            dve.tensor_tensor(kc[:, 0, c], kTc[:, c, 0, :].unsqueeze(1).broadcast_to([P, HC, LC]),
                                              mask[:, :].unsqueeze(2).broadcast_to([P, HC, LC]), ALU.mult) \
                                .then_inc(vector.sem, vector.mark(("ctx blocks", name, 0, c)))
                        dve.wait_ge(set_pool.sem, set_pool.at("vc"))
                        dve.wait_ge(load_w[si].sem, load_w[si].at((name, 4)))
                        dve.wait_ge(tensor.sem, tensor.at(("ctx values", name)))
                        for u in range(LANES):
                            for e in range(2):
                                r = slice(e * LC, (e + 1) * LC)
                                src = pads[3][r, u * C:(u + 1) * C].rearrange("p (a e d) -> p a e d", e=2, d=D)
                                bias = pl["vrow"][r, :].rearrange("p (a e d) -> p a e d", e=2, d=D)
                                dve.tensor_tensor(vc[r, u, :, e, 0:D], src[:, :, e, :], bias[:, :, e, :],
                                                  ALU.add) \
                                    .then_inc(vector.sem, vector.mark(("ctx values", name, u, e)))
                    if kind == "full":
                        for what, x_, k in full_order():
                            if what == "project":
                                u = x_
                                for w, src, pad in (("q", qT, 1), ("k", kT, 2)):
                                    for c in range(CH):
                                        dve.wait_ge(scalar.sem, scalar.at(("high", name, u, w, c)))
                                        dve.scalar_tensor_tensor(
                                            out=src[:, 1, c, :].bitcast(F32R), in0=cols(pad, CH)[:, c, :],
                                            scalar=column(s["bqkv"], c + (CH if w == "k" else 0)),
                                            in1=src[:, 0, c, :], op0=ALU.add, op1=ALU.subtract) \
                                            .then_inc(vector.sem, vector.mark(("low", name, u, w, c)))
                                dve.wait_ge(load_w[si].sem, load_w[si].at((name, 1)))
                                dve.wait_ge(tensor.sem, tensor.at(("v", name, u)))
                                dve.tensor_tensor(
                                    vp[:, u, :, :, 0:D],
                                    pads[1][:, :].rearrange("p (t h d) -> p t h d", t=TT, d=D),
                                    pl["vrow"].rearrange("p (h d) -> p h d", d=D).unsqueeze(1)
                                    .broadcast_to([P, TT, H, D]), ALU.add) \
                                    .then_inc(vector.sem, vector.mark(("v", name, u)))
                            if what == "maxima":
                                dve.wait_ge(tensor.sem, tensor.at(("maxima", name, x_, k)))
                                if k == 0 and x_ >= 2:
                                    dve.wait_ge(tensor.sem, tensor.at(("turn", name, x_ - 2)))
                                b_ = (x_ * (GH * TT + 1) + k) % 2
                                dve.tensor_reduce(nm[:, x_ % 2, k:k + 1], pads[0][:, b_ * L:(b_ + 1) * L], AX.X,
                                                  ALU.max, negate=True) \
                                    .then_inc(vector.sem, vector.mark(("maxima", name, x_, k)))
                            if what == "turn":
                                dve.wait_ge(tensor.sem, tensor.at(("turn", name, x_)))
                                if x_ >= 2:
                                    dve.wait_ge(max_out.sem, max_out.at((name, x_ - 2)))
                                b_ = (x_ * (GH * TT + 1) + GH * TT) % 2
                                src = pads[0][0:GH * TT, b_ * L:b_ * L + P]
                                dve.tensor_copy(nmT[:, x_ % 2, 0].bitcast(F32R), src) \
                                    .then_inc(vector.sem, vector.mark(("max high", name, x_)))
                                mine(("max high", name, x_))
                                dve.tensor_tensor(nmT[:, x_ % 2, 1].bitcast(F32R), src, nmT[:, x_ % 2, 0],
                                                  ALU.subtract) \
                                    .then_inc(vector.sem, vector.mark(("max low", name, x_)))
                            if what == "split":
                                for t in range(TT):
                                    o = pads[1 + t // 2][:, (t % 2) * L:(t % 2 + 1) * L] \
                                        .rearrange("p (h d) -> p h d", d=2 * D)
                                    dve.wait_ge(tensor.sem, tensor.at(("split", name, x_)))
                                    dve.reciprocal(rs[:, t % 2, :].unsqueeze(2), o[:, :, D:D + 1]) \
                                        .then_inc(vector.sem, vector.mark(("1/sums", name, x_, t)))
                                    mine(("1/sums", name, x_, t))
                                    dve.tensor_tensor(on4[:, t, :].rearrange("p (h d) -> p h d", d=D), o[:, :, 0:D],
                                                      rs[:, t % 2, :].unsqueeze(2).broadcast_to([P, H, D]),
                                                      ALU.mult).then_inc(vector.sem, vector.mark(("o", name, x_, t)))
                            if what == "out":
                                branch(x_, 2)
                        continue
                    if kind == "win":
                        dve.wait_ge(set_pool.sem, set_pool.at("mask"))
                        dve.wait_ge(scalar.sem, scalar.at(("keys", name, 0)))
                        for c in range(CH):
                            for h in range(HC):
                                dve.tensor_scalar(kd[:, 0, c, h, :], kT[:, 0, c, :], mask[:, h:h + 1], None,
                                                  ALU.mult).then_inc(vector.sem, vector.mark(("blocks", name, 0, c, h)))
                        for u in range(LANES):
                            dve.wait_ge(load_w[si].sem, load_w[si].at((name, 3)))
                            dve.wait_ge(tensor.sem, tensor.at(("v", name, u)))
                            dve.tensor_tensor(vp[:, u, :, :, 0:D], pads[u].rearrange("p (t h d) -> p t h d", t=TT, d=D),
                                              pl["vrow"].rearrange("p (h d) -> p h d", d=D).unsqueeze(1)
                                              .broadcast_to([P, TT, H, D]), ALU.add) \
                                .then_inc(vector.sem, vector.mark(("v", name, u)))
                    if kind in KEYS:
                        nk = KEYS[kind]
                        nh = PAD // nk
                        N = len(units_of(s))

                        def select(n):
                            dve.wait_ge(scalar.sem, scalar.at(("copied", n)))
                            p3 = pr[:, n % RP, :].rearrange("p (h k) -> p h k", k=nk)
                            r3 = rk[:, n % 2, :].rearrange("p (h k) -> p h k", k=nk)
                            if n - 2 >= first_unit[name, 0]:
                                dve.wait_ge(pool.sem, pool.at(("kept", n - 2)))
                            for step in range(TOPK // 8):
                                src = r3 if step else p3
                                for h in range(nh):
                                    i = dve.max(top[:, n % 2, step, h, :], src[:, h, :])
                                i.then_inc(vector.sem, vector.mark(("top", n, step)))
                                mine(("top", n, step))
                                for h in range(nh):
                                    i = dve.match_replace(out=r3[:, h, :], in_to_replace=top[:, n % 2, step, h, :],
                                                          in_values=src[:, h, :], imm_value=LOWEST)
                                i.then_inc(vector.sem, vector.mark(("replaced", n, step)))
                                mine(("replaced", n, step))
                            dve.tensor_tensor(r3, p3, r3, ALU.is_gt) \
                                .then_inc(vector.sem, vector.mark(("selected", n)))

                        def shift(n):
                            maxima = mx[:, n % RP, 0:nh]
                            p3 = pr[:, n % RP, :].rearrange("p (h k) -> p h k", k=nk)
                            dve.wait_ge(tensor.sem, tensor.at(("scores", n)))
                            dve.tensor_reduce(maxima, cols(n % 2, nh), AX.X, ALU.max) \
                                .then_inc(vector.sem, vector.mark(("max", n)))
                            if n >= RP:
                                dve.wait_ge(tensor.sem, tensor.at(("turned probs", n - RP)))
                            mine(("max", n))
                            dve.tensor_tensor(p3, cols(n % 2, nh), maxima.unsqueeze(2).broadcast_to([P, nh, nk]),
                                              ALU.subtract).then_inc(vector.sem, vector.mark(("shifted", n)))

                        for u in range(LANES):
                            for j in range(N + 3):
                                if j < N:
                                    (select if kind == "topk" else shift)(first_unit[name, u] + j)
                                if tile_done(s, j - 3):
                                    t = units_of(s)[j - 3][0]
                                    o = pads[3][:, (t % 2) * L:(t % 2) * L + H * (D + 1)] \
                                        .rearrange("p (h d) -> p h d", d=D + 1)
                                    dve.wait_ge(tensor.sem, tensor.at(("values", first_unit[name, u] + j - 3)))
                                    dve.reciprocal(rs[:, t % 2, :].unsqueeze(2), o[:, :, D:D + 1]) \
                                        .then_inc(vector.sem, vector.mark(("1/sums", name, u, t)))
                                    mine(("1/sums", name, u, t))
                                    dve.tensor_tensor(on[:, u, t, :].rearrange("p (h d) -> p h d", d=D), o[:, :, 0:D],
                                                      rs[:, t % 2, :].unsqueeze(2).broadcast_to([P, H, D]),
                                                      ALU.mult).then_inc(vector.sem, vector.mark(("o", name, u, t)))
                    if kind == "swiglu":
                        for u in range(LANES):
                            for m in range(MC):
                                k = u * MC + m
                                dve.wait_ge(scalar.sem, scalar.at(("silu", name, u, m)))
                                dve.scalar_tensor_tensor(out=hid[:, u, m, :], in0=pads[k % 3][:, L:2 * L],
                                                         scalar=column(s["b1"], MC + m),
                                                         in1=rk[:, 0, (k % 2) * L:(k % 2 + 1) * L],
                                                         op0=ALU.add, op1=ALU.mult) \
                                    .then_inc(vector.sem, vector.mark(("hidden", name, u, m)))
                    for u in range(LANES):
                        branch(u, u)
                end_pass(dve, "vector")

        @block.tensor
        def _(pe):
            mm = pe.matmul
            pe.wait_ge(set_pool.sem, set_pool.at("ident"))
            pe.wait_ge(load_cond.sem, load_cond.at("cond"))
            for c in range(CH):
                i = pe.transpose(pads[0][:, c * B:(c + 1) * B], crow[:, c * P:(c + 1) * P], ident[0:B, 0:B])
            i.then_inc(set_tensor.sem, set_tensor.mark("cond"))
            pe.wait_ge(load_rows.sem, load_rows.at(MODS[-1][1]))
            pe.wait_ge(set_pool.sem, set_pool.at("mask"))
            pe.transpose(pads[1][:, 0:nrows], brow[0:nrows, :], ident[0:nrows, 0:nrows]) \
                .then_inc(set_tensor.sem, set_tensor.mark("bias columns"))
            pe.wait_ge(set_scalar.sem, set_scalar.at("silu"))
            ring = arena[:, 0:16 * CH * C].rearrange("p (s c n) -> p s c n", s=16, c=CH)
            for vec in range(NMOD):
                ld = load_mod[vec % 16]
                pe.wait_ge(ld.sem, ld.at(vec))
                for m in range(CH):
                    k = vec * CH + m
                    for c in range(CH):
                        i = mm(pads[2][:, k * B:(k + 1) * B], ring[:, vec % 16, c, m * P:(m + 1) * P], condT[:, c, :],
                               start=(c == 0), stop=(c == CH - 1))
                i.then_inc(set_tensor.sem, set_tensor.mark(("mod", vec)))
            pe.wait_ge(set_vector.sem, set_vector.at("1 + scale"))
            for g, vec in enumerate(GATES):
                for c in range(CH):
                    k = g * CH + c
                    pad, o = pads[k // 8], (k % 8) * P
                    i = pe.transpose(pad[0:B, o:o + P], modT[:, vec * CH + c, :], ident[:, :])
            i.then_inc(set_tensor.sem, set_tensor.mark("gates"))
            pe.wait_ge(set_vector.sem, set_vector.at("gate rows"))

            with pe.Fori(0, PASSES) as it:
                holder = [None] * 8

                def claim(pad, drained_by, half=None):
                    banks = [2 * pad, 2 * pad + 1] if half is None else [2 * pad + half]
                    for b in sorted({banks[0], banks[-1]}):
                        if holder[b] and not (b != banks[0] and holder[b] == before):
                            pe.wait_ge(holder[b][0].sem, holder[b][0].at(holder[b][1]))
                        before = holder[b]
                        holder[b] = drained_by

                for si, s in enumerate(SITES):
                    name, kind = s["name"], s["kind"]
                    pl, lw = place[name], load_w[si]
                    drained = "branch" if s["gate"] is not None else "x"
                    for u in range(LANES):
                        claim(u, (scalar, ("h", name, u, CH - 1)))
                        for t in range(TT):
                            pe.wait_ge(vector.sem, vector.at(("normed", name, u, t)))
                            for c in range(CH):
                                i = pe.transpose(cols(u, CH)[:, c, t * P:(t + 1) * P], hn[:, u, t, c * P:(c + 1) * P],
                                                 ident[:, :])
                        i.then_inc(tensor.sem, tensor.mark(("turned", name, u)))
                    if kind in CROSS:
                        claim(3, (scalar, ("ctx", name, CH - 1, LANES - 1)))
                        if s["ctx_ln"]:
                            pe.wait_ge(vector.sem, vector.at(("ctx normed", name)))
                            src = cn
                        else:
                            pe.wait_ge(load_ctx.sem, load_ctx.at("context"))
                            src = ctok
                        for c in range(CH):
                            i = pe.transpose(pads[3][:, c * P:(c + 1) * P], src[:, c * P:(c + 1) * P], ident[:, :])
                        i.then_inc(tensor.sem, tensor.mark(("ctx turned", name)))
                    if kind == "full":
                        pe.wait_ge(lw.sem, lw.at((name, LOADS[kind] - 1)))
                        wq = pl["qkv"]
                        for what, x_, k in full_order():
                            g, u = x_ % GROUPS, x_ // GROUPS
                            if what == "project":
                                u = x_
                                pe.wait_ge(scalar.sem, scalar.at(("h", name, u, CH - 1)))
                                for w, pad, first in (("q", 1, 0), ("k", 2, C)):
                                    claim(pad, (vector, ("low", name, u, w, CH - 1)))
                                    for m in range(CH):
                                        for c in range(CH):
                                            i = mm(cols(pad, CH)[:, m, :],
                                                   wq[:, c, first + m * P:first + (m + 1) * P], hT[:, u, c, :],
                                                   start=(c == 0), stop=(c == CH - 1))
                                    i.then_inc(tensor.sem, tensor.mark((w, name, u)))
                                claim(1, (vector, ("v", name, u)))
                                for t in range(TT):
                                    for c in range(CH):
                                        i = mm(cols(1, TT)[:, t, :], hT[:, u, c, t * P:(t + 1) * P],
                                               wq[:, c, 2 * C:3 * C], start=(c == 0), stop=(c == CH - 1))
                                i.then_inc(tensor.sem, tensor.mark(("v", name, u)))
                            if what == "maxima":
                                b_ = (x_ * (GH * TT + 1) + k) % 2
                                claim(0, (vector, ("maxima", name, x_, k)), half=b_)
                                if k == 0:
                                    pe.wait_ge(load_stack[g].sem, load_stack[g].at((name, x_, "k", 1)))
                                    pe.wait_ge(pool.sem, pool.at(("cleared", name)))
                                j, t = k // TT, k % TT
                                mm(pads[0][:, b_ * L:(b_ + 1) * L], Qs[0:MR, g, j // 2, j % 2, t * P:(t + 1) * P],
                                   Ks[0:MR, g, j // 2, j % 2, :], start=True, stop=True) \
                                    .then_inc(tensor.sem, tensor.mark(("maxima", name, x_, k)))
                            if what == "turn":
                                b_ = (x_ * (GH * TT + 1) + GH * TT) % 2
                                claim(0, (vector, ("max low", name, x_)), half=b_)
                                pe.wait_ge(vector.sem, vector.at(("maxima", name, x_, GH * TT - 1)))
                                pe.transpose(pads[0][0:GH * TT, b_ * L:b_ * L + P], nm[:, x_ % 2, :], ident[:, :]) \
                                    .then_inc(tensor.sem, tensor.mark(("turn", name, x_)))
                            if what == "scores":
                                if k == 0:
                                    pe.wait_ge(load_max[g].sem, load_max[g].at((name, x_)))
                                e, kt = k % 2, k // 2
                                claim(1 + e, (scalar, ("probs", name, x_, k)))
                                for j in (2 * e, 2 * e + 1):
                                    i = mm(pads[1 + e][:, (j % 2) * L:(j % 2 + 1) * L],
                                           Ks[:, g, j // 2, j % 2, kt * P:(kt + 1) * P], Qs[:, g, j // 2, j % 2, :],
                                           start=True, stop=True)
                                i.then_inc(tensor.sem, tensor.mark(("scores", name, x_, k)))
                            if what == "values":
                                e, kt = k % 2, k // 2
                                if k == 0:
                                    claim(3, (scalar, ("o", name, x_)), half=x_ % 2)
                                    if g == 0:
                                        pe.wait_ge(vector.sem, vector.at(("v", name, u)))
                                pe.wait_ge(scalar.sem, scalar.at(("probs", name, x_, k)))
                                for j in (2 * e, 2 * e + 1):
                                    n = x_ * 2 * TT + k
                                    i = mm(pads[3][2 * D * j:2 * D * (j + 1), (x_ % 2) * L:(x_ % 2 + 1) * L],
                                           vp[:, u, kt, GH * g + j, :], pr[:, n % RP, (j % 2) * L:(j % 2 + 1) * L],
                                           start=(kt == 0), stop=(kt == TT - 1))
                                i.then_inc(tensor.sem, tensor.mark(("values", name, x_, k)))
                            if what == "split":
                                pe.wait_ge(scalar.sem, scalar.at(("o", name, GROUPS * x_ + GROUPS - 1)))
                                for t in range(TT):
                                    claim(1 + t // 2, (vector, ("o", name, x_, t)), half=t % 2)
                                    for q in range(GROUPS):
                                        o = (t % 2) * L + q * P
                                        i = pe.transpose(pads[1 + t // 2][:, o:o + P], O4[:, q, t * P:(t + 1) * P],
                                                         ident[:, :])
                                i.then_inc(tensor.sem, tensor.mark(("split", name, x_)))
                            if what == "turn back":
                                pe.wait_ge(vector.sem, vector.at(("o", name, x_, TT - 1)))
                                claim(1, (scalar, ("oT", name, x_)))
                                for t in range(TT):
                                    for c in range(CH):
                                        i = pe.transpose(cols(1, CH)[:, c, t * P:(t + 1) * P],
                                                         on4[:, t, c * P:(c + 1) * P], ident[:, :])
                                i.then_inc(tensor.sem, tensor.mark(("turned back", name, x_)))
                            if what == "out":
                                claim(2, (vector, (drained, name, x_)))
                                pe.wait_ge(scalar.sem, scalar.at(("oT", name, x_)))
                                for t in range(TT):
                                    for c in range(CH):
                                        i = mm(cols(2, TT)[:, t, :], oT[:, x_, c, t * P:(t + 1) * P], pl["o"][:, c, :],
                                               start=(c == 0), stop=(c == CH - 1))
                                i.then_inc(tensor.sem, tensor.mark(("out", name, x_)))
                        continue
                    if kind in KEYS:
                        nk = KEYS[kind]
                        pe.wait_ge(lw.sem, lw.at((name, 3 if kind in SELF else 4)))
                        for u in range(LANES):
                            pe.wait_ge(scalar.sem, scalar.at(("h", name, u, CH - 1)))
                            wq = pl["qkv"] if kind in SELF else pl["q"]
                            claim(2 - u, (scalar, ("q", name, u, CH - 1)))
                            for m in range(CH):
                                for c in range(CH):
                                    i = mm(cols(2 - u, CH)[:, m, :], wq[:, c, m * P:(m + 1) * P], hT[:, u, c, :],
                                           start=(c == 0), stop=(c == CH - 1))
                            i.then_inc(tensor.sem, tensor.mark(("queries", name, u)))
                            if kind in SELF:
                                claim(3, (scalar, ("keys", name, u)))
                                for m in range(CH):
                                    for c in range(CH):
                                        i = mm(cols(3, CH)[:, m, :], wq[:, c, C + m * P:C + (m + 1) * P],
                                               hT[:, u, c, :], start=(c == 0), stop=(c == CH - 1))
                                i.then_inc(tensor.sem, tensor.mark(("keys", name, u)))
                                claim(u, (vector, ("v", name, u)))
                                for t in range(TT):
                                    for c in range(CH):
                                        i = mm(cols(u, TT)[:, t, :], hT[:, u, c, t * P:(t + 1) * P],
                                               wq[:, c, 2 * C:3 * C], start=(c == 0), stop=(c == CH - 1))
                                i.then_inc(tensor.sem, tensor.mark(("v", name, u)))
                        if kind in CROSS:
                            claim(0, (scalar, ("ctx keys", name, CH - 1)))
                            pe.wait_ge(scalar.sem, scalar.at(("ctx", name, CH - 1, LANES - 1)))
                            for m in range(CH):
                                for c in range(CH):
                                    i = mm(pads[0][:, m * P:(m + 1) * P].rearrange("p (u k) -> p u k", u=LANES),
                                           pl["kv"][:, c, m * P:(m + 1) * P], cT[:, c, :, 0, :],
                                           start=(c == 0), stop=(c == CH - 1))
                            i.then_inc(tensor.sem, tensor.mark(("ctx keys", name)))
                            claim(3, (vector, ("ctx values", name, LANES - 1, 1)))
                            for u in range(LANES):
                                for c in range(CH):
                                    i = mm(pads[3][:, u * C:(u + 1) * C], cT[:, c, u].rearrange("p e k -> p (e k)"),
                                           pl["kv"][:, c, C:2 * C], start=(c == 0), stop=(c == CH - 1))
                            i.then_inc(tensor.sem, tensor.mark(("ctx values", name)))
                        for u in range(LANES):
                            f, units = first_unit[name, u], units_of(s)
                            N = len(units)

                            def scores(j):
                                n = f + j
                                t, h0, nh = units[j]
                                if kind == "topk":
                                    claim(n % 2, (scalar, ("copied", n)))
                                else:
                                    claim(n % 2, (vector, ("shifted", n)))
                                if j == 0:
                                    pe.wait_ge(scalar.sem, scalar.at(("q", name, u, CH - 1)))
                                blocks = pool if u else vector
                                if kind in CROSS and j == 0:
                                    blocks_made = blocks.at(("ctx blocks", name, u, CH - 1))
                                    pe.wait_ge(blocks.sem, blocks_made)
                                if kind in SELF and j < H // nh:
                                    hl = h0 + nh - 1
                                    pe.wait_ge(blocks.sem, blocks.at(("blocks", name, u, hl // HC, hl % HC)))
                                for g in range(2):
                                    o = pads[n % 2][:, g * L:(g + 1) * L]
                                    if kind == "win":
                                        c, h = h0 // HC, h0 % HC + g * (L // nk)
                                        rhs = kd[:, u, c, h:h + L // nk, t * P:(t + 1) * P]
                                        o = o.rearrange("p (h k) -> p h k", k=nk)
                                    else:
                                        c, rhs = g, kc[:, u, g].rearrange("p h k -> p (h k)")
                                    i = mm(o, qT[:, u, c, t * P:(t + 1) * P], rhs, start=True, stop=True)
                                i.then_inc(tensor.sem, tensor.mark(("scores", n)))

                            def turn(j):
                                n = f + j
                                claim(2, (scalar, ("pT", n)))
                                probs = (pool, ("kept", n)) if kind == "topk" else (scalar, ("exp", n))
                                pe.wait_ge(probs[0].sem, probs[0].at(probs[1]))
                                for k in range(PAD // P):
                                    i = pe.transpose(pads[2][:, k * P:(k + 1) * P],
                                                     pr[:, n % RP, k * P:(k + 1) * P], ident[:, :])
                                i.then_inc(tensor.sem, tensor.mark(("turned probs", n)))

                            def values(j):
                                n = f + j
                                t, h0, nh = units[j]
                                if h0 == 0:
                                    claim(3, (scalar, ("o", name, u, t)), half=t % 2)
                                if j == 0:
                                    made = ("v", name, u) if kind in SELF else ("ctx values", name, u, 1)
                                    pe.wait_ge(vector.sem, vector.at(made))
                                pe.wait_ge(scalar.sem, scalar.at(("pT", n)))
                                first = (t % 2) * L
                                for k in range(PAD // P):
                                    if kind in SELF:
                                        o, w = first + (h0 + k) * (D + 1), D + 1
                                        rhs = vp[:, u, t, h0 + k, 0:D + 1]
                                    else:
                                        o, w = first + 2 * k * (D + 1), 2 * (D + 1)
                                        rhs = vc[:, u, k].rearrange("p e d -> p (e d)")
                                    i = mm(pads[3][:, o:o + w], pT[:, n % RT, k, :], rhs, start=True, stop=True)
                                i.then_inc(tensor.sem, tensor.mark(("values", n)))

                            def turn_output(t):
                                pe.wait_ge(vector.sem, vector.at(("o", name, u, t)))
                                for c in range(CH):
                                    o = (t % 2) * L + c * P
                                    i = pe.transpose(pads[3][:, o:o + P], on[:, u, t, c * P:(c + 1) * P], ident[:, :])
                                i.then_inc(tensor.sem, tensor.mark(("o turned", name, u, t)))

                            for j in range(N + 4):
                                if j < N:
                                    scores(j)
                                if 0 <= j - 2 < N:
                                    turn(j - 2)
                                if 0 <= j - 3 < N:
                                    values(j - 3)
                                if tile_done(s, j - 4):
                                    turn_output(units[j - 4][0])
                        for u in range(LANES):
                            claim(u, (vector, (drained, name, u)))
                            pe.wait_ge(scalar.sem, scalar.at(("o", name, u, TT - 1)))
                            for t in range(TT):
                                for c in range(CH):
                                    i = mm(cols(u, TT)[:, t, :], oT[:, u, c, t * P:(t + 1) * P], pl["o"][:, c, :],
                                           start=(c == 0), stop=(c == CH - 1))
                            i.then_inc(tensor.sem, tensor.mark(("out", name, u)))
                    else:
                        pe.wait_ge(lw.sem, lw.at((name, 2)))
                        for u in range(LANES):
                            pe.wait_ge(scalar.sem, scalar.at(("h", name, u, CH - 1)))
                            for m in range(MC):
                                if kind == "swiglu":
                                    k = u * MC + m
                                    claim(k % 3, (vector, ("hidden", name, u, m)))
                                    halves = [(0, m * P), (1, HID + m * P)]
                                else:
                                    if m % 2:
                                        continue
                                    k = (u * MC + m) // 2
                                    claim(k % 3, (scalar, ("hidden", name, u, m + 1)))
                                    halves = [(0, m * P), (1, (m + 1) * P)]
                                for g, col in halves:
                                    for c in range(CH):
                                        i = mm(cols(k % 3, 2)[:, g, :], pl["w1"][:, c, col:col + P], hT[:, u, c, :],
                                               start=(c == 0), stop=(c == CH - 1))
                                i.then_inc(tensor.sem, tensor.mark(("up", name, u, m)))
                        for u in range(LANES):
                            claim(u, (vector, (drained, name, u)))
                            sig = vector if kind == "swiglu" else scalar
                            pe.wait_ge(sig.sem, sig.at(("hidden", name, u, MC - 1)))
                            for t in range(TT):
                                for m in range(MC):
                                    i = mm(cols(u, TT)[:, t, :], hid[:, u, m, t * P:(t + 1) * P], pl["w2"][:, m, :],
                                           start=(m == 0), stop=(m == MC - 1))
                            i.then_inc(tensor.sem, tensor.mark(("out", name, u)))
                end_pass(pe, "tensor")
    return {name: s.order for name, s in signals.items()}


def kernel(**inputs):
    import numpy as np
    from concourse import bacc
    from concourse.bass_utils import run_bass_kernel_spmd

    arrays = {f"in_{k}": np.ascontiguousarray(v) for k, v in inputs.items()}

    def program(known):
        nc = bacc.Bacc("TRN2", target_bir_lowering=False, num_devices=1)
        a = {k: nc.dram_tensor(f"in_{k}", v.shape, F32, kind="ExternalInput").ap() for k, v in inputs.items()}
        out = nc.dram_tensor("out", (B, L, C), F32, kind="ExternalOutput").ap()
        return nc, build(nc, a, out, known)

    _, events = program({})
    nc, _ = program(events)
    r = run_bass_kernel_spmd(nc, [arrays], core_ids=[0])
    return r.results[0]["out"]
```

```python
from contextlib import ExitStack

import concourse.bass as bass
import concourse.mybir as mybir

F32 = mybir.dt.float32
F32R = mybir.dt.float32r
ALU = mybir.AluOpType
ACT = mybir.ActivationFunctionType
AX = mybir.AxisListType

P = 128
B, L, C = 4, 512, 256
LC = 64
H, D = 16, 16
CH = C // P
TT = L // P
HC = H // CH
HID = 1024
MC = HID // P
LANES = 2
PASSES = B // LANES
SHIFT = 64
TOPK = 16
SCALE = D ** -0.5
PAD = 1024
RP = 4
GROUPS, GH = 4, 4
LEAD = 26
PATTERN = "SmSmVmm"
RT = 2
LOWEST = -3.4028234e38

MODS = [("L0_xcond_w_ada", "L0_xcond_b_ada", 9), ("L1_xcond_Wss_q", "L1_xcond_bss_q", 2),
        ("L1_xcond_Wss_kv", "L1_xcond_bss_kv", 2), ("L2_xcond_W_mod", "L2_xcond_b_mod", 6),
        ("L3_xcond_adaln_w", "L3_xcond_adaln_b", 6)]
NMOD = sum(n for _, _, n in MODS)
SCALES = [1, 4, 7, 9, 11, 14, 17, 20, 23]
GATES = [2, 5, 8, 15, 18, 21, 24]

COLS = [("L0_xcond_b_qkv", 4), ("L0_xcond_b_q", 2), ("L0_xcond_b_kv", 2), ("L0_xcond_b_m1", 16),
        ("L1_xcond_bq", 2), ("L1_xcond_bkv", 2), ("L2_xcond_b_qkv", 4), ("L2_xcond_b_qc", 2),
        ("L2_xcond_b_kvc", 2), ("L2_xcond_b_mlp1", 8), ("L3_xcond_qkv_b", 4), ("L3_xcond_q_b", 2),
        ("L3_xcond_kv_b", 2), ("L3_xcond_fc1_b", 8)]

SITES = [
    dict(name="self0", kind="win", layer=0, ln=(1e-6, 1, 0), wqkv="L0_xcond_w_qkv", bqkv="L0_xcond_b_qkv",
         wo="L0_xcond_w_so", bo="L0_xcond_b_so", gate=2),
    dict(name="cross0", kind="topk", layer=0, ln=(1e-6, 4, 3), ctx_ln=None, wq="L0_xcond_w_q", bq="L0_xcond_b_q",
         wkv="L0_xcond_w_kv", bkv="L0_xcond_b_kv", wo="L0_xcond_w_co", bo="L0_xcond_b_co", gate=5),
    dict(name="mlp0", kind="swiglu", layer=0, ln=(1e-6, 7, 6), w1="L0_xcond_w_m1", b1="L0_xcond_b_m1",
         w2="L0_xcond_w_m2", bo="L0_xcond_b_m2", gate=8),
    dict(name="cross1", kind="cross", layer=1, ln=(1e-5, 9, 10), ctx_ln=(1e-5, 11, 12), wq="L1_xcond_Wq",
         bq="L1_xcond_bq", wkv="L1_xcond_Wkv", bkv="L1_xcond_bkv", wo="L1_xcond_Wp", bo="L1_xcond_bp", gate=None),
    dict(name="self2", kind="full", layer=2, ln=(1e-6, 14, 13), wqkv="L2_xcond_W_qkv", bqkv="L2_xcond_b_qkv",
         wo="L2_xcond_W_proj", bo="L2_xcond_b_proj", gate=15),
    dict(name="cross2", kind="cross", layer=2, ln=(1e-6, None, None), ctx_ln=(1e-6, None, None),
         wq="L2_xcond_W_qc", bq="L2_xcond_b_qc", wkv="L2_xcond_W_kvc", bkv="L2_xcond_b_kvc",
         wo="L2_xcond_W_cproj", bo="L2_xcond_b_cproj", gate=None),
    dict(name="mlp2", kind="gelu", layer=2, ln=(1e-6, 17, 16), w1="L2_xcond_W_mlp1", b1="L2_xcond_b_mlp1",
         w2="L2_xcond_W_mlp2", bo="L2_xcond_b_mlp2", gate=18),
    dict(name="self3", kind="full", layer=3, ln=(1e-6, 20, 19), wqkv="L3_xcond_qkv_w", bqkv="L3_xcond_qkv_b",
         wo="L3_xcond_sa_proj_w", bo="L3_xcond_sa_proj_b", gate=21),
    dict(name="cross3", kind="cross", layer=3, ln=(1e-6, None, None), ctx_ln=None, wq="L3_xcond_q_w",
         bq="L3_xcond_q_b", wkv="L3_xcond_kv_w", bkv="L3_xcond_kv_b", wo="L3_xcond_ca_proj_w",
         bo="L3_xcond_ca_proj_b", gate=None),
    dict(name="mlp3", kind="gelu", layer=3, ln=(1e-6, 23, 22), w1="L3_xcond_fc1_w", b1="L3_xcond_fc1_b",
         w2="L3_xcond_fc2_w", bo="L3_xcond_fc2_b", gate=24),
]
SELF, CROSS, MLP = ("win", "full"), ("topk", "cross"), ("swiglu", "gelu")
LOADS = {"win": 4, "full": 4, "topk": 5, "cross": 5, "swiglu": 3, "gelu": 3}
KEYS = {"win": P, "full": L, "topk": LC, "cross": LC}


class Signal:

    def __init__(self, sem, known, step=1):
        self.sem, self.known, self.step = sem, known or {}, step
        self.order = {}

    def mark(self, event):
        assert event not in self.order, event
        self.order[event] = len(self.order) + 1
        return self.step

    def at(self, event):
        return self.step * self.known.get(event, 1)


def full_order():
    order, ahead = [("project", u, 0) for u in range(LANES)], []
    for x in range(LANES * GROUPS):
        ahead += [("maxima", x, k) for k in range(GH * TT)] + [("turn", x, 0)]

    def more(n):
        while n and ahead:
            n -= ahead[0][0] == "maxima"
            order.append(ahead.pop(0))

    more(LEAD)
    steps = [(x, kt) for x in range(LANES * GROUPS) for kt in range(TT)]
    for i, (x, kt) in enumerate(steps):
        k = 2 * kt
        for piece in PATTERN:
            if piece == "S":
                order.append(("scores", x, k))
                k += 1
            elif piece == "m":
                more(1)
            elif i:
                order.append(("values", *steps[i - 1]))
        for at, what in (1, "split"), (3, "turn back"), (4, "out"):
            if i == GROUPS * TT + at:
                order.append((what, 0, 0))
    return order + [("values", *steps[-1]), ("split", 1, 0), ("turn back", 1, 0), ("out", 1, 0)]


def units_of(site):
    if site["kind"] == "full":
        return []
    nh = PAD // KEYS[site["kind"]]
    return [(u, t, h0, nh) for u in range(LANES) for t in range(TT) for h0 in range(0, H, nh)]


def build(nc, a, out, known):
    ctx = ExitStack()
    with ctx:
        starts = {}

        def sb(name, shape):
            starts[name] = nc.sbuf_base
            return ctx.enter_context(nc.sbuf_tensor(name, shape, F32))

        def rounded(name, like, shape, skip=0):
            return nc.alloc_sbuf_tensor_at(name, shape, F32R, offset=starts[like] + skip)

        x = sb("x", [P, LANES, TT, C])
        ht = sb("ht", [P, LANES, TT, C])
        hn = ht
        on = ht
        O4 = ht[:, :, :, :].rearrange("p a t c -> p (a t c)").rearrange("p (g l) -> p g l", g=GROUPS)
        hT = sb("hT", [P, LANES, CH, L])
        qT = sb("qT", [P, LANES, CH, L])
        kT = sb("kT", [P, LANES, CH, L])
        start, half_bytes = nc.sbuf_base, GROUPS * GH * L * 4
        arena = sb("arena", [P, 2 * GROUPS * GH * L])

        def in_arena(name, shape, dt, part, skip=0):
            return nc.alloc_sbuf_tensor_at(name, shape, dt, offset=start + part * half_bytes + skip)

        kd = in_arena("kd", [P, LANES, CH, HC, L], F32, 0)
        kc = in_arena("kc", [P, LANES, CH, HC, LC], F32, 0)
        hid = in_arena("hid", [P, LANES, MC, L], F32R, 0)
        act_out = in_arena("act_out", [P, 4, L], F32, 1)
        wH = in_arena("wH", [P, 24 * C], F32R, 1, half_bytes // 4)
        Qs = in_arena("Qs", [P, GROUPS, CH, 2, L], F32R, 0)
        Ks = in_arena("Ks", [P, GROUPS, CH, 2, L], F32R, 1)
        vp = sb("vp", [P, LANES, TT, H, 2 * D])
        pr = sb("pr", [P, RP, PAD])
        pT = sb("pT", [P, RT, PAD // P, P])
        halves = [(qT, kT)] + [[pr[:, 2 * i:2 * i + 2, :].rearrange("p r (c l) -> p r c l", c=CH) for i in range(2)]]
        oT = hT
        rk = in_arena("rk", [P, 2, PAD], F32, 0, half_bytes // 2)
        wA = sb("wA", [P, 2, 8 * C])
        nm = sb("nm", [P, 2, GH * TT])
        nmT = sb("nmT", [GH * TT, 2, 2, P])
        wM = sb("wM", [P, 24 * C])
        rows = sb("rows", [P, 5, C])
        gate = sb("gate", [P, LANES, C])
        ctok = sb("ctok", [P, C])
        cn = in_arena("cn", [P, C], F32, 1)
        cT = in_arena("cT", [P, CH, LANES, 2, LC], F32, 1, C * 4)
        kTc = in_arena("kTc", [P, CH, LANES, LC], F32, 1, 3 * C * 4)
        vc = sb("vc", [P, LANES, H // 2, 2, D + 1])
        ident = sb("ident", [P, P])
        mask = sb("mask", [P, HC])
        bcol = sb("bcol", [P, P])
        modT = sb("modT", [P, NMOD * CH, B])
        cur = sb("cur", [P, NMOD * CH, LANES])
        stats = sb("stats", [P, 2, TT, 6])
        mv = sb("mv", [P, 2, TT, 2])
        rstd = sb("rstd", [P, 2, TT])
        cstats = sb("cstats", [P, 10])
        half = sb("half", [P, TT])
        mx = sb("mx", [P, RP, H])
        rs = sb("rs", [P, 2, H])
        gb = sb("gb", [P, C])
        top = sb("top", [P, 2, 2, H, 8])
        condT = sb("condT", [P, CH, B])
        crow = ht[0:B, 0, 0, :]
        grow = pT[0:B].rearrange("p r a b -> p (r a b)")[:, 0:len(GATES) * C]
        pads = [ctx.enter_context(nc.psum_tensor(f"pad{i}", [P, PAD], F32)) for i in range(4)]
        brow = act_out[:, 0, 0:P]
        nm_dram = nc.dram_tensor("maxima_rows", (2, 2, GH * TT * P), F32, kind="Internal").ap()
        q_dram = nc.dram_tensor("stack_queries", (LANES, H, D, 2, L), F32, kind="Internal").ap()
        k_dram = nc.dram_tensor("stack_keys", (LANES, 2, H, D, 2, L), F32, kind="Internal").ap()
        ones_dram = nc.dram_tensor("ones", (2, GROUPS * GH * L), F32, kind="Internal").ap()
        gates_dram = nc.dram_tensor("gate_rows", (B, len(GATES), C), F32, kind="Internal").ap()

        wL = rounded("wL", "wM", [P, 24 * C])
        hH = rounded("hH", "qT", [P, LANES, CH, L])
        hL = rounded("hL", "kT", [P, LANES, CH, L])
        low_of = [rounded("hidden_low0", "pr", [P, MC, L]), rounded("hidden_low1", "pT", [P, MC // 2, L]),
                  rounded("hidden_low2", "hT", [P, MC // 2, L])]

        def hidden_low(u, m):
            return low_of[0][:, m, :] if u == 0 else low_of[1 + m // (MC // 2)][:, m % (MC // 2), :]

        on4 = pT[:, 0].rearrange("p a b -> p (a b)").rearrange("p (t c) -> p t c", t=TT)
        MR = 96
        signals = {}

        def signal(name, step=1):
            sem = ctx.enter_context(nc.semaphore(name))
            signals[name] = Signal(sem, known.get(name), step)
            return signals[name]

        tensor = signal("tensor_filled")
        scalar = signal("scalar_wrote")
        vector = signal("vector_wrote")
        pool = signal("pool_wrote")
        set_tensor = signal("setup_tensor")
        set_scalar = signal("setup_scalar")
        set_vector = signal("setup_vector")
        set_pool = signal("setup_pool")
        load_cond = signal("cond_loaded", 16)
        load_rows = signal("bias_rows_loaded", 16)
        load_mod = [signal(f"mod_weights_loaded{i}", 16) for i in range(16)]
        gates_out = signal("gates_stored", 16)
        ones_out = signal("ones_stored", 16)
        load_ones = signal("ones_loaded", 16)
        load_x = [signal(f"x_loaded{u}", 16) for u in range(LANES)]
        load_ctx = signal("context_loaded", 16)
        load_w = [signal(f"weights_loaded{i}", 16) for i in range(len(SITES))]
        load_gate = signal("gate_loaded", 16)
        load_stack = [signal(f"stack_loaded{i}", 16) for i in range(GROUPS)]
        load_max = [signal(f"maxima_loaded{i}", 16) for i in range(GROUPS)]
        max_out = signal("maxima_stored", 16)
        stack_out = [signal(f"stack_stored{c}", 16) for c in range(CH)]
        stored = signal("stored", 16)
        in_pass = [tensor, scalar, vector, pool, *load_x, load_ctx, *load_w, load_gate, *load_stack, *load_max, load_ones,
                   max_out, *stack_out, stored]
        arrived = ctx.enter_context(nc.semaphore("arrived"))
        resume = {e: ctx.enter_context(nc.semaphore(f"resume_{e}")) for e in ("tensor", "scalar", "vector", "pool")}

        def end_pass(eng, name):
            eng.wait_ge(stored.sem, stored.at(("start", LANES - 1)))
            eng.sem_inc(arrived, 1)
            eng.wait_ge(resume[name], 1)
            eng.sem_clear(resume[name])

        place = {}
        attention_sites = [s["name"] for s in SITES if s["kind"] in KEYS]
        for s in SITES:
            n = s["name"]
            par = attention_sites.index(n) % 2 if n in attention_sites else 0
            region, first = wA[:, par], 0
            if s["kind"] in SELF:
                place[n] = dict(qkv=region[:, 0:6 * C].rearrange("p (c n) -> p c n", c=CH),
                                o=region[:, 6 * C:8 * C].rearrange("p (c n) -> p c n", c=CH),
                                vrow=rows[:, 2 * par], orow=rows[:, 2 * par + 1])
            elif s["kind"] in CROSS:
                place[n] = dict(q=region[:, first:first + 2 * C].rearrange("p (c n) -> p c n", c=CH),
                                kv=region[:, first + 2 * C:first + 6 * C].rearrange("p (c n) -> p c n", c=CH),
                                o=region[:, first + 6 * C:first + 8 * C].rearrange("p (c n) -> p c n", c=CH),
                                vrow=rows[:, 2 * par], orow=rows[:, 2 * par + 1])
            else:
                up = 2 * HID if s["kind"] == "swiglu" else HID
                place[n] = dict(used=[(0, CH * up), (16 * C, 24 * C)], orow=rows[:, 4])
                for part, w_ in (("", wM), ("H", wH), ("L", wL)):
                    place[n]["w1" + part] = w_[:, 0:CH * up].rearrange("p (c n) -> p c n", c=CH)
                    place[n]["w2" + part] = w_[:, 16 * C:24 * C].rearrange("p (m n) -> p m n", m=MC)

        col_of, n = {}, 0
        for name, k in COLS:
            col_of[name] = n
            n += k
        mod_col = n
        nrows = mod_col + NMOD * CH
        assert nrows <= P

        def column(name, i):
            return bcol[:, col_of[name] + i:col_of[name] + i + 1]

        def modulation(vec, c, u):
            return cur[:, vec * CH + c, u:u + 1]

        def cols(pad, shape):
            return pads[pad][:, :].rearrange("p (a b) -> p a b", a=shape)

        def pads_of(kind, u):
            return (u, 2 - u) if kind not in CROSS or u == 0 else (2, 3)

        attn_units = []
        first_unit = {}
        for s in SITES:
            if s["kind"] in KEYS:
                n = len(units_of(s))
                for u in range(LANES):
                    first_unit[s["name"], u] = len(attn_units) + u * n // LANES
                attn_units += units_of(s)

        def last_user_of_weights(site):
            names = [s["name"] for s in SITES]
            same = [s for s in SITES[:names.index(site["name"])] if (s["kind"] in MLP) == (site["kind"] in MLP)]
            back = 1 if site["kind"] in MLP else 2
            return ("out", same[-back]["name"], LANES - 1) if len(same) >= back else None

        def tile_done(site, j):
            units = units_of(site)
            return 0 <= j < len(units) and units[j][2] + units[j][3] == H

        def weight_pieces(site):
            mlp = SITES[(SITES.index(site) + 1) % len(SITES)]
            if site["kind"] not in CROSS or mlp["kind"] not in MLP:
                return mlp, []
            return mlp, [(a_, a_ + PAD) for lo, hi in place[mlp["name"]]["used"] for a_ in range(lo, hi, PAD)]

        def first_lane_done(site):
            return len(units_of(site)) // LANES + 5

        block = ctx.enter_context(nc.Block())

        @block.sync
        def _(sp):
            sp.dma_start(crow, a["cond_1024"]).then_inc(load_cond.sem, load_cond.mark("cond"))
            ring = arena[:, 0:16 * CH * C].rearrange("p (s c n) -> p s c n", s=16, c=CH)

            def load_bias_rows():
                for name, k in COLS:
                    r = col_of[name]
                    sp.dma_start(brow[r:r + k, :], a[name][0:k * P].rearrange("(k p) -> k p", p=P)) \
                        .then_inc(load_rows.sem, load_rows.mark(name))
                r = mod_col
                for _, name, k in MODS:
                    sp.dma_start(brow[r:r + CH * k, :], a[name].rearrange("(k p) -> k p", p=P)) \
                        .then_inc(load_rows.sem, load_rows.mark(name))
                    r += CH * k

            vec = 0
            for w, _, n in MODS:
                for i in range(n):
                    if vec == 16:
                        load_bias_rows()
                    if vec >= 16:
                        sp.wait_ge(set_tensor.sem, set_tensor.at(("mod", vec - 16)))
                    ld = load_mod[vec % 16]
                    sp.dma_start(ring[:, vec % 16], a[w][:, i * C:(i + 1) * C].rearrange("(c p) n -> p c n", p=P)) \
                        .then_inc(ld.sem, ld.mark(vec))
                    vec += 1
            with sp.Fori(0, PASSES) as it:
                def load_weights(i):
                    s, pl, ld = SITES[i], place[SITES[i]["name"]], load_w[i]
                    before = last_user_of_weights(s)
                    if before:
                        sp.wait_ge(tensor.sem, tensor.at(before))
                        sp.wait_ge(vector.sem, vector.at(("x",) + before[1:]))
                        sp.wait_ge(pool.sem, pool.at(("biased",) + before[1:]))

                    def w(dst, src):
                        sp.dma_start(dst, src).then_inc(ld.sem, ld.mark((s["name"], len(ld.order))))

                    def row(dst, src):
                        w(dst, src.unsqueeze(0).broadcast_to([P, C]))

                    if s["kind"] in SELF:
                        w(pl["qkv"], a[s["wqkv"]].rearrange("(c p) n -> p c n", p=P))
                        row(pl["vrow"], a[s["bqkv"]][2 * C:3 * C])
                    elif s["kind"] in CROSS:
                        w(pl["q"], a[s["wq"]].rearrange("(c p) n -> p c n", p=P))
                        w(pl["kv"], a[s["wkv"]].rearrange("(c p) n -> p c n", p=P))
                        row(pl["vrow"], a[s["bkv"]][C:2 * C])
                    else:
                        w(pl["w1"], a[s["w1"]].rearrange("(c p) n -> p c n", p=P))
                        w(pl["w2"], a[s["w2"]].rearrange("(m p) n -> p m n", p=P))
                    if s["kind"] not in MLP:
                        w(pl["o"], a[s["wo"]].rearrange("(c p) n -> p c n", p=P))
                    row(pl["orow"], a[s["bo"]])

                for u in range(LANES):
                    b = it * LANES + u
                    xb = a["x"][bass.ds(b, 1), :, :].rearrange("o t c -> (o t) c")
                    ld = load_x[u]
                    sp.dma_start(x[:, u, 0:TT - 1, :],
                                 xb[SHIFT:SHIFT + (TT - 1) * P, :].rearrange("(t p) c -> p t c", p=P)) \
                        .then_inc(ld.sem, ld.mark("tiles"))
                    sp.dma_start(x[0:P - SHIFT, u, TT - 1, :], xb[L - SHIFT:L, :]).then_inc(ld.sem, ld.mark("end"))
                    sp.dma_start(x[P - SHIFT:P, u, TT - 1, :], xb[0:SHIFT, :]).then_inc(ld.sem, ld.mark("start"))
                sp.dma_start(ctok[:, :], a["ctx_1024"][bass.ds(it * LANES, LANES), :, :].rearrange("u t c -> (u t) c")) \
                    .then_inc(load_ctx.sem, load_ctx.mark("context"))
                loaded = set()
                for i, s in enumerate(SITES):
                    if last_user_of_weights(s) is None:
                        load_weights(i)
                        loaded.add(i)
                gated = [s for s in SITES if s["gate"] is not None]
                for i, s in enumerate(SITES):
                    if s["gate"] is not None:
                        g = gated.index(s)
                        if g >= 1:
                            sp.wait_ge(pool.sem, pool.at(("biased", gated[g - 1]["name"], LANES - 1)))
                            sp.wait_ge(vector.sem, vector.at(("x", gated[g - 1]["name"], LANES - 1)))
                        gi = GATES.index(s["gate"])
                        sp.wait_ge(gates_out.sem, gates_out.at("gates"))
                        sp.dma_start(gate[:, :, :],
                                     gates_dram[bass.ds(it * LANES, LANES), gi, :].unsqueeze(0)
                                     .broadcast_to([P, LANES, C])) \
                            .then_inc(load_gate.sem, load_gate.mark(s["name"]))
                    if s["kind"] == "full":
                        name = s["name"]

                        def store_heads(u, c):
                            for w, src in zip("qk", halves[u]):
                                sp.wait_ge(scalar.sem, scalar.at(("high", name, u, w, c)))
                                sp.wait_ge(vector.sem, vector.at(("low", name, u, w, c)))
                                for low in range(2):
                                    for part in range(2 if w == "k" else 1):
                                        hs = slice(c * HC, (c + 1) * HC)
                                        dst = k_dram[u, part, hs, :, low ^ part, :] if w == "k" else \
                                            q_dram[u, hs, :, low, :]
                                        sp.dma_start(dst.rearrange("h d l -> (h d) l"), src[:, low, c, :]) \
                                            .then_inc(stack_out[c].sem, stack_out[c].mark((name, u, w, low, part)))

                        def load_stacks(x_):
                            u, g = x_ // GROUPS, x_ % GROUPS
                            if x_ >= GROUPS:
                                sp.wait_ge(tensor.sem, tensor.at(("scores", name, x_ - GROUPS, 2 * TT - 1)))
                            so = stack_out[g // (GROUPS // CH)]
                            sp.wait_ge(so.sem, so.at((name, u, "k", 1, 1)))
                            ld, hs = load_stack[g], slice(GH * g, GH * (g + 1))
                            for part in range(2):
                                rows_ = slice(2 * D * part, 2 * D * (part + 1))
                                sp.dma_start(Qs[rows_, g].rearrange("p c e l -> p (c e) l").bitcast(F32),
                                             q_dram[u, hs].rearrange("h d s l -> (d s) h l")) \
                                    .then_inc(ld.sem, ld.mark((name, x_, "q", part)))
                                sp.dma_start(Ks[rows_, g].rearrange("p c e l -> p (c e) l").bitcast(F32),
                                             k_dram[u, part, hs].rearrange("h d s l -> (d s) h l")) \
                                    .then_inc(ld.sem, ld.mark((name, x_, "k", part)))

                        for what, x_, k in full_order():
                            g = x_ % GROUPS
                            if what == "project":
                                for c in range(CH):
                                    store_heads(x_, c)
                                    if x_ == 0 and c == 0:
                                        load_stacks(0)
                                        load_stacks(1)
                            if what == "turn":
                                sp.wait_ge(vector.sem, vector.at(("max low", name, x_)))
                                if x_ >= 2:
                                    sp.wait_ge(load_max[(x_ - 2) % GROUPS].sem,
                                               load_max[(x_ - 2) % GROUPS].at((name, x_ - 2)))
                                sp.dma_start(nm_dram[x_ % 2].rearrange("s (r q) -> r s q", q=P), nmT[:, x_ % 2]) \
                                    .then_inc(max_out.sem, max_out.mark((name, x_)))
                                sp.wait_ge(max_out.sem, max_out.at((name, x_)))
                                if x_ >= GROUPS:
                                    sp.wait_ge(tensor.sem, tensor.at(("scores", name, x_ - GROUPS, 2 * TT - 1)))
                                if x_ == 0:
                                    sp.wait_ge(pool.sem, pool.at(("cleared", name)))
                                    sp.wait_ge(ones_out.sem, ones_out.at("ones"))
                                    sp.dma_start(Ks[MR:MR + 2].rearrange("p g c e l -> p (g c e l)").bitcast(F32),
                                                 ones_dram).then_inc(load_ones.sem, load_ones.mark(name))
                                sp.dma_start(Qs[MR:MR + 2, g].rearrange("p c e l -> p (c e l)").bitcast(F32),
                                             nm_dram[x_ % 2]) \
                                    .then_inc(load_max[g].sem, load_max[g].mark((name, x_)))
                                if x_ + 2 < GROUPS:
                                    load_stacks(x_ + 2)
                            if what == "scores" and k == 2 * TT - 1 and x_ < GROUPS:
                                load_stacks(x_ + GROUPS)
                    for j in range(i + 1, len(SITES)):
                        before = last_user_of_weights(SITES[j])
                        if j not in loaded and before and before[1] == s["name"]:
                            load_weights(j)
                            loaded.add(j)
                assert len(loaded) == len(SITES)
                for u in range(LANES):
                    last = SITES[-1]["name"]
                    sp.wait_ge(vector.sem, vector.at(("x", last, u)))
                    ob = out[bass.ds(it * LANES + u, 1), :, :].rearrange("o t c -> (o t) c")
                    sp.dma_start(ob[SHIFT:SHIFT + (TT - 1) * P, :].rearrange("(t p) c -> p t c", p=P),
                                 x[:, u, 0:TT - 1, :]).then_inc(stored.sem, stored.mark(("tiles", u)))
                    sp.dma_start(ob[L - SHIFT:L, :], x[0:P - SHIFT, u, TT - 1, :]) \
                        .then_inc(stored.sem, stored.mark(("end", u)))
                    sp.dma_start(ob[0:SHIFT, :], x[P - SHIFT:P, u, TT - 1, :]) \
                        .then_inc(stored.sem, stored.mark(("start", u)))
                sp.wait_ge(stored.sem, stored.at(("start", LANES - 1)))
                sp.wait_ge(arrived, len(resume))
                for sig in in_pass:
                    sp.sem_clear(sig.sem)
                sp.sem_clear(arrived)
                for sem in resume.values():
                    sp.sem_inc(sem, 1)

        @block.gpsimd
        def _(gp):
            gp.memset(ident[:, :], 0.0).then_inc(set_pool.sem, set_pool.mark("ident 0"))
            gp.memset(mask[:, :], 1.0).then_inc(set_pool.sem, set_pool.mark("mask 1"))
            gp.memset(vc[:, :, :, :], 0.0).then_inc(set_pool.sem, set_pool.mark("vc"))
            gp.memset(vp[:, :, :, :, D:2 * D], 1.0).then_inc(set_pool.sem, set_pool.mark("ones"))
            gp.memset(half[:, :], -0.5).then_inc(set_pool.sem, set_pool.mark("half"))
            gp.wait_ge(set_pool.sem, set_pool.at("half"))
            for e in range(2):
                gp.memset(vc[e * LC:(e + 1) * LC, :, :, e, D:D + 1], 1.0) \
                    .then_inc(set_pool.sem, set_pool.mark(("context ones", e)))
                gp.wait_ge(set_pool.sem, set_pool.at(("context ones", e)))
            gp.affine_select(out=ident[:, :], in_=ident[:, :], compare_op=ALU.not_equal, fill=1.0, base=0,
                             pattern=[[-1, P]], channel_multiplier=1) \
                .then_inc(set_pool.sem, set_pool.mark("ident"))
            gp.affine_select(out=mask[:, :], in_=mask[:, :], compare_op=ALU.is_ge, fill=0.0, base=0,
                             pattern=[[-D, HC]], channel_multiplier=1) \
                .then_inc(set_pool.sem, set_pool.mark("mask low"))
            gp.wait_ge(set_pool.sem, set_pool.at("mask low"))
            gp.affine_select(out=mask[:, :], in_=mask[:, :], compare_op=ALU.is_ge, fill=0.0, base=D - 1,
                             pattern=[[D, HC]], channel_multiplier=-1) \
                .then_inc(set_pool.sem, set_pool.mark("mask"))
            gp.wait_ge(set_pool.sem, set_pool.at("mask"))
            gp.wait_ge(set_tensor.sem, set_tensor.at("gates"))

            def bias(s, u):
                name = s["name"]
                row = place[name]["orow"]
                gp.wait_ge(load_w[SITES.index(s)].sem, load_w[SITES.index(s)].at((name, LOADS[s["kind"]] - 1)))
                gp.wait_ge(vector.sem, vector.at(("normed", name, u, TT - 1)))
                if s["gate"] is not None:
                    gp.wait_ge(load_gate.sem, load_gate.at(name))
                    gp.tensor_tensor(gb[:, :], row, gate[:, u, :], ALU.mult) \
                        .then_inc(pool.sem, pool.mark(("gated bias", name, u)))
                    gp.wait_ge(pool.sem, pool.at(("gated bias", name, u)))
                    row = gb[:, :]
                gp.tensor_tensor(x[:, u], x[:, u], row.unsqueeze(1).broadcast_to([P, TT, C]), ALU.add) \
                    .then_inc(pool.sem, pool.mark(("biased", name, u)))
                gp.wait_ge(pool.sem, pool.at(("biased", name, u)))

            with gp.Fori(0, PASSES) as it:
                for s in SITES:
                    name, kind = s["name"], s["kind"]
                    def deviations(u):
                        gp.wait_ge(vector.sem, vector.at(("stats", name, u)))
                        gp.tensor_scalar(rstd[:, u, :], mv[:, u, :, 1], s["ln"][0], None, ALU.add) \
                            .then_inc(pool.sem, pool.mark(("var", name, u)))
                        gp.wait_ge(pool.sem, pool.at(("var", name, u)))
                        gp.tensor_tensor(rstd[:, u, :], rstd[:, u, :], half[:, :], ALU.pow) \
                            .then_inc(pool.sem, pool.mark(("rstd", name, u)))

                    deviations(0)
                    if kind not in CROSS:
                        deviations(1)
                    else:
                        if s["ctx_ln"]:
                            gp.wait_ge(vector.sem, vector.at(("ctx stats", name)))
                            gp.tensor_scalar(cstats[:, 8:9], cstats[:, 7:8], s["ctx_ln"][0], None, ALU.add) \
                                .then_inc(pool.sem, pool.mark(("ctx var", name)))
                            gp.wait_ge(pool.sem, pool.at(("ctx var", name)))
                            gp.tensor_tensor(cstats[:, 9:10], cstats[:, 8:9], half[:, 0:1], ALU.pow) \
                                .then_inc(pool.sem, pool.mark(("ctx rstd", name)))
                        deviations(1)
                        gp.wait_ge(scalar.sem, scalar.at(("ctx keys", name, CH - 1)))
                        for c in range(CH):
                            gp.tensor_tensor(kc[:, 1, c], kTc[:, c, 1, :].unsqueeze(1).broadcast_to([P, HC, LC]),
                                             mask[:, :].unsqueeze(2).broadcast_to([P, HC, LC]), ALU.mult) \
                                .then_inc(pool.sem, pool.mark(("ctx blocks", name, 1, c)))
                    if kind == "full":
                        gp.wait_ge(pool.sem, pool.at(("rstd", name, LANES - 1)))
                        gp.memset(Ks[4 * D:P].rearrange("p g c e l -> p (g c e l)").bitcast(F32), 0.0) \
                            .then_inc(pool.sem, pool.mark(("keys cleared", name)))
                        gp.wait_ge(pool.sem, pool.at(("keys cleared", name)))
                        gp.memset(Qs[4 * D:P].rearrange("p g c e l -> p (g c e l)").bitcast(F32), 0.0) \
                            .then_inc(pool.sem, pool.mark(("cleared", name)))
                        gp.wait_ge(pool.sem, pool.at(("cleared", name)))
                        for u in range(LANES):
                            bias(s, u)
                        continue
                    if kind == "win":
                        gp.wait_ge(scalar.sem, scalar.at(("keys", name, 1)))
                        for c in range(CH):
                            for h in range(HC):
                                gp.tensor_scalar(kd[:, 1, c, h, :], kT[:, 1, c, :], mask[:, h:h + 1], None,
                                                 ALU.mult).then_inc(pool.sem, pool.mark(("blocks", name, 1, c, h)))
                    for u in range(LANES):
                        bias(s, u)
                    mlp, pieces = weight_pieces(s)

                    def split_weights():
                        a_, b_ = pieces.pop(0)
                        gp.wait_ge(scalar.sem, scalar.at(("weights high", mlp["name"], a_)))
                        gp.tensor_tensor(wL[:, a_:b_], wM[:, a_:b_], wH[:, a_:b_].bitcast(F32), ALU.subtract) \
                            .then_inc(pool.sem, pool.mark(("weights split", mlp["name"]) if not pieces else
                                                          ("weights low", mlp["name"], a_)))

                    while kind == "cross" and pieces:
                        split_weights()
                    if kind == "topk":
                        for n in range(first_unit[name, 0], first_unit[name, 0] + len(units_of(s))):
                            p3 = pr[:, n % RP, :].rearrange("p (h k) -> p h k", k=LC)
                            gp.wait_ge(vector.sem, vector.at(("selected", n)))
                            gp.tensor_tensor(p3, p3, top[:, n % 2, 0, :, 0:1].broadcast_to([P, H, LC]), ALU.subtract) \
                                .then_inc(pool.sem, pool.mark(("shifted", n)))
                            gp.wait_ge(scalar.sem, scalar.at(("exp", n)))
                            gp.tensor_tensor(pr[:, n % RP, :], pr[:, n % RP, :], rk[:, n % 2, :], ALU.mult) \
                                .then_inc(pool.sem, pool.mark(("kept", n)))
                            if pieces:
                                split_weights()
                end_pass(gp, "pool")

        @block.scalar
        def _(act):
            act.wait_ge(set_tensor.sem, set_tensor.at("cond"))
            act.activation(condT[:, :, :].rearrange("p c b -> p (c b)"), pads[0][:, 0:CH * B], ACT.Silu) \
                .then_inc(set_scalar.sem, set_scalar.mark("silu"))

            act.wait_ge(set_vector.sem, set_vector.at("gate rows"))
            act.dma_start(gates_dram.rearrange("b g n -> b (g n)"), grow) \
                .then_inc(gates_out.sem, gates_out.mark("gates"))
            act.wait_ge(gates_out.sem, gates_out.at("gates"))
            act.wait_ge(set_pool.sem, set_pool.at("ones"))
            act.dma_start(ones_dram.rearrange("a (g p l) -> p (a g) l", p=P, l=D),
                         vp[:, 0, :, :, D:2 * D].rearrange("p t h d -> p (t h) d")[:, 0:2 * GROUPS * GH * L // P // D]) \
                .then_inc(ones_out.sem, ones_out.mark("ones"))
            act.wait_ge(ones_out.sem, ones_out.at("ones"))

            with act.Fori(0, PASSES) as it:
                def modulate(dst, src, vecs, c, u, event):
                    if vecs[1] is None:
                        i = act.activation(dst, src, ACT.Copy)
                    else:
                        i = act.activation(dst, src, ACT.Identity, bias=modulation(vecs[2], c, u),
                                           scale=modulation(vecs[1], c, u))
                    i.then_inc(scalar.sem, scalar.mark(event))

                act.wait_ge(vector.sem, vector.at("modulation"))
                for s in SITES:
                    name, kind = s["name"], s["kind"]
                    def modulated(u):
                        src = cols(pads_of(kind, u)[0], CH)
                        act.wait_ge(tensor.sem, tensor.at(("turned", name, u)))
                        if kind in MLP:
                            for c in range(CH):
                                modulate(hH[:, u, c, :], src[:, c, :], s["ln"], c, u, ("h high", name, u, c))
                        for c in range(CH):
                            modulate(hT[:, u, c, :], src[:, c, :], s["ln"], c, u, ("h", name, u, c))

                    modulated(0)
                    if kind in CROSS:
                        act.wait_ge(tensor.sem, tensor.at(("ctx turned", name)))
                        lnv = s["ctx_ln"] or (0, None, None)
                        for c in range(CH):
                            for u in range(LANES):
                                src = pads[3][:, c * P + u * LC:c * P + (u + 1) * LC]
                                modulate(cT[:, c, u], src.unsqueeze(1).broadcast_to([P, 2, LC]), lnv, c, u,
                                         ("ctx", name, c, u))
                    if kind == "full":
                        for what, x_, k in full_order():
                            if what == "project":
                                for w, dst, pad in zip("qk", halves[x_], (1, 2)):
                                    act.wait_ge(tensor.sem, tensor.at((w, name, x_)))
                                    for c in range(CH):
                                        act.activation(dst[:, 0, c, :].bitcast(F32R), cols(pad, CH)[:, c, :],
                                                       ACT.Identity,
                                                       bias=column(s["bqkv"], c + (CH if w == "k" else 0))) \
                                            .then_inc(scalar.sem, scalar.mark(("high", name, x_, w, c)))
                                if x_ == 0:
                                    modulated(1)
                            if what == "scores":
                                n = x_ * 2 * TT + k
                                act.wait_ge(tensor.sem, tensor.at(("scores", name, x_, k)))
                                if n == 0:
                                    for so in stack_out:
                                        act.wait_ge(so.sem, so.at((name, 1, "k", 1, 1)))
                                if n >= RP:
                                    m = n - RP
                                    act.wait_ge(tensor.sem, tensor.at(("values", name, m // (2 * TT),
                                                                       m % (2 * TT) // 2)))
                                act.activation(pr[:, n % RP, :], pads[1 + k % 2][:, :], ACT.Exp, scale=SCALE) \
                                    .then_inc(scalar.sem, scalar.mark(("probs", name, x_, k)))
                            if what == "values" and k == TT - 1:
                                act.wait_ge(tensor.sem, tensor.at(("values", name, x_, k)))
                                if x_ == GROUPS:
                                    act.wait_ge(tensor.sem, tensor.at(("split", name, 0)))
                                if x_ == GROUPS + 2:
                                    act.wait_ge(vector.sem, vector.at(("x", name, 0)))
                                act.activation(O4[:, x_ % GROUPS, :], pads[3][:, (x_ % 2) * L:(x_ % 2 + 1) * L],
                                               ACT.Copy).then_inc(scalar.sem, scalar.mark(("o", name, x_)))
                            if what == "turn back":
                                act.wait_ge(tensor.sem, tensor.at(("turned back", name, x_)))
                                act.activation(oT[:, x_].rearrange("p c l -> p (c l)"), pads[1][:, :], ACT.Copy) \
                                    .then_inc(scalar.sem, scalar.mark(("oT", name, x_)))
                        continue
                    if kind in KEYS:
                        def projected(u):
                            if u:
                                modulated(u)
                            act.wait_ge(tensor.sem, tensor.at(("queries", name, u)))
                            for c in range(CH):
                                act.activation(qT[:, u, c, :], cols(pads_of(kind, u)[1], CH)[:, c, :], ACT.Identity,
                                               bias=column(s.get("bq") or s["bqkv"], c)) \
                                    .then_inc(scalar.sem, scalar.mark(("q", name, u, c)))
                            if kind in SELF:
                                act.wait_ge(tensor.sem, tensor.at(("keys", name, u)))
                                for c in range(CH):
                                    i = act.activation(kT[:, u, c, :], cols(3, CH)[:, c, :], ACT.Identity,
                                                       bias=column(s["bqkv"], CH + c))
                                    i.then_inc(scalar.sem, scalar.mark(("keys", name, u) if c else ("k0", name, u)))
                            if kind in CROSS and u == 0:
                                act.wait_ge(tensor.sem, tensor.at(("ctx keys", name)))
                                for c in range(CH):
                                    act.activation(kTc[:, c].rearrange("p u k -> p (u k)"), pads[0][:, c * P:(c + 1) * P],
                                                   ACT.Identity, bias=column(s["bkv"], c)) \
                                        .then_inc(scalar.sem, scalar.mark(("ctx keys", name, c)))

                        projected(0)
                        if kind not in CROSS:
                            projected(1)
                        units = units_of(s)
                        N, f = len(units), first_unit[name, 0]

                        def copied(n):
                            act.wait_ge(tensor.sem, tensor.at(("scores", n)))
                            if n >= RP:
                                act.wait_ge(tensor.sem, tensor.at(("turned probs", n - RP)))
                            act.activation(pr[:, n % RP, :], pads[n % 2][:, :], ACT.Copy) \
                                .then_inc(scalar.sem, scalar.mark(("copied", n)))

                        def exponentials(j):
                            n = f + j
                            if j < N:
                                sig = pool if kind == "topk" else vector
                                act.wait_ge(sig.sem, sig.at(("shifted", n)))
                                act.activation(pr[:, n % RP, :], pr[:, n % RP, :], ACT.Exp, scale=SCALE) \
                                    .then_inc(scalar.sem, scalar.mark(("exp", n)))

                        def turned(j):
                            if 0 <= j - 2 < N:
                                n = f + j - 2
                                act.wait_ge(tensor.sem, tensor.at(("turned probs", n)))
                                if n >= RT:
                                    act.wait_ge(tensor.sem, tensor.at(("values", n - RT)))
                                act.activation(pT[:, n % RT].rearrange("p a b -> p (a b)"), pads[2][:, :],
                                               ACT.Copy).then_inc(scalar.sem, scalar.mark(("pT", n)))
                            if tile_done(s, j - 4):
                                u, t = units[j - 4][0:2]
                                act.wait_ge(tensor.sem, tensor.at(("o turned", name, u, t)))
                                src = pads[3][:, (t % 2) * L:(t % 2) * L + C].rearrange("p (c q) -> p c q", c=CH)
                                act.activation(oT[:, u, :, t * P:(t + 1) * P], src, ACT.Copy) \
                                    .then_inc(scalar.sem, scalar.mark(("o", name, u, t)))

                        mlp, pieces = weight_pieces(s)
                        lw = load_w[SITES.index(mlp)]
                        for j in range(N + 4):
                            n = f + j
                            if pieces and j > 0:
                                a_, b_ = pieces.pop(0)
                                act.wait_ge(lw.sem, lw.at((mlp["name"], LOADS[mlp["kind"]] - 1)))
                                act.activation(wH[:, a_:b_], wM[:, a_:b_], ACT.Copy) \
                                    .then_inc(scalar.sem, scalar.mark(("weights high", mlp["name"], a_)))
                            if j < N and kind == "topk":
                                if j == 0:
                                    copied(n)
                                if j + 1 < N:
                                    copied(n + 1)
                            if kind in CROSS and j == 0:
                                projected(1)
                            turned(j)
                            exponentials(j)
                    elif kind == "swiglu":
                        for u in range(LANES):
                            for m in range(MC):
                                if (u, m) == (0, MC // 2):
                                    modulated(1)
                                act.wait_ge(tensor.sem, tensor.at(("up", name, u, m)))
                                k = u * MC + m
                                if k >= 2:
                                    act.wait_ge(vector.sem, vector.at(("product", name, (k - 2) // MC, (k - 2) % MC)))
                                act.activation(act_out[:, k % 2, :], pads[k % 3][:, 0:L], ACT.Silu,
                                               bias=column(s["b1"], m)) \
                                    .then_inc(scalar.sem, scalar.mark(("silu", name, u, m)))
                    else:
                        for u in range(LANES):
                            for m in range(MC):
                                if (u, m) == (0, MC // 2):
                                    modulated(1)
                                act.wait_ge(tensor.sem, tensor.at(("up", name, u, m - m % 2)))
                                k = (u * MC + m) // 2
                                n = u * MC + m
                                if n >= 4:
                                    act.wait_ge(vector.sem, vector.at(("hidden", name, (n - 4) // MC, (n - 4) % MC)))
                                act.activation(act_out[:, n % 4, :], pads[k % 3][:, (m % 2) * L:(m % 2 + 1) * L],
                                               ACT.Gelu_apprx_tanh, bias=column(s["b1"], m)) \
                                    .then_inc(scalar.sem, scalar.mark(("gelu", name, u, m)))
                end_pass(act, "scalar")

        @block.vector
        def _(dve):
            dve.wait_ge(set_tensor.sem, set_tensor.at("bias columns"))
            dve.tensor_copy(bcol[:, 0:nrows], pads[1][:, 0:nrows]).then_inc(set_vector.sem, set_vector.mark("bias columns"))
            dve.wait_ge(set_vector.sem, set_vector.at("bias columns"))
            dve.wait_ge(set_tensor.sem, set_tensor.at(("mod", NMOD - 1)))
            dve.tensor_tensor(modT[:, :, :], pads[2][:, 0:NMOD * CH * B].rearrange("p (m b) -> p m b", b=B),
                              bcol[:, mod_col:mod_col + NMOD * CH].unsqueeze(2).broadcast_to([P, NMOD * CH, B]),
                              ALU.add).then_inc(set_vector.sem, set_vector.mark("modulation"))
            dve.wait_ge(set_vector.sem, set_vector.at("modulation"))
            for v in SCALES:
                i = dve.tensor_scalar(modT[:, v * CH:(v + 1) * CH, :], modT[:, v * CH:(v + 1) * CH, :], 1.0, None,
                                      ALU.add)
            i.then_inc(set_vector.sem, set_vector.mark("1 + scale"))
            dve.wait_ge(set_vector.sem, set_vector.at("1 + scale"))
            dve.wait_ge(set_tensor.sem, set_tensor.at("gates"))
            dve.tensor_copy(grow[:, 0:PAD], pads[0][0:B, :]).then_inc(set_vector.sem, set_vector.mark("gate rows 0"))
            dve.tensor_copy(grow[:, PAD:], pads[1][0:B, 0:len(GATES) * C - PAD]) \
                .then_inc(set_vector.sem, set_vector.mark("gate rows"))

            with dve.Fori(0, PASSES) as it:
                dve.tensor_copy(cur[:, :, :], modT[:, :, bass.ds(it * LANES, LANES)]) \
                    .then_inc(vector.sem, vector.mark("modulation"))
                for si, s in enumerate(SITES):
                    name, kind = s["name"], s["kind"]
                    pl = place[name]

                    def mine(event):
                        dve.wait_ge(vector.sem, vector.at(event))

                    def normalise(si, u):
                        name = SITES[si]["name"]
                        if si == 0:
                            dve.wait_ge(load_x[u].sem, load_x[u].at("start"))
                        else:
                            mine(("x", SITES[si - 1]["name"], u))
                        for t in range(TT):
                            dve.bn_stats(stats[:, u, t, :], x[:, u, t, :]) \
                                .then_inc(vector.sem, vector.mark(("bn", name, u, t)))
                        for t in range(TT):
                            mine(("bn", name, u, t))
                            dve.bn_aggr(mv[:, u, t, :], stats[:, u, t, :]).then_inc(
                                vector.sem, vector.mark(("stats", name, u) if t == TT - 1 else ("aggr", name, u, t)))
                        dve.wait_ge(pool.sem, pool.at(("rstd", name, u)))
                        for t in range(TT):
                            dve.tensor_scalar(hn[:, u, t, :], x[:, u, t, :], mv[:, u, t, 0:1], rstd[:, u, t:t + 1],
                                              ALU.subtract, ALU.mult) \
                                .then_inc(vector.sem, vector.mark(("normed", name, u, t)))

                    def branch(u, pad):
                        if u and si + 1 < len(SITES):
                            normalise(si + 1, 0)
                        dve.wait_ge(pool.sem, pool.at(("biased", name, u)))
                        dve.wait_ge(tensor.sem, tensor.at(("out", name, u)))
                        out_ = cols(pad, TT)
                        tmp = ht[:, 1 if kind == "full" else u]
                        if s["gate"] is not None:
                            dve.wait_ge(load_gate.sem, load_gate.at(name))
                            if u:
                                mine(("x", name, u - 1))
                            dve.tensor_tensor(tmp, out_, gate[:, u, :].unsqueeze(1).broadcast_to([P, TT, C]),
                                              ALU.mult).then_inc(vector.sem, vector.mark(("branch", name, u)))
                            mine(("branch", name, u))
                            out_ = tmp
                        dve.tensor_tensor(x[:, u], x[:, u], out_, ALU.add) \
                            .then_inc(vector.sem, vector.mark(("x", name, u)))

                    if si == 0:
                        normalise(0, 0)
                    if kind in CROSS and s["ctx_ln"]:
                        dve.wait_ge(load_ctx.sem, load_ctx.at("context"))
                        dve.bn_stats(cstats[:, 0:6], ctok[:, :]).then_inc(vector.sem, vector.mark(("ctx bn", name)))
                        mine(("ctx bn", name))
                        dve.bn_aggr(cstats[:, 6:8], cstats[:, 0:6]) \
                            .then_inc(vector.sem, vector.mark(("ctx stats", name)))
                    if kind not in CROSS:
                        normalise(si, 1)
                    else:
                        if s["ctx_ln"]:
                            dve.wait_ge(pool.sem, pool.at(("ctx rstd", name)))
                            dve.tensor_scalar(cn[:, :], ctok[:, :], cstats[:, 6:7], cstats[:, 9:10], ALU.subtract,
                                              ALU.mult).then_inc(vector.sem, vector.mark(("ctx normed", name)))
                        normalise(si, 1)
                        dve.wait_ge(set_pool.sem, set_pool.at("mask"))
                        dve.wait_ge(scalar.sem, scalar.at(("ctx keys", name, CH - 1)))
                        for c in range(CH):
                            dve.tensor_tensor(kc[:, 0, c], kTc[:, c, 0, :].unsqueeze(1).broadcast_to([P, HC, LC]),
                                              mask[:, :].unsqueeze(2).broadcast_to([P, HC, LC]), ALU.mult) \
                                .then_inc(vector.sem, vector.mark(("ctx blocks", name, 0, c)))
                        dve.wait_ge(set_pool.sem, set_pool.at("vc"))
                        dve.wait_ge(load_w[si].sem, load_w[si].at((name, 4)))
                        dve.wait_ge(tensor.sem, tensor.at(("ctx values", name)))
                        for u in range(LANES):
                            for e in range(2):
                                r = slice(e * LC, (e + 1) * LC)
                                src = pads[3][r, u * C:(u + 1) * C].rearrange("p (a e d) -> p a e d", e=2, d=D)
                                bias = pl["vrow"][r, :].rearrange("p (a e d) -> p a e d", e=2, d=D)
                                dve.tensor_tensor(vc[r, u, :, e, 0:D], src[:, :, e, :], bias[:, :, e, :],
                                                  ALU.add) \
                                    .then_inc(vector.sem, vector.mark(("ctx values", name, u, e)))
                    if kind == "full":
                        for what, x_, k in full_order():
                            if what == "project":
                                u = x_
                                for w, src, pad in zip("qk", halves[u], (1, 2)):
                                    for c in range(CH):
                                        dve.wait_ge(scalar.sem, scalar.at(("high", name, u, w, c)))
                                        dve.scalar_tensor_tensor(
                                            out=src[:, 1, c, :].bitcast(F32R), in0=cols(pad, CH)[:, c, :],
                                            scalar=column(s["bqkv"], c + (CH if w == "k" else 0)),
                                            in1=src[:, 0, c, :], op0=ALU.add, op1=ALU.subtract) \
                                            .then_inc(vector.sem, vector.mark(("low", name, u, w, c)))
                                dve.wait_ge(load_w[si].sem, load_w[si].at((name, 1)))
                                dve.wait_ge(tensor.sem, tensor.at(("v", name, u)))
                                dve.tensor_tensor(
                                    vp[:, u, :, :, 0:D],
                                    pads[3][:, :].rearrange("p (t h d) -> p t h d", t=TT, d=D),
                                    pl["vrow"].rearrange("p (h d) -> p h d", d=D).unsqueeze(1)
                                    .broadcast_to([P, TT, H, D]), ALU.add) \
                                    .then_inc(vector.sem, vector.mark(("v", name, u)))
                            if what == "maxima":
                                dve.wait_ge(tensor.sem, tensor.at(("maxima", name, x_, k)))
                                if k == 0 and x_ >= 2:
                                    dve.wait_ge(tensor.sem, tensor.at(("turn", name, x_ - 2)))
                                b_ = (x_ * (GH * TT + 1) + k) % 2
                                dve.tensor_reduce(nm[:, x_ % 2, k:k + 1], pads[0][:, b_ * L:(b_ + 1) * L], AX.X,
                                                  ALU.max, negate=True) \
                                    .then_inc(vector.sem, vector.mark(("maxima", name, x_, k)))
                            if what == "turn":
                                dve.wait_ge(tensor.sem, tensor.at(("turn", name, x_)))
                                if x_ >= 2:
                                    dve.wait_ge(max_out.sem, max_out.at((name, x_ - 2)))
                                b_ = (x_ * (GH * TT + 1) + GH * TT) % 2
                                src = pads[0][0:GH * TT, b_ * L:b_ * L + P]
                                dve.tensor_copy(nmT[:, x_ % 2, 0].bitcast(F32R), src) \
                                    .then_inc(vector.sem, vector.mark(("max high", name, x_)))
                                mine(("max high", name, x_))
                                dve.tensor_tensor(nmT[:, x_ % 2, 1].bitcast(F32R), src, nmT[:, x_ % 2, 0],
                                                  ALU.subtract) \
                                    .then_inc(vector.sem, vector.mark(("max low", name, x_)))
                            if what == "split":
                                for t in range(TT):
                                    o = pads[1 + t // 2][:, (t % 2) * L:(t % 2 + 1) * L] \
                                        .rearrange("p (h d) -> p h d", d=2 * D)
                                    dve.wait_ge(tensor.sem, tensor.at(("split", name, x_)))
                                    dve.reciprocal(rs[:, t % 2, :].unsqueeze(2), o[:, :, D:D + 1]) \
                                        .then_inc(vector.sem, vector.mark(("1/sums", name, x_, t)))
                                    mine(("1/sums", name, x_, t))
                                    dve.tensor_tensor(on4[:, t, :].rearrange("p (h d) -> p h d", d=D), o[:, :, 0:D],
                                                      rs[:, t % 2, :].unsqueeze(2).broadcast_to([P, H, D]),
                                                      ALU.mult).then_inc(vector.sem, vector.mark(("o", name, x_, t)))
                            if what == "out":
                                branch(x_, 2)
                        continue
                    if kind == "win":
                        dve.wait_ge(set_pool.sem, set_pool.at("mask"))
                        dve.wait_ge(scalar.sem, scalar.at(("keys", name, 0)))
                        for c in range(CH):
                            for h in range(HC):
                                dve.tensor_scalar(kd[:, 0, c, h, :], kT[:, 0, c, :], mask[:, h:h + 1], None,
                                                  ALU.mult).then_inc(vector.sem, vector.mark(("blocks", name, 0, c, h)))
                        for u in range(LANES):
                            dve.wait_ge(load_w[si].sem, load_w[si].at((name, 3)))
                            dve.wait_ge(tensor.sem, tensor.at(("v", name, u)))
                            dve.tensor_tensor(vp[:, u, :, :, 0:D], pads[u].rearrange("p (t h d) -> p t h d", t=TT, d=D),
                                              pl["vrow"].rearrange("p (h d) -> p h d", d=D).unsqueeze(1)
                                              .broadcast_to([P, TT, H, D]), ALU.add) \
                                .then_inc(vector.sem, vector.mark(("v", name, u)))
                    if kind in KEYS:
                        nk = KEYS[kind]
                        nh = PAD // nk
                        N = len(units_of(s))

                        def select(n):
                            dve.wait_ge(scalar.sem, scalar.at(("copied", n)))
                            p3 = pr[:, n % RP, :].rearrange("p (h k) -> p h k", k=nk)
                            r3 = rk[:, n % 2, :].rearrange("p (h k) -> p h k", k=nk)
                            if n - 2 >= first_unit[name, 0]:
                                dve.wait_ge(pool.sem, pool.at(("kept", n - 2)))
                            for step in range(TOPK // 8):
                                src = r3 if step else p3
                                for h in range(nh):
                                    i = dve.max(top[:, n % 2, step, h, :], src[:, h, :])
                                i.then_inc(vector.sem, vector.mark(("top", n, step)))
                                mine(("top", n, step))
                                for h in range(nh):
                                    i = dve.match_replace(out=r3[:, h, :], in_to_replace=top[:, n % 2, step, h, :],
                                                          in_values=src[:, h, :], imm_value=LOWEST)
                                i.then_inc(vector.sem, vector.mark(("replaced", n, step)))
                                mine(("replaced", n, step))
                            dve.tensor_tensor(r3, p3, r3, ALU.is_gt) \
                                .then_inc(vector.sem, vector.mark(("selected", n)))

                        def shift(n):
                            maxima = mx[:, n % RP, 0:nh]
                            p3 = pr[:, n % RP, :].rearrange("p (h k) -> p h k", k=nk)
                            dve.wait_ge(tensor.sem, tensor.at(("scores", n)))
                            dve.tensor_reduce(maxima, cols(n % 2, nh), AX.X, ALU.max) \
                                .then_inc(vector.sem, vector.mark(("max", n)))
                            if n >= RP:
                                dve.wait_ge(tensor.sem, tensor.at(("turned probs", n - RP)))
                            mine(("max", n))
                            dve.tensor_tensor(p3, cols(n % 2, nh), maxima.unsqueeze(2).broadcast_to([P, nh, nk]),
                                              ALU.subtract).then_inc(vector.sem, vector.mark(("shifted", n)))

                        for j in range(N + 3):
                            if j < N:
                                (select if kind == "topk" else shift)(first_unit[name, 0] + j)
                            if tile_done(s, j - 3):
                                u, t = units_of(s)[j - 3][0:2]
                                o = pads[3][:, (t % 2) * L:(t % 2) * L + H * (D + 1)] \
                                    .rearrange("p (h d) -> p h d", d=D + 1)
                                dve.wait_ge(tensor.sem, tensor.at(("values", first_unit[name, 0] + j - 3)))
                                dve.reciprocal(rs[:, t % 2, :].unsqueeze(2), o[:, :, D:D + 1]) \
                                    .then_inc(vector.sem, vector.mark(("1/sums", name, u, t)))
                                mine(("1/sums", name, u, t))
                                dve.tensor_tensor(on[:, u, t, :].rearrange("p (h d) -> p h d", d=D), o[:, :, 0:D],
                                                  rs[:, t % 2, :].unsqueeze(2).broadcast_to([P, H, D]),
                                                  ALU.mult).then_inc(vector.sem, vector.mark(("o", name, u, t)))
                            if j == first_lane_done(s):
                                branch(0, 0)
                    if kind in MLP:
                        def split_input(u):
                            dve.wait_ge(scalar.sem, scalar.at(("h", name, u, CH - 1)))
                            dve.tensor_tensor(hL[:, u].rearrange("p c l -> p (c l)"),
                                              hT[:, u].rearrange("p c l -> p (c l)"),
                                              hH[:, u].rearrange("p c l -> p (c l)").bitcast(F32), ALU.subtract) \
                                .then_inc(vector.sem, vector.mark(("h low", name, u)))

                        split_input(0)
                        for u in range(LANES):
                            for m in range(MC):
                                if (u, m) == (0, MC // 2):
                                    split_input(1)
                                k = u * MC + m
                                if kind == "swiglu":
                                    if k >= 2:
                                        mine(("hidden", name, (k - 2) // MC, (k - 2) % MC))
                                    dve.wait_ge(scalar.sem, scalar.at(("silu", name, u, m)))
                                    src = act_out[:, 2 + k % 2, :]
                                    dve.scalar_tensor_tensor(out=src, in0=pads[k % 3][:, L:2 * L],
                                                             scalar=column(s["b1"], MC + m), in1=act_out[:, k % 2, :],
                                                             op0=ALU.add, op1=ALU.mult) \
                                        .then_inc(vector.sem, vector.mark(("product", name, u, m)))
                                    mine(("product", name, u, m))
                                else:
                                    src = act_out[:, k % 4, :]
                                    dve.wait_ge(scalar.sem, scalar.at(("gelu", name, u, m)))
                                dve.tensor_copy(hid[:, u, m, :], src) \
                                    .then_inc(vector.sem, vector.mark(("hidden high", name, u, m)))
                                mine(("hidden high", name, u, m))
                                dve.tensor_tensor(hidden_low(u, m), src, hid[:, u, m, :].bitcast(F32), ALU.subtract) \
                                    .then_inc(vector.sem, vector.mark(("hidden", name, u, m)))
                    for u in range(kind in KEYS, LANES):
                        branch(u, u)
                end_pass(dve, "vector")

        @block.tensor
        def _(pe):
            mm = pe.matmul
            pe.wait_ge(set_pool.sem, set_pool.at("ident"))
            pe.wait_ge(load_cond.sem, load_cond.at("cond"))
            for c in range(CH):
                i = pe.transpose(pads[0][:, c * B:(c + 1) * B], crow[:, c * P:(c + 1) * P], ident[0:B, 0:B])
            i.then_inc(set_tensor.sem, set_tensor.mark("cond"))
            pe.wait_ge(set_scalar.sem, set_scalar.at("silu"))
            ring = arena[:, 0:16 * CH * C].rearrange("p (s c n) -> p s c n", s=16, c=CH)
            for vec in range(NMOD):
                ld = load_mod[vec % 16]
                pe.wait_ge(ld.sem, ld.at(vec))
                for m in range(CH):
                    k = vec * CH + m
                    for c in range(CH):
                        i = mm(pads[2][:, k * B:(k + 1) * B], ring[:, vec % 16, c, m * P:(m + 1) * P], condT[:, c, :],
                               start=(c == 0), stop=(c == CH - 1))
                i.then_inc(set_tensor.sem, set_tensor.mark(("mod", vec)))
                if vec == NMOD // 2:
                    pe.wait_ge(load_rows.sem, load_rows.at(MODS[-1][1]))
                    pe.wait_ge(set_pool.sem, set_pool.at("mask"))
                    pe.transpose(pads[1][:, 0:nrows], brow[0:nrows, :], ident[0:nrows, 0:nrows]) \
                        .then_inc(set_tensor.sem, set_tensor.mark("bias columns"))
            pe.wait_ge(set_vector.sem, set_vector.at("1 + scale"))
            for g, vec in enumerate(GATES):
                for c in range(CH):
                    k = g * CH + c
                    pad, o = pads[k // 8], (k % 8) * P
                    i = pe.transpose(pad[0:B, o:o + P], modT[:, vec * CH + c, :], ident[:, :])
            i.then_inc(set_tensor.sem, set_tensor.mark("gates"))
            pe.wait_ge(set_vector.sem, set_vector.at("gate rows"))

            with pe.Fori(0, PASSES) as it:
                holder = [None] * 8

                def claim(pad, drained_by, half=None):
                    banks = [2 * pad, 2 * pad + 1] if half is None else [2 * pad + half]
                    for b in sorted({banks[0], banks[-1]}):
                        if holder[b] and not (b != banks[0] and holder[b] == before):
                            pe.wait_ge(holder[b][0].sem, holder[b][0].at(holder[b][1]))
                        before = holder[b]
                        holder[b] = drained_by

                for si, s in enumerate(SITES):
                    name, kind = s["name"], s["kind"]
                    pl, lw = place[name], load_w[si]
                    drained = "branch" if s["gate"] is not None else "x"
                    def turn_in(u):
                        pad = pads_of(kind, u)[0]
                        claim(pad, (scalar, ("h", name, u, CH - 1)))
                        for t in range(TT):
                            pe.wait_ge(vector.sem, vector.at(("normed", name, u, t)))
                            for c in range(CH):
                                i = pe.transpose(cols(pad, CH)[:, c, t * P:(t + 1) * P], hn[:, u, t, c * P:(c + 1) * P],
                                                 ident[:, :])
                        i.then_inc(tensor.sem, tensor.mark(("turned", name, u)))

                    turn_in(0)
                    if kind in CROSS:
                        claim(3, (scalar, ("ctx", name, CH - 1, LANES - 1)))
                        if s["ctx_ln"]:
                            pe.wait_ge(vector.sem, vector.at(("ctx normed", name)))
                            src = cn
                        else:
                            pe.wait_ge(load_ctx.sem, load_ctx.at("context"))
                            src = ctok
                        for c in range(CH):
                            i = pe.transpose(pads[3][:, c * P:(c + 1) * P], src[:, c * P:(c + 1) * P], ident[:, :])
                        i.then_inc(tensor.sem, tensor.mark(("ctx turned", name)))
                    if kind == "full":
                        pe.wait_ge(lw.sem, lw.at((name, LOADS[kind] - 1)))
                        wq = pl["qkv"]
                        for what, x_, k in full_order():
                            g, u = x_ % GROUPS, x_ // GROUPS
                            if what == "project":
                                u = x_
                                pe.wait_ge(scalar.sem, scalar.at(("h", name, u, CH - 1)))
                                for w, pad, first in (("q", 1, 0), ("k", 2, C)):
                                    claim(pad, (vector, ("low", name, u, w, CH - 1)))
                                    for m in range(CH):
                                        for c in range(CH):
                                            i = mm(cols(pad, CH)[:, m, :],
                                                   wq[:, c, first + m * P:first + (m + 1) * P], hT[:, u, c, :],
                                                   start=(c == 0), stop=(c == CH - 1))
                                    i.then_inc(tensor.sem, tensor.mark((w, name, u)))
                                claim(3, (vector, ("v", name, u)))
                                for t in range(TT):
                                    for c in range(CH):
                                        i = mm(cols(3, TT)[:, t, :], hT[:, u, c, t * P:(t + 1) * P],
                                               wq[:, c, 2 * C:3 * C], start=(c == 0), stop=(c == CH - 1))
                                i.then_inc(tensor.sem, tensor.mark(("v", name, u)))
                                if u == 0:
                                    turn_in(1)
                            if what == "maxima":
                                b_ = (x_ * (GH * TT + 1) + k) % 2
                                claim(0, (vector, ("maxima", name, x_, k)), half=b_)
                                if k == 0:
                                    pe.wait_ge(load_stack[g].sem, load_stack[g].at((name, x_, "k", 1)))
                                    pe.wait_ge(pool.sem, pool.at(("cleared", name)))
                                j, t = k // TT, k % TT
                                mm(pads[0][:, b_ * L:(b_ + 1) * L], Qs[0:MR, g, j // 2, j % 2, t * P:(t + 1) * P],
                                   Ks[0:MR, g, j // 2, j % 2, :], start=True, stop=True) \
                                    .then_inc(tensor.sem, tensor.mark(("maxima", name, x_, k)))
                            if what == "turn":
                                b_ = (x_ * (GH * TT + 1) + GH * TT) % 2
                                claim(0, (vector, ("max low", name, x_)), half=b_)
                                pe.wait_ge(vector.sem, vector.at(("maxima", name, x_, GH * TT - 1)))
                                pe.transpose(pads[0][0:GH * TT, b_ * L:b_ * L + P], nm[:, x_ % 2, :], ident[:, :]) \
                                    .then_inc(tensor.sem, tensor.mark(("turn", name, x_)))
                            if what == "scores":
                                if k == 0:
                                    if x_ == 0:
                                        pe.wait_ge(load_ones.sem, load_ones.at(name))
                                    pe.wait_ge(load_max[g].sem, load_max[g].at((name, x_)))
                                e, kt = k % 2, k // 2
                                claim(1 + e, (scalar, ("probs", name, x_, k)))
                                for j in (2 * e, 2 * e + 1):
                                    i = mm(pads[1 + e][:, (j % 2) * L:(j % 2 + 1) * L],
                                           Ks[:, g, j // 2, j % 2, kt * P:(kt + 1) * P], Qs[:, g, j // 2, j % 2, :],
                                           start=True, stop=True)
                                i.then_inc(tensor.sem, tensor.mark(("scores", name, x_, k)))
                            if what == "values":
                                if k == 0:
                                    claim(3, (scalar, ("o", name, x_)), half=x_ % 2)
                                    if g == 0:
                                        pe.wait_ge(vector.sem, vector.at(("v", name, u)))
                                pe.wait_ge(scalar.sem, scalar.at(("probs", name, x_, 2 * k + 1)))
                                for j in range(GH):
                                    n = (x_ * TT + k) * 2 + j // 2
                                    i = mm(pads[3][2 * D * j:2 * D * (j + 1), (x_ % 2) * L:(x_ % 2 + 1) * L],
                                           vp[:, u, k, GH * g + j, :], pr[:, n % RP, (j % 2) * L:(j % 2 + 1) * L],
                                           start=(k == 0), stop=(k == TT - 1))
                                i.then_inc(tensor.sem, tensor.mark(("values", name, x_, k)))
                            if what == "split":
                                pe.wait_ge(scalar.sem, scalar.at(("o", name, GROUPS * x_ + GROUPS - 1)))
                                for t in range(TT):
                                    claim(1 + t // 2, (vector, ("o", name, x_, t)), half=t % 2)
                                    for q in range(GROUPS):
                                        o = (t % 2) * L + q * P
                                        i = pe.transpose(pads[1 + t // 2][:, o:o + P], O4[:, q, t * P:(t + 1) * P],
                                                         ident[:, :])
                                i.then_inc(tensor.sem, tensor.mark(("split", name, x_)))
                            if what == "turn back":
                                claim(1, (scalar, ("oT", name, x_)))
                                for t in range(TT):
                                    pe.wait_ge(vector.sem, vector.at(("o", name, x_, t)))
                                    for c in range(CH):
                                        i = pe.transpose(cols(1, CH)[:, c, t * P:(t + 1) * P],
                                                         on4[:, t, c * P:(c + 1) * P], ident[:, :])
                                i.then_inc(tensor.sem, tensor.mark(("turned back", name, x_)))
                            if what == "out":
                                claim(2, (vector, (drained, name, x_)))
                                pe.wait_ge(scalar.sem, scalar.at(("oT", name, x_)))
                                for t in range(TT):
                                    for c in range(CH):
                                        i = mm(cols(2, TT)[:, t, :], oT[:, x_, c, t * P:(t + 1) * P], pl["o"][:, c, :],
                                               start=(c == 0), stop=(c == CH - 1))
                                i.then_inc(tensor.sem, tensor.mark(("out", name, x_)))
                        continue
                    if kind in KEYS:
                        nk = KEYS[kind]
                        pe.wait_ge(lw.sem, lw.at((name, 3 if kind in SELF else 4)))
                        def project(u):
                            if u:
                                turn_in(u)
                            pad = pads_of(kind, u)[1]
                            pe.wait_ge(scalar.sem, scalar.at(("h", name, u, CH - 1)))
                            wq = pl["qkv"] if kind in SELF else pl["q"]
                            claim(pad, (scalar, ("q", name, u, CH - 1)))
                            for m in range(CH):
                                for c in range(CH):
                                    i = mm(cols(pad, CH)[:, m, :], wq[:, c, m * P:(m + 1) * P], hT[:, u, c, :],
                                           start=(c == 0), stop=(c == CH - 1))
                            i.then_inc(tensor.sem, tensor.mark(("queries", name, u)))
                            if kind in SELF:
                                claim(3, (scalar, ("keys", name, u)))
                                for m in range(CH):
                                    for c in range(CH):
                                        i = mm(cols(3, CH)[:, m, :], wq[:, c, C + m * P:C + (m + 1) * P],
                                               hT[:, u, c, :], start=(c == 0), stop=(c == CH - 1))
                                i.then_inc(tensor.sem, tensor.mark(("keys", name, u)))
                                claim(u, (vector, ("v", name, u)))
                                for t in range(TT):
                                    for c in range(CH):
                                        i = mm(cols(u, TT)[:, t, :], hT[:, u, c, t * P:(t + 1) * P],
                                               wq[:, c, 2 * C:3 * C], start=(c == 0), stop=(c == CH - 1))
                                i.then_inc(tensor.sem, tensor.mark(("v", name, u)))
                            if kind in CROSS and u == 0:
                                claim(0, (scalar, ("ctx keys", name, CH - 1)))
                                pe.wait_ge(scalar.sem, scalar.at(("ctx", name, CH - 1, LANES - 1)))
                                for m in range(CH):
                                    for c in range(CH):
                                        i = mm(pads[0][:, m * P:(m + 1) * P].rearrange("p (u k) -> p u k", u=LANES),
                                               pl["kv"][:, c, m * P:(m + 1) * P], cT[:, c, :, 0, :],
                                               start=(c == 0), stop=(c == CH - 1))
                                i.then_inc(tensor.sem, tensor.mark(("ctx keys", name)))
                                claim(3, (vector, ("ctx values", name, LANES - 1, 1)))
                                for lane in range(LANES):
                                    for c in range(CH):
                                        i = mm(pads[3][:, lane * C:(lane + 1) * C], cT[:, c, lane].rearrange("p e k -> p (e k)"),
                                               pl["kv"][:, c, C:2 * C], start=(c == 0), stop=(c == CH - 1))
                                i.then_inc(tensor.sem, tensor.mark(("ctx values", name)))

                        project(0)
                        if kind not in CROSS:
                            project(1)
                        f, units = first_unit[name, 0], units_of(s)
                        N = len(units)

                        def scores(j):
                            n = f + j
                            u, t, h0, nh = units[j]
                            if kind == "topk":
                                claim(n % 2, (scalar, ("copied", n)))
                            else:
                                claim(n % 2, (vector, ("shifted", n)))
                            if j in (0, N // LANES):
                                pe.wait_ge(scalar.sem, scalar.at(("q", name, u, CH - 1)))
                            blocks = pool if u else vector
                            if kind in CROSS and j in (0, N // LANES):
                                blocks_made = blocks.at(("ctx blocks", name, u, CH - 1))
                                pe.wait_ge(blocks.sem, blocks_made)
                            if kind in SELF and t == 0:
                                hl = h0 + nh - 1
                                pe.wait_ge(blocks.sem, blocks.at(("blocks", name, u, hl // HC, hl % HC)))
                            for g in range(2):
                                o = pads[n % 2][:, g * L:(g + 1) * L]
                                if kind == "win":
                                    c, h = h0 // HC, h0 % HC + g * (L // nk)
                                    rhs = kd[:, u, c, h:h + L // nk, t * P:(t + 1) * P]
                                    o = o.rearrange("p (h k) -> p h k", k=nk)
                                else:
                                    c, rhs = g, kc[:, u, g].rearrange("p h k -> p (h k)")
                                i = mm(o, qT[:, u, c, t * P:(t + 1) * P], rhs, start=True, stop=True)
                            i.then_inc(tensor.sem, tensor.mark(("scores", n)))

                        def turn(j):
                            n = f + j
                            claim(2, (scalar, ("pT", n)))
                            probs = (pool, ("kept", n)) if kind == "topk" else (scalar, ("exp", n))
                            pe.wait_ge(probs[0].sem, probs[0].at(probs[1]))
                            for k in range(PAD // P):
                                i = pe.transpose(pads[2][:, k * P:(k + 1) * P],
                                                 pr[:, n % RP, k * P:(k + 1) * P], ident[:, :])
                            i.then_inc(tensor.sem, tensor.mark(("turned probs", n)))

                        def values(j):
                            n = f + j
                            u, t, h0, nh = units[j]
                            if h0 == 0:
                                claim(3, (scalar, ("o", name, u, t)), half=t % 2)
                            if j in (0, N // LANES):
                                made = ("v", name, u) if kind in SELF else ("ctx values", name, u, 1)
                                pe.wait_ge(vector.sem, vector.at(made))
                            pe.wait_ge(scalar.sem, scalar.at(("pT", n)))
                            first = (t % 2) * L
                            for k in range(PAD // P):
                                if kind in SELF:
                                    o, w = first + (h0 + k) * (D + 1), D + 1
                                    rhs = vp[:, u, t, h0 + k, 0:D + 1]
                                else:
                                    o, w = first + 2 * k * (D + 1), 2 * (D + 1)
                                    rhs = vc[:, u, k].rearrange("p e d -> p (e d)")
                                i = mm(pads[3][:, o:o + w], pT[:, n % RT, k, :], rhs, start=True, stop=True)
                            i.then_inc(tensor.sem, tensor.mark(("values", n)))

                        def turn_output(u, t):
                            pe.wait_ge(vector.sem, vector.at(("o", name, u, t)))
                            for c in range(CH):
                                o = (t % 2) * L + c * P
                                i = pe.transpose(pads[3][:, o:o + P], on[:, u, t, c * P:(c + 1) * P], ident[:, :])
                            i.then_inc(tensor.sem, tensor.mark(("o turned", name, u, t)))

                        def product(u):
                            claim(u, (vector, (drained, name, u)))
                            pe.wait_ge(scalar.sem, scalar.at(("o", name, u, TT - 1)))
                            for t in range(TT):
                                for c in range(CH):
                                    i = mm(cols(u, TT)[:, t, :], oT[:, u, c, t * P:(t + 1) * P], pl["o"][:, c, :],
                                           start=(c == 0), stop=(c == CH - 1))
                            i.then_inc(tensor.sem, tensor.mark(("out", name, u)))

                        for j in range(N + 4):
                            if j < N:
                                scores(j)
                            if kind in CROSS and j == 1:
                                project(1)
                            if 0 <= j - 2 < N:
                                turn(j - 2)
                            if 0 <= j - 3 < N:
                                values(j - 3)
                            if tile_done(s, j - 4):
                                turn_output(*units[j - 4][0:2])
                            if j == first_lane_done(s):
                                product(0)
                        product(1)
                    else:
                        pe.wait_ge(pool.sem, pool.at(("weights split", name)))
                        for u in range(LANES):
                            pe.wait_ge(scalar.sem, scalar.at(("h high", name, u, CH - 1)))
                            for m in range(MC):
                                if (u, m) == (0, MC // 2):
                                    turn_in(1)
                                if kind == "swiglu":
                                    k = u * MC + m
                                    claim(k % 3, (vector, ("product", name, u, m)))
                                    columns = [m * P, HID + m * P]
                                else:
                                    if m % 2:
                                        continue
                                    k = (u * MC + m) // 2
                                    claim(k % 3, (scalar, ("gelu", name, u, m + 1)))
                                    columns = [m * P, (m + 1) * P]
                                for g, col in enumerate(columns):
                                    parts = [(c, w_, h_) for w_, h_ in ((pl["w1L"], hH), (pl["w1H"], hH),
                                                                        (pl["w1H"], hL)) for c in range(CH)]
                                    for q, (c, w_, h_) in enumerate(parts):
                                        if h_ is hL and m == 0:
                                            pe.wait_ge(vector.sem, vector.at(("h low", name, u)))
                                        i = mm(cols(k % 3, 2)[:, g, :], w_[:, c, col:col + P], h_[:, u, c, :],
                                               start=(q == 0), stop=(q == len(parts) - 1))
                                i.then_inc(tensor.sem, tensor.mark(("up", name, u, m)))
                        for u in range(LANES):
                            claim(u, (vector, (drained, name, u)))
                            pe.wait_ge(vector.sem, vector.at(("hidden", name, u, MC - 1)))
                            for t in range(TT):
                                ts = slice(t * P, (t + 1) * P)
                                parts = [(m, h_, w_) for m in range(MC)
                                         for h_, w_ in ((hid[:, u, m, ts], pl["w2H"]), (hid[:, u, m, ts], pl["w2L"]),
                                                        (hidden_low(u, m)[:, ts], pl["w2H"]))]
                                for q, (m, h_, w_) in enumerate(parts):
                                    i = mm(cols(u, TT)[:, t, :], h_, w_[:, m, :],
                                           start=(q == 0), stop=(q == len(parts) - 1))
                            i.then_inc(tensor.sem, tensor.mark(("out", name, u)))
                end_pass(pe, "tensor")
    return {name: s.order for name, s in signals.items()}


def kernel(**inputs):
    import numpy as np
    from concourse import bacc
    from concourse.bass_utils import run_bass_kernel_spmd

    arrays = {f"in_{k}": np.ascontiguousarray(v) for k, v in inputs.items()}

    def program(known):
        nc = bacc.Bacc("TRN2", target_bir_lowering=False, num_devices=1)
        a = {k: nc.dram_tensor(f"in_{k}", v.shape, F32, kind="ExternalInput").ap() for k, v in inputs.items()}
        out = nc.dram_tensor("out", (B, L, C), F32, kind="ExternalOutput").ap()
        return nc, build(nc, a, out, known)

    _, events = program({})
    nc, _ = program(events)
    r = run_bass_kernel_spmd(nc, [arrays], core_ids=[0])
    return r.results[0]["out"]
```
